# Optimizing a Trainium2 kernel written in Bass

```python
import numpy as np
import jax
import jax.numpy as jnp

def _softmax(x, axis=-1):
    return jax.nn.softmax(x, axis=axis)

def _gelu(x):
    return jax.nn.gelu(x, approximate=True)

def _silu(x):
    return jax.nn.silu(x)

def _sigmoid(x):
    return jax.nn.sigmoid(x)

def _layernorm(x, axis=-1, eps=1e-05):
    m = jnp.mean(x, axis=axis, keepdims=True)
    v = jnp.var(x, axis=axis, keepdims=True)
    return (x - m) / jnp.sqrt(v + eps)

def _scatter_add(tgt, idx, src, axis=0):
    return tgt.at[idx].add(src)

def _segment_sum(src, seg, n):
    return jax.ops.segment_sum(src, seg, n)
kernel_name = 'mk_gnn_resnorm_d2_gnn_r32_3f4dea'

def setup_inputs(seed: int=0):
    np.random.seed(seed)
    _w = jnp.asarray

    def _rec_inputs():
        import jax
        import jax.numpy as jnp
        _gk = jax.random.key(seed)
        x = -0.000202 + 1 * jax.random.normal(jax.random.fold_in(_gk, 1), (50000, 128), jnp.float32)
        src = jax.random.randint(jax.random.fold_in(_gk, 2), (50000,), 0, 50000, jnp.int32)
        dst = jax.random.randint(jax.random.fold_in(_gk, 3), (50000,), 0, 50000, jnp.int32)
        _o = jnp.argsort(dst, stable=True)
        src = src[_o]
        dst = dst[_o]
        edge_attr_64 = 0.000155561 + 1.00019 * jax.random.normal(jax.random.fold_in(_gk, 11), (50000, 64), jnp.float32)
        return (x, src, dst, edge_attr_64)
    x, src, dst, edge_attr_64 = _rec_inputs()

    def _L0_gnn_setup():
        import jax, jax.numpy as jnp
        import numpy as np
        N_NODES = 50000
        N_EDGES = 25000
        IN_CH = 128
        OUT_CH = 128
        MLP_HID = 64
        key = jax.random.key(seed)
        ks = jax.random.split(key, 8)
        x = jax.random.normal(ks[0], (N_NODES, IN_CH), dtype=jnp.float32)
        edge_index = jax.random.randint(ks[1], (2, N_EDGES), 0, N_NODES, dtype=jnp.int64)
        s1 = 1.0 / np.sqrt(2 * IN_CH)
        mlp_w1 = jax.random.uniform(ks[2], (2 * IN_CH, MLP_HID), jnp.float32, -s1, s1)
        mlp_b1 = jax.random.uniform(ks[3], (MLP_HID,), jnp.float32, -s1, s1)
        s2 = 1.0 / np.sqrt(MLP_HID)
        mlp_w2 = jax.random.uniform(ks[4], (MLP_HID, 1), jnp.float32, -s2, s2)
        mlp_b2 = jax.random.uniform(ks[5], (1,), jnp.float32, -s2, s2)
        s3 = 1.0 / np.sqrt(IN_CH)
        conv_w = jax.random.uniform(ks[6], (IN_CH, OUT_CH), jnp.float32, -s3, s3)
        conv_b = jnp.zeros((OUT_CH,), jnp.float32)
        return {'x': x, 'edge_index': edge_index, 'mlp_w1': mlp_w1, 'mlp_b1': mlp_b1, 'mlp_w2': mlp_w2, 'mlp_b2': mlp_b2, 'conv_w': conv_w, 'conv_b': conv_b}
    _L0_gnn_all = _L0_gnn_setup()
    _L0_gnn_in = {k: v for k, v in _L0_gnn_all.items() if k in ('mlp_w1', 'mlp_b1', 'mlp_w2', 'mlp_b2', 'conv_w', 'conv_b')}
    del _L0_gnn_all

    def _L1_gnn_setup():
        import jax, jax.numpy as jnp
        import numpy as np
        N_NODES = 50000
        N_EDGES = 18750
        NODE_DIM = 128
        EDGE_DIM = 64
        HID_DIM = 128
        OUT_DIM = 128
        BN_EPS = 1e-05

        def _gine_conv(x, src, dst, edge_attr, We, be, Wa, ba, Wb, bb):
            msg = jax.nn.relu(x[src] + edge_attr @ We + be)
            aggr = jax.ops.segment_sum(msg, dst, num_segments=x.shape[0])
            h = x + aggr
            return jax.nn.relu(h @ Wa + ba) @ Wb + bb
        key = jax.random.key(seed)
        ks = jax.random.split(key, 16)
        s = 0.02
        return {'x': jax.random.normal(ks[0], (N_NODES, NODE_DIM), dtype=jnp.float32), 'edge_index': jax.random.randint(ks[1], (2, N_EDGES), 0, N_NODES, dtype=jnp.int64), 'edge_attr': jax.random.normal(ks[2], (N_EDGES, EDGE_DIM), dtype=jnp.float32), 'We1': jax.random.normal(ks[3], (EDGE_DIM, NODE_DIM), dtype=jnp.float32) * s, 'be1': jnp.zeros((NODE_DIM,), dtype=jnp.float32), 'W1': jax.random.normal(ks[4], (NODE_DIM, HID_DIM), dtype=jnp.float32) * s, 'b1': jnp.zeros((HID_DIM,), dtype=jnp.float32), 'W2': jax.random.normal(ks[5], (HID_DIM, HID_DIM), dtype=jnp.float32) * s, 'b2': jnp.zeros((HID_DIM,), dtype=jnp.float32), 'We2': jax.random.normal(ks[6], (EDGE_DIM, HID_DIM), dtype=jnp.float32) * s, 'be2': jnp.zeros((HID_DIM,), dtype=jnp.float32), 'W3': jax.random.normal(ks[7], (HID_DIM, OUT_DIM), dtype=jnp.float32) * s, 'b3': jnp.zeros((OUT_DIM,), dtype=jnp.float32), 'W4': jax.random.normal(ks[8], (OUT_DIM, OUT_DIM), dtype=jnp.float32) * s, 'b4': jnp.zeros((OUT_DIM,), dtype=jnp.float32), 'gamma': jnp.ones((OUT_DIM,), dtype=jnp.float32), 'beta': jnp.zeros((OUT_DIM,), dtype=jnp.float32)}
    _L1_gnn_all = _L1_gnn_setup()
    _L1_gnn_in = {k: v for k, v in _L1_gnn_all.items() if k in ('We1', 'be1', 'W1', 'b1', 'W2', 'b2', 'We2', 'be2', 'W3', 'b3', 'W4', 'b4', 'gamma', 'beta')}
    del _L1_gnn_all
    return {'x': x, 'src': src, 'dst': dst, 'edge_attr_64': edge_attr_64, 'L0_gnn_mlp_w1': _L0_gnn_in['mlp_w1'], 'L0_gnn_mlp_b1': _L0_gnn_in['mlp_b1'], 'L0_gnn_mlp_w2': _L0_gnn_in['mlp_w2'], 'L0_gnn_mlp_b2': _L0_gnn_in['mlp_b2'], 'L0_gnn_conv_w': _L0_gnn_in['conv_w'], 'L0_gnn_conv_b': _L0_gnn_in['conv_b'], 'L1_gnn_We1': _L1_gnn_in['We1'], 'L1_gnn_be1': _L1_gnn_in['be1'], 'L1_gnn_W1': _L1_gnn_in['W1'], 'L1_gnn_b1': _L1_gnn_in['b1'], 'L1_gnn_W2': _L1_gnn_in['W2'], 'L1_gnn_b2': _L1_gnn_in['b2'], 'L1_gnn_We2': _L1_gnn_in['We2'], 'L1_gnn_be2': _L1_gnn_in['be2'], 'L1_gnn_W3': _L1_gnn_in['W3'], 'L1_gnn_b3': _L1_gnn_in['b3'], 'L1_gnn_W4': _L1_gnn_in['W4'], 'L1_gnn_b4': _L1_gnn_in['b4'], 'L1_gnn_gamma': _L1_gnn_in['gamma'], 'L1_gnn_beta': _L1_gnn_in['beta']}

def reference(x, src, dst, edge_attr_64, L0_gnn_mlp_w1, L0_gnn_mlp_b1, L0_gnn_mlp_w2, L0_gnn_mlp_b2, L0_gnn_conv_w, L0_gnn_conv_b, L1_gnn_We1, L1_gnn_be1, L1_gnn_W1, L1_gnn_b1, L1_gnn_W2, L1_gnn_b2, L1_gnn_We2, L1_gnn_be2, L1_gnn_W3, L1_gnn_b3, L1_gnn_W4, L1_gnn_b4, L1_gnn_gamma, L1_gnn_beta):
    import jax
    import jax.numpy as jnp

    def _L0_gnn_ref(x, edge_index, mlp_w1, mlp_b1, mlp_w2, mlp_b2, conv_w, conv_b):
        import jax, jax.numpy as jnp
        import numpy as np
        N_NODES = 50000
        N_EDGES = 25000
        IN_CH = 128
        OUT_CH = 128
        MLP_HID = 64
        n = x.shape[0]
        row, col = (edge_index[0], edge_index[1])
        edge_feat = jnp.concatenate([x[row], x[col]], axis=-1)
        h = jax.nn.gelu(edge_feat @ mlp_w1 + mlp_b1, approximate=False)
        edge_weight = jax.nn.sigmoid(h @ mlp_w2 + mlp_b2)[:, 0]
        loop = jnp.arange(n, dtype=row.dtype)
        row_f = jnp.concatenate([row, loop])
        col_f = jnp.concatenate([col, loop])
        ew_f = jnp.concatenate([edge_weight, jnp.ones((n,), x.dtype)])
        deg = jax.ops.segment_sum(ew_f, col_f, num_segments=n)
        dinv = jnp.where(deg > 0, jax.lax.rsqrt(deg), 0.0)
        norm = dinv[row_f] * ew_f * dinv[col_f]
        xt = x @ conv_w
        msg = xt[row_f] * norm[:, None]
        out = jax.ops.segment_sum(msg, col_f, num_segments=n)
        return out + conv_b

    def _L1_gnn_ref(x, edge_index, edge_attr, We1, be1, W1, b1, W2, b2, We2, be2, W3, b3, W4, b4, gamma, beta):
        import jax, jax.numpy as jnp
        import numpy as np
        N_NODES = 50000
        N_EDGES = 18750
        NODE_DIM = 128
        EDGE_DIM = 64
        HID_DIM = 128
        OUT_DIM = 128
        BN_EPS = 1e-05

        def _gine_conv(x, src, dst, edge_attr, We, be, Wa, ba, Wb, bb):
            msg = jax.nn.relu(x[src] + edge_attr @ We + be)
            aggr = jax.ops.segment_sum(msg, dst, num_segments=x.shape[0])
            h = x + aggr
            return jax.nn.relu(h @ Wa + ba) @ Wb + bb
        src, dst = (edge_index[0], edge_index[1])
        h = jax.nn.relu(_gine_conv(x, src, dst, edge_attr, We1, be1, W1, b1, W2, b2))
        h = _gine_conv(h, src, dst, edge_attr, We2, be2, W3, b3, W4, b4)
        mean = jnp.mean(h, axis=0)
        var = jnp.mean(jnp.square(h - mean), axis=0)
        return gamma * (h - mean) * jax.lax.rsqrt(var + BN_EPS) + beta
    edge_index = jnp.stack([src, dst])
    x = _layernorm(x + _L0_gnn_ref(x, edge_index, L0_gnn_mlp_w1, L0_gnn_mlp_b1, L0_gnn_mlp_w2, L0_gnn_mlp_b2, L0_gnn_conv_w, L0_gnn_conv_b), axis=-1)
    x = _layernorm(x + _L1_gnn_ref(x, edge_index, edge_attr_64, L1_gnn_We1, L1_gnn_be1, L1_gnn_W1, L1_gnn_b1, L1_gnn_W2, L1_gnn_b2, L1_gnn_We2, L1_gnn_be2, L1_gnn_W3, L1_gnn_b3, L1_gnn_W4, L1_gnn_b4, L1_gnn_gamma, L1_gnn_beta), axis=-1)
    return x

_drawn_inputs = setup_inputs


def setup_inputs(seed=0):
    import zlib

    import numpy as np

    out = dict(_drawn_inputs(seed))
    spreads = {'L0_gnn_conv_b': (0.0, 0.1),
     'L1_gnn_be1': (0.0, 0.714),
     'L1_gnn_b1': (0.0, 0.1),
     'L1_gnn_b2': (0.0, 0.1),
     'L1_gnn_be2': (0.0, 0.1),
     'L1_gnn_b3': (0.0, 0.1),
     'L1_gnn_b4': (0.0, 2.0),
     'L1_gnn_gamma': (1.0, 0.2),
     'L1_gnn_beta': (0.0, 0.1)}
    factors = {'L0_gnn_mlp_w1': 4.879,
     'L0_gnn_mlp_b1': 29.615,
     'L0_gnn_mlp_w2': 4.751,
     'L1_gnn_We1': 3.718}
    for name, (base, spread) in spreads.items():
        noise = np.random.default_rng([zlib.crc32(name.encode()), seed]).standard_normal(out[name].shape)
        drawn = base * np.exp(spread * noise) if base else spread * noise
        out[name] = jnp.asarray(drawn.astype(out[name].dtype))
    for name, factor in factors.items():
        out[name] = (out[name] * factor).astype(out[name].dtype)
    return out
```

```python
from contextlib import ExitStack

import concourse.bass as bass
from concourse import mybir
from concourse.alu_op_type import AluOpType as ALU

P = 128
TILES = 4
G = TILES * P
WP = 96
WJ = 2
W = WP * WJ
D = 128
LAG = 4
SPREAD = 512
EPS = 1e-5

F32 = mybir.dt.float32
BF16 = mybir.dt.bfloat16
I32 = mybir.dt.int32
ACT = mybir.ActivationFunctionType
AX = mybir.AxisListType


class Names(dict):

    def __getattr__(self, name):
        return self[name]

    def __setattr__(self, name, value):
        self[name] = value


def ds(start, size):
    return bass.ds(start, size)


def over_rows(ap, rows):
    return ap.unsqueeze(1).broadcast_to([ap.shape[0], rows, ap.shape[1]])


def over_cols(ap, cols):
    return ap.unsqueeze(2).broadcast_to([ap.shape[0], ap.shape[1], cols])


def window(dram, start):
    return dram[ds(start, W), :].rearrange("(p j) f -> p (j f)", j=WJ)


def node_rows(dram, group):
    return dram[ds(group * G, G), :].rearrange("(q p) f -> p q f", p=P)


def edge_rows(dram, batch):
    return dram[ds(batch * G, G), :].rearrange("(p j) f -> p j f", j=TILES)


def pairs(eng, first, last, body):
    if last - first >= 1:
        with eng.Fori(first, last) as pair:
            body(pair)


def done(n):
    return n + 3


def freed(n):
    return n + 1


def credit(eng, *sems, by=2):
    for s in sems:
        eng.sem_inc(s, by)


def interleave(eng, c, edges, nodes):
    half, lag = c.batches // 2, LAG // 2
    edges = edges or (lambda pair: None)
    regular = eng.value_load(c.flag[0:1, 0:1], min_val=0, max_val=1)
    with eng.If(regular == 1):
        pairs(eng, 0, lag, edges)

        def both(pair):
            edges(pair)
            nodes(pair - lag, general=False)
        pairs(eng, lag, half, both)
        for pair in range(half - lag, half):
            nodes(pair, general=False)
    with eng.Else():
        pairs(eng, 0, half, edges)
        pairs(eng, 0, half - 1, lambda pair: nodes(pair, general=True))
        nodes(half - 1, general=True)


def build_setup(nc, c, a):
    A_ROWS = c.tiles // 16 + 1
    with ExitStack() as ctx:
        sb = lambda name, shape, dt=F32: ctx.enter_context(nc.sbuf_tensor(name, shape, dt))
        sem = lambda name: ctx.enter_context(nc.semaphore(name))
        iota_i = sb("iota_i", [P, P], I32)
        zeros = sb("zeros", [P, 512])
        dst_nat = sb("dst_nat", [P, c.cols], I32)
        dst_next = sb("dst_next", [P, c.cols], I32)
        part = sb("part", [P, 2, c.cols], I32)
        part_f = sb("part_f", [P, 2, c.cols])
        hot_a = sb("hot_a", [P, c.cols, A_ROWS], BF16)
        hot_b = sb("hot_b", [P, c.cols, 16], BF16)
        disorder = sb("disorder", [P, c.cols])
        disorder_sum = sb("disorder_sum", [P, 1])
        ones_col = sb("ones_col", [P, 1])
        hist = sb("hist", [A_ROWS, 16])
        row = sb("row", [1, 8, A_ROWS * 16])
        row_i = sb("row_i", [1, A_ROWS * 16], I32)
        late = sb("late", [1, 4])
        base_i = sb("base_i", [WP, c.tiles, WJ], I32)
        src_i = sb("src_i", [P, c.cols], I32)
        dst_i = sb("dst_i", [P, c.cols], I32)
        bits = sb("bits", [P, 4, c.cols], I32)
        p_hist = ctx.enter_context(nc.psum_tensor("p_hist", [A_ROWS, 16], F32))
        p_dis = ctx.enter_context(nc.psum_tensor("p_dis", [1, 1], F32))
        loaded, consts, made, step, one_hots, counted, hist_done, hist_out, hist_in, pads, kept = (sem(f"s0_{n}") for n in (
            "loaded", "consts", "made", "step", "one_hots", "counted", "hist_done", "hist_out", "hist_in", "pads", "kept"))
        block = ctx.enter_context(nc.Block())
        t_used = c.tiles
        loads = [
            (c.W1[:, 0, :], a.mlp_w1[0:D, :]), (c.W1[:, 1, :], a.mlp_w1[D:2 * D, :]),
            (c.b1[:, :], a.mlp_b1.unsqueeze(1)), (c.w2[:, :], a.mlp_w2),
            (c.b2[:, :], a.mlp_b2.unsqueeze(0).to_broadcast([P, 1])),
            (c.conv_w[:, :], a.conv_w),
            (c.conv_b[:, :], a.conv_b.unsqueeze(0).to_broadcast([P, D])),
            (c.Wa[:, 0, :], a.W1), (c.Wb[:, 0, :], a.W2), (c.Wa[:, 1, :], a.W3), (c.Wb[:, 1, :], a.W4),
            (c.We[0:c.K, 0, :], a.We1), (c.We[0:c.K, 1, :], a.We2),
            (c.We[c.K:c.K + 1, 0, :], a.be1.unsqueeze(0)), (c.We[c.K:c.K + 1, 1, :], a.be2.unsqueeze(0)),
            (c.ba[:, 0:1], a.b1.unsqueeze(1)), (c.ba[:, 1:2], a.b3.unsqueeze(1)),
            (c.bb[:, :], a.b2.unsqueeze(0).to_broadcast([P, D])),
            (c.b4[:, :], a.b4.unsqueeze(1)), (c.gamma[:, :], a.gamma.unsqueeze(1)),
            (c.beta[:, :], a.beta.unsqueeze(1)),
        ]

        @block.sync
        def _(sp):
            sp.dma_start(dst_nat[:, :], a.dst_order[0:c.E].rearrange("(p n) -> p n", p=P)).then_inc(loaded, 16)
            sp.dma_start(dst_next[:, :], a.dst_order[1:c.E + 1].rearrange("(p n) -> p n", p=P)).then_inc(loaded, 16)
            sp.dma_start(src_i[:, :], a.src_cols).then_inc(loaded, 16)
            sp.dma_start(dst_i[:, :], a.dst_cols).then_inc(loaded, 16)
            for to, of in loads:
                sp.dma_start(to, of).then_inc(consts, 16)
            sp.wait_ge(made, 2)
            for table in (c.rec0, c.rec1):
                for r in range(0, W, WP):
                    sp.dma_start(table[c.E + r:c.E + r + WP, :], zeros[0:WP, 0:D]).then_inc(pads, 16)
            sp.dma_start(c.edge_val[c.E:c.E + W, :].rearrange("(p j) f -> p (j f)", j=WJ),
                         zeros[0:WP, 0:2 * WJ]).then_inc(pads, 16)
            sp.wait_ge(hist_done, 1)
            sp.dma_start(c.hist_d[:].rearrange("(r n) -> r n", n=16), hist[:, :]).then_inc(hist_out, 16)
            sp.wait_ge(hist_out, 16)
            sp.dma_start(row[:, 0, :], c.hist_d[:].unsqueeze(0)).then_inc(hist_in, 16)
            sp.wait_ge(kept, 1)
            by_batch = c.spread_idx[:, :].rearrange("(b p) j -> p b j", p=P)
            idx_now = bits[:, 3, :].rearrange("p (b j) -> p b j", j=TILES)
            sp.dma_start(by_batch[:, 0:c.batches, :], idx_now).then_inc(pads, 16)
            sp.dma_start(by_batch[:, c.batches:, :], idx_now[:, 0:2, :]).then_inc(pads, 16)
            sp.wait_ge(pads, 16 * (2 * WJ + 3))
            sp.wait_ge(consts, 16 * len(loads))

        @block.gpsimd
        def _(pool):
            nc.gpsimd.memset(c.ident[:, :], 0.0).then_inc(made, 1)
            nc.gpsimd.memset(zeros[:, :], 0.0).then_inc(made, 1)
            pool.wait_ge(made, 2)
            nc.gpsimd.affine_select(out=c.ident[:, :], in_=c.ident[:, :], compare_op=ALU.not_equal, fill=1.0, base=0,
                                    pattern=[[-1, P]], channel_multiplier=1).then_inc(made, 1)
            nc.gpsimd.iota(iota_i[:, :], pattern=[[1, P]], base=0, channel_multiplier=0).then_inc(made, 1)
            nc.gpsimd.iota(base_i[:, :, :], pattern=[[P, c.tiles], [0, WJ]], base=0, channel_multiplier=0).then_inc(made, 1)
            nc.gpsimd.iota(c.iota_t_i[:, :], pattern=[[1, c.tiles]], base=0, channel_multiplier=0).then_inc(made, 1)

        @block.vector
        def _(dve):
            n = [0]

            def link(ins):
                n[0] += 1
                ins.then_inc(step, 1)
                dve.wait_ge(step, n[0])

            v = nc.vector
            v.memset(c.ones_row[:, :], 1.0)
            v.memset(c.dinv[:, :], 0.0)
            link(v.memset(ones_col[:, :], 1.0))
            dve.wait_ge(made, 6)
            v.tensor_copy(c.iota[:, :], iota_i[:, :])
            v.tensor_copy(c.iota_t[:, :], c.iota_t_i[:, :])
            link(v.tensor_copy(c.base[:, :], base_i[:, :, :].rearrange("p t j -> p (t j)")))
            dve.wait_ge(loaded, 64)
            v.tensor_scalar(part[:, 0, :], dst_nat[:, :], 11, None, ALU.logical_shift_right)
            link(v.tensor_scalar(part[:, 1, :], dst_nat[:, :], 7, 15, ALU.logical_shift_right, ALU.bitwise_and))
            link(v.tensor_copy(part_f[:, :, :], part[:, :, :]))
            v.tensor_tensor(hot_a[:, :, :], over_cols(part_f[:, 0, :], A_ROWS), over_rows(c.iota[:, 0:A_ROWS], c.cols),
                            ALU.is_equal)
            v.tensor_tensor(hot_b[:, :, :], over_cols(part_f[:, 1, :], 16), over_rows(c.iota[:, 0:16], c.cols),
                            ALU.is_equal)
            link(v.tensor_tensor(disorder[:, :], dst_nat[:, :], dst_next[:, :], ALU.is_gt))
            link(v.tensor_reduce(disorder_sum[:, :], disorder[:, :], AX.X, ALU.add))
            link(v.memset(late[:, :], 0.0))
            dve.sem_inc(one_hots, 1)
            v.tensor_scalar(bits[:, 0, :], src_i[:, :], P - 1, 9, ALU.bitwise_and, ALU.logical_shift_left)
            v.tensor_scalar(bits[:, 1, :], src_i[:, :], 7, None, ALU.logical_shift_right)
            link(v.tensor_scalar(bits[:, 2, :], dst_i[:, :], P - 1, None, ALU.bitwise_and))
            v.tensor_tensor(bits[:, 3, :], bits[:, 0, :], bits[:, 1, :], ALU.bitwise_or).then_inc(kept, 1)
            v.tensor_copy(c.dst_f[:, :], dst_i[:, :])
            v.tensor_copy(c.dst_lo[:, :], bits[:, 2, :])
            link(v.tensor_scalar(part[:, 0, :], dst_i[:, :], 7, None, ALU.logical_shift_right))
            link(v.tensor_copy(c.dst_hi[:, :], part[:, 0, :]))
            dve.wait_ge(counted, 2)
            v.tensor_copy(late[:, 0:1], p_dis[:, :]).then_inc(step, 1)
            n[0] += 1
            v.tensor_copy(hist[:, :], p_hist[:, :]).then_inc(hist_done, 1)
            dve.wait_ge(step, n[0])
            link(v.tensor_scalar(late[:, 1:2], late[:, 0:1], 1.0, None, ALU.min))
            link(v.tensor_scalar(late[:, 2:3], late[:, 1:2], -1.0, 1.0, ALU.mult, ALU.add))
            link(v.tensor_scalar(late[:, 3:4], late[:, 1:2], float(c.E), None, ALU.mult))
            dve.wait_ge(hist_in, 16)
            link(v.memset(row[:, 7, :], 1.0))
            link(v.tensor_tensor_scan(row[:, 1, :], row[:, 7, :], row[:, 0, :], 0.0, ALU.mult, ALU.add))
            link(v.tensor_tensor(row[:, 2, :], row[:, 1, :], row[:, 0, :], ALU.subtract))
            link(v.tensor_scalar(row[:, 3, :], row[:, 2, :], late[:, 2:3], None, ALU.mult))
            link(v.tensor_scalar(row[:, 4, :], row[:, 1, :], late[:, 2:3], late[:, 3:4], ALU.mult, ALU.add))
            v.tensor_copy(c.starts[:, :], row[:, 3, 0:t_used])
            link(v.tensor_tensor(row[:, 5, :], row[:, 4, :], row[:, 3, :], ALU.subtract))
            link(v.tensor_scalar(row[:, 6, :], row[:, 5, :], -0.5, 1.0 / W, ALU.add, ALU.mult))
            link(v.tensor_scalar(row[:, 5, :], row[:, 6, :], -0.5, 0.0, ALU.add, ALU.max))
            link(v.tensor_copy(row_i[:, :], row[:, 5, :]))
            v.tensor_copy(c.extra[:, :], row_i[:, 0:t_used])
            link(v.tensor_copy(row[:, 5, :], row_i[:, :]))
            q = row[:, 6, 0:t_used]
            link(v.tensor_scalar(q, row[:, 3, 0:t_used], float(W), float(c.E), ALU.add, ALU.min))
            link(v.scalar_tensor_tensor(row[:, 7, 0:t_used], c.iota_t[0:1, :], -float(P), q, ALU.mult, ALU.add))
            link(v.tensor_scalar(row[:, 7, 0:t_used], row[:, 7, 0:t_used], -float(LAG * G - 3 * P), 0.0, ALU.add, ALU.max))
            link(v.tensor_tensor(row[:, 7, 0:t_used], row[:, 7, 0:t_used], row[:, 5, 0:t_used], ALU.add))
            link(v.tensor_reduce(late[:, 0:1], row[:, 7, 0:t_used], AX.X, ALU.max))
            link(v.tensor_scalar(c.flag[:, :], late[:, 0:1], 0.5, None, ALU.is_lt))
            dve.wait_ge(consts, 16 * len(loads))
            link(v.tensor_scalar(c.b2[:, :], c.b2[:, :], 0.5, None, ALU.mult))

        @block.tensor
        def _(pe):
            pe.wait_ge(one_hots, 1)
            for n in range(c.cols):
                mm = nc.tensor.matmul(p_hist[:, :], hot_a[:, n, :], hot_b[:, n, :], start=(n == 0), stop=(n == c.cols - 1))
            mm.then_inc(counted, 1)
            nc.tensor.matmul(p_dis[:, :], disorder_sum[:, :], ones_col[:, :], start=True, stop=True).then_inc(counted, 1)


def build_edge_weights(nc, c, a):
    with ExitStack() as ctx:
        sb = lambda name, shape, dt=F32: ctx.enter_context(nc.sbuf_tensor(name, shape, dt))
        sem = lambda name: ctx.enter_context(nc.semaphore(name))
        two = lambda make, name, *args: [make(f"{name}{k}", *args) for k in range(2)]
        psum = lambda name, shape: ctx.enter_context(nc.psum_tensor(name, shape, F32))
        idx = two(sb, "a_idx", [P, 2 * TILES], I32)
        rows = two(sb, "a_rows", [P, 2, TILES, D])
        rows_t = two(sb, "a_rows_t", [P, 2, G])
        hid = two(sb, "a_hid", [c.M, G])
        tanh = two(sb, "a_tanh", [P, TILES])
        wk = two(sb, "a_wk", [P, TILES])
        hot_lo = two(sb, "a_hot_lo", [P, TILES, P])
        hot_hi = two(sb, "a_hot_hi", [P, TILES, c.tiles])
        zero = sb("a_zero", [1, max(P, c.tiles)])
        root = sb("a_root", [P, c.tiles])
        p_t = [two(psum, f"ap_t{side}", [P, G]) for side in range(2)]
        p_h = psum("ap_h", [c.M, G])
        p_w = psum("ap_w", [P, 2, TILES])
        p_deg = psum("ap_deg", [P, c.tiles])
        idx_in, gathered, kept = two(sem, "a_idx_in"), two(sem, "a_gathered"), two(sem, "a_kept")
        idle, turned, src_copied, dst_copied, hidden, gelu_done, logits, tanh_done, w_done, hot, deg_added = (
            sem(f"a_{n}") for n in ("idle", "turned", "src_copied", "dst_copied", "hidden", "gelu_done", "logits",
                                    "tanh_done", "w_done", "hot", "deg_added"))
        cleared, root_done, table_out = sem("a_cleared"), sem("a_root_done"), sem("a_table_out")
        half = c.batches // 2
        ROWS = 16 * 2 * TILES
        block = ctx.enter_context(nc.Block())

        @block.sync
        def _(sp):
            credit(sp, *kept, by=16)
            for k in range(2):
                sp.dma_start(idx[k][:, :], a.edge_idx[k * P:(k + 1) * P, :]).then_inc(idx_in[k], 16)

            def pair(p):
                for k in range(2):
                    n = 2 * p + k
                    sp.wait_ge(gathered[k], ROWS * p + ROWS)
                    sp.sem_inc(idle, 1)
                    sp.dma_start(edge_rows(c.rec0, n), rows[k][:, 0, :, :]).then_inc(kept[k], 16)
                    sp.dma_start(idx[k][:, :], a.edge_idx[ds((n + 2) * P, P), :]).then_inc(idx_in[k], 16)
            pairs(sp, 0, half, pair)
            for k in range(2):
                sp.wait_ge(idx_in[k], 16 * half + 16)
                sp.wait_ge(kept[k], 16 * half + 16)
            sp.wait_ge(root_done, 3)
            sp.dma_start(c.dinv_d[:, :].rearrange("(p n) o -> p (n o)", n=SPREAD), c.dinv[:, :]).then_inc(table_out, 16)
            sp.wait_ge(table_out, 16)

        @block.gpsimd
        def _(pool):
            def pair(p):
                for k in range(2):
                    n = 2 * p + k
                    pool.wait_ge(idx_in[k], 16 * p + 16)
                    pool.sem_inc(idle, 1)
                    pool.wait_ge(turned, freed(n))
                    pool.sem_inc(idle, 1)
                    pool.wait_ge(kept[k], 16 * p + 16)
                    pool.sem_inc(idle, 1)
                    for col in range(2 * TILES):
                        nc.gpsimd.indirect_dma_start(
                            rows[k][:, col // TILES, col % TILES, :], None, a.x,
                            bass.IndirectOffsetOnAxis(ap=idx[k][:, col:col + 1], axis=0)).then_inc(gathered[k], 16)
            pairs(pool, 0, half, pair)

        @block.tensor
        def _(pe):
            credit(pe, turned, hidden, logits, deg_added)
            pe.wait_ge(cleared, 1)
            nc.tensor.matmul(p_deg[:, :], zero[0:1, 0:P], zero[:, 0:c.tiles], start=True, stop=False, skip_group_check=True)

            def pair(p):
                for k in range(2):
                    n = 2 * p + k
                    pe.wait_ge(gathered[k], ROWS * p + ROWS)
                    pe.wait_ge(src_copied, freed(n))
                    pe.wait_ge(dst_copied, freed(n))
                    for side in range(2):
                        for j in range(TILES):
                            mm = nc.tensor.transpose(p_t[side][k][:, j * P:(j + 1) * P], rows[k][:, side, j, :],
                                                     c.ident[:, :])
                    mm.then_inc(turned, 1)
                for k in range(2):
                    n = 2 * p + k
                    pe.wait_ge(src_copied, done(n))
                    pe.wait_ge(dst_copied, done(n))
                    pe.wait_ge(gelu_done, done(n - 1))
                    nc.tensor.matmul(p_h[:, :], c.W1[:, 0, :], rows_t[k][:, 0, :], start=True, stop=False)
                    nc.tensor.matmul(p_h[:, :], c.W1[:, 1, :], rows_t[k][:, 1, :], start=False, stop=True).then_inc(hidden, 1)
                    pe.wait_ge(tanh_done, done(n - 1))
                    pe.wait_ge(gelu_done, done(n))
                    for j in range(TILES):
                        mm = nc.tensor.matmul(p_w[:, k, j:j + 1], hid[k][:, j * P:(j + 1) * P], c.w2[:, :],
                                              start=True, stop=True)
                    mm.then_inc(logits, 1)
                for k in range(2):
                    n = 2 * p + k
                    pe.wait_ge(hot, n + 1)
                    for j in range(TILES):
                        mm = nc.tensor.matmul(p_deg[:, :], hot_lo[k][:, j, :], hot_hi[k][:, j, :], start=False, stop=False,
                                              skip_group_check=True)
                    mm.then_inc(deg_added, 1)
            pairs(pe, 0, half, pair)

        @block.scalar
        def _(act):
            credit(act, src_copied, gelu_done, tanh_done)
            act.preload_act_table(ACT.Gelu)

            def pair(p):
                for k in range(2):
                    n = 2 * p + k
                    act.wait_ge(turned, done(n))
                    act.wait_ge(hidden, freed(n))
                    nc.scalar.activation(rows_t[k][:, 0, :], p_t[0][k][:, :], ACT.Copy).then_inc(src_copied, 1)
                for k in range(2):
                    n = 2 * p + k
                    act.wait_ge(hidden, done(n))
                    act.wait_ge(logits, freed(n))
                    nc.scalar.activation(hid[k][:, :], p_h[:, :], ACT.Gelu, bias=c.b1[:, 0:1]).then_inc(gelu_done, 1)
                for k in range(2):
                    n = 2 * p + k
                    act.wait_ge(logits, done(n))
                    act.wait_ge(w_done, freed(n))
                    nc.scalar.activation(tanh[k][:, :], p_w[:, k, :], ACT.Tanh, bias=c.b2[:, 0:1], scale=0.5).then_inc(tanh_done, 1)
            pairs(act, 0, half, pair)
            act.wait_ge(root_done, 1)
            nc.scalar.activation(root[:, :], root[:, :], ACT.Sqrt).then_inc(root_done, 1)

        @block.vector
        def _(dve):
            v = nc.vector
            credit(dve, dst_copied, w_done)
            v.memset(zero[:, :], 0.0).then_inc(cleared, 1)

            def pair(p):
                for k in range(2):
                    n = 2 * p + k
                    dve.wait_ge(deg_added, freed(n))
                    v.tensor_tensor(hot_hi[k][:, :, :], over_cols(c.dst_hi[:, ds(TILES * n, TILES)], c.tiles),
                                    over_rows(c.iota_t[:, :], TILES), ALU.is_equal)
                for k in range(2):
                    n = 2 * p + k
                    dve.wait_ge(turned, done(n))
                    dve.wait_ge(hidden, freed(n))
                    v.tensor_copy(rows_t[k][:, 1, :], p_t[1][k][:, :]).then_inc(dst_copied, 1)
                for k in range(2):
                    n = 2 * p + k
                    dve.wait_ge(tanh_done, done(n))
                    v.tensor_scalar(wk[k][:, :], tanh[k][:, :], 0.5, 0.5, ALU.mult, ALU.add).then_inc(w_done, 1)
                    dve.wait_ge(w_done, done(n))
                    v.tensor_copy(c.w_all[:, ds(TILES * n, TILES)], wk[k][:, :])
                    for j in range(TILES):
                        ins = v.tensor_scalar(hot_lo[k][:, j, :], c.iota[:, :], c.dst_lo[:, ds(TILES * n + j, 1)],
                                              wk[k][:, j:j + 1], ALU.is_equal, ALU.mult)
                    ins.then_inc(hot, 1)
            pairs(dve, 0, half, pair)
            dve.wait_ge(deg_added, done(c.batches - 1))
            v.tensor_scalar(root[:, :], p_deg[:, :], 1.0, None, ALU.add).then_inc(root_done, 1)
            dve.wait_ge(root_done, 2)
            v.reciprocal(c.dinv[:, 0:c.tiles], root[:, :]).then_inc(root_done, 1)


class Extras:

    def __init__(self, nc, c, sb, sem, name):
        self.nc, self.c = nc, c
        self.rows = sb(f"{name}_x_rows", [WP, WJ * D])
        self.val = sb(f"{name}_x_val", [WP, WJ, 2])
        self.place = sb(f"{name}_x_place", [WP, WJ])
        self.hot = sb(f"{name}_x_hot", [WP, WJ, P])
        self.free, self.loaded, self.hot_done, self.place_done = (
            sem(f"{name}_x_{n}") for n in ("free", "loaded", "hot_done", "place_done"))

    def start(self, pe):
        pe.sem_inc(self.free, 1)

    def _each(self, eng, tile, body):
        count = eng.value_load(self.c.extra[0:1, ds(tile, 1)], min_val=0, max_val=self.c.E // W + 1)
        with eng.If(count > 0):
            with eng.Fori(0, count) as i:
                body(i)
        with eng.Else():
            eng.sem_inc(self.c.none, 1)

    def load(self, sp, tile, table):
        start = sp.value_load(self.c.starts[0:1, ds(tile, 1)], min_val=0, max_val=self.c.E)

        def one(i):
            sp.wait_ge(self.free, 1)
            sp.sem_clear(self.free)
            at = self.nc.s_assert_within(start + W + i * W, 0, self.c.E,
                                         skip_runtime_bounds_check_because="a further window starts before its tile's last edge")
            sp.dma_start(self.rows[:, :], window(table, at)).then_inc(self.loaded, 16)
            sp.dma_start(self.val[:, :, :].rearrange("p j c -> p (j c)"), window(self.c.edge_val, at)).then_inc(self.loaded, 16)
        self._each(sp, tile, one)

    def one_hot(self, dve, tile, weigh):
        v = self.nc.vector

        def one(i):
            dve.wait_ge(self.loaded, 32)
            dve.sem_clear(self.loaded)
            v.tensor_tensor(self.place[:, :], self.val[:, :, 1], self.c.base[:, ds(tile * WJ, WJ)],
                            ALU.subtract).then_inc(self.place_done, 1)
            dve.wait_ge(self.place_done, 1)
            dve.sem_clear(self.place_done)
            for j in range(WJ):
                if weigh:
                    ins = v.tensor_scalar(self.hot[:, j, :], self.c.iota[0:WP, :], self.place[:, j:j + 1],
                                          self.val[:, j, 0:1], ALU.is_equal, ALU.mult)
                else:
                    ins = v.tensor_scalar(self.hot[:, j, :], self.c.iota[0:WP, :], self.place[:, j:j + 1], None,
                                          ALU.is_equal)
            ins.then_inc(self.hot_done, 1)
        self._each(dve, tile, one)

    def add(self, pe, tile, out):
        def one(i):
            pe.wait_ge(self.hot_done, 1)
            pe.sem_clear(self.hot_done)
            for j in range(WJ):
                mm = self.nc.tensor.matmul(out, self.rows[:, j * D:(j + 1) * D], self.hot[:, j, :], start=False,
                                             stop=False, skip_group_check=True)
            mm.then_inc(self.free, 1)
        self._each(pe, tile, one)


def aggregate(nc, pe, ex, g, out, rows, diag, win, hot, general):
    for q in range(TILES):
        cols = slice(q * P, (q + 1) * P)
        nc.tensor.matmul(out[:, cols], rows[:, q, :], diag[q], start=True, stop=False, skip_group_check=True)
        if general:
            ex.add(pe, g * TILES + q, out[:, cols])
        for j in range(WJ):
            mm = nc.tensor.matmul(out[:, cols], win[:, q, j * D:(j + 1) * D], hot[:, WJ * q + j, :],
                                  start=False, stop=(j == WJ - 1), skip_group_check=True)
    return mm


class LayerNorm:

    def __init__(self, nc, sb, sem, name):
        two = lambda make, what, *args: [make(f"{name}_{what}{k}", *args) for k in range(2)]
        self.nc = nc
        self.y = two(sb, "y", [P, TILES, D])
        self.out = two(sb, "out", [P, TILES, D])
        self.stats = two(sb, "stats", [P, TILES, 6])
        self.mv = two(sb, "mv", [P, TILES, 2])
        self.std = two(sb, "std", [P, TILES])
        self.rstd = two(sb, "rstd", [P, TILES])
        self.shift = two(sb, "shift", [P, TILES])
        self.y_done, self.stats_done, self.mean_done, self.var_done, self.root_done, self.rstd_done, self.shift_done, self.normed = (
            sem(f"{name}_{n}") for n in ("y_done", "stats_done", "mean_done", "var_done", "root_done", "rstd_done",
                                         "shift_done", "normed"))
        self.stored, self.idle = two(sem, "stored"), sem(f"{name}_idle")

    def start_vector(self, dve):
        credit(dve, self.y_done, self.stats_done, self.mean_done, self.var_done, self.rstd_done, self.shift_done)

    def start_scalar(self, act):
        credit(act, self.root_done, self.normed)
        credit(act, *self.stored, by=16)

    def statistics(self, dve, n, k):
        v = self.nc.vector
        dve.wait_ge(self.y_done, done(n))
        for q in range(TILES):
            ins = v.bn_stats(self.stats[k][:, q, :], self.y[k][:, q, :])
        ins.then_inc(self.stats_done, 1)
        dve.wait_ge(self.stats_done, done(n))
        dve.sem_inc(self.idle, 1)
        for q in range(TILES):
            ins = v.bn_aggr(self.mv[k][:, q, :], self.stats[k][:, q, :])
        ins.then_inc(self.mean_done, 1)
        dve.wait_ge(self.mean_done, done(n))
        v.tensor_scalar(self.std[k][:, :], self.mv[k][:, :, 1], EPS, None, ALU.add).then_inc(self.var_done, 1)

    def root(self, act, n, k):
        act.wait_ge(self.var_done, done(n))
        self.nc.scalar.activation(self.std[k][:, :], self.std[k][:, :], ACT.Sqrt).then_inc(self.root_done, 1)

    def scales(self, dve, n, k):
        v = self.nc.vector
        dve.wait_ge(self.root_done, done(n))
        dve.wait_ge(self.normed, freed(n))
        v.reciprocal(self.rstd[k][:, :], self.std[k][:, :]).then_inc(self.rstd_done, 1)
        dve.wait_ge(self.rstd_done, done(n))
        v.scalar_tensor_tensor(self.shift[k][:, :], self.mv[k][:, :, 0], -1.0, self.rstd[k][:, :], ALU.mult,
                               ALU.mult).then_inc(self.shift_done, 1)

    def apply(self, act, n, k, p, to):
        act.wait_ge(self.shift_done, done(n))
        act.wait_ge(self.stored[k], 16 * p + 16)
        for q in range(TILES):
            ins = self.nc.scalar.activation(self.out[k][:, q, :], self.y[k][:, q, :], ACT.Identity,
                                            bias=self.shift[k][:, q:q + 1], scale=self.rstd[k][:, q:q + 1])
        ins.then_inc(self.normed, 1)
        act.wait_ge(self.normed, done(n))
        act.dma_start(to, self.out[k][:, :, :]).then_inc(self.stored[k], 16)

    def finish(self, act, half):
        for k in range(2):
            act.wait_ge(self.stored[k], 16 * half + 16)


def load_windows(sp, c, s, ex, p, k, table, rows_of, rows, win, wval, general):
    g, half = 2 * p + k, c.batches // 2
    upto = half if general else (min(p + LAG // 2, half) if isinstance(p, int) else p + LAG // 2)
    for slot in range(2):
        sp.wait_ge(s.edges_out[slot], 16 * upto + 16)
        sp.sem_inc(s.idle, 1)
    sp.wait_ge(s.agg_done, freed(g))
    sp.sem_inc(s.idle, 1)
    sp.wait_ge(s.prepared, freed(g))
    sp.sem_inc(s.idle, 1)
    sp.dma_start(rows[k][:, :, :], node_rows(rows_of, g)).then_inc(s.win_in[k], 16)
    for q in range(TILES):
        start = sp.value_load(c.starts[0:1, ds(g * TILES + q, 1)], min_val=0, max_val=c.E)
        sp.dma_start(win[k][:, q, :], window(table, start)).then_inc(s.win_in[k], 16)
        if wval is not None:
            sp.dma_start(wval[k][:, WJ * q:WJ * (q + 1), :].rearrange("p j c -> p (j c)"),
                         window(c.edge_val, start)).then_inc(s.win_in[k], 16)
    if general:
        for q in range(TILES):
            ex.load(sp, g * TILES + q, table)


def build_gcn(nc, c, a):
    with ExitStack() as ctx:
        sb = lambda name, shape, dt=F32: ctx.enter_context(nc.sbuf_tensor(name, shape, dt))
        sem = lambda name: ctx.enter_context(nc.semaphore(name))
        two = lambda make, name, *args: [make(f"{name}{k}", *args) for k in range(2)]
        psum = lambda name, shape: ctx.enter_context(nc.psum_tensor(name, shape, F32))
        idx = two(sb, "b_idx", [P, TILES], I32)
        dsrc = two(sb, "b_dsrc", [P, TILES])
        val = two(sb, "b_val", [P, TILES, 2])
        win = two(sb, "b_win", [WP, TILES, WJ * D])
        wval = two(sb, "b_wval", [WP, TILES * WJ, 2])
        place = two(sb, "b_place", [WP, TILES * WJ])
        hot = two(sb, "b_hot", [WP, TILES * WJ, P])
        diag = two(sb, "b_diag", [P, TILES, P])
        rows = two(sb, "b_rows", [P, TILES, D])
        resid = two(sb, "b_resid", [P, TILES, D])
        summed = two(sb, "b_summed", [P, G])
        p_sum, p_out = two(psum, "bp_sum", [P, G]), two(psum, "bp_out", [P, G])
        ex = Extras(nc, c, sb, sem, "b")
        ln = LayerNorm(nc, sb, sem, "b_ln")
        s = Names(**{n: sem(f"b_{n}") for n in (
            "idle", "scaled", "placed", "prepared", "agg_done", "sum_copied", "projected")})
        s.idx_in, s.gathered, s.edges_out, s.win_in = (two(sem, f"b_{n}") for n in ("idx_in", "gathered", "edges_out", "win_in"))
        half = c.batches // 2
        LOADS = 16 * (2 * TILES + 1)
        block = ctx.enter_context(nc.Block())

        @block.sync
        def _(sp):
            for k in range(2):
                sp.dma_start(idx[k][:, :], c.spread_idx[k * P:(k + 1) * P, :]).then_inc(s.idx_in[k], 16)

            def edges(p):
                for k in range(2):
                    sp.wait_ge(s.gathered[k], 64 * p + 64)
                    sp.sem_inc(s.idle, 1)
                    sp.dma_start(idx[k][:, :], c.spread_idx[ds((2 * p + k + 2) * P, P), :]).then_inc(s.idx_in[k], 16)

            def nodes(p, general):
                for k in range(2):
                    load_windows(sp, c, s, ex, p, k, c.rec0, a.x, rows, win, wval, general)
            interleave(sp, c, edges, nodes)
            for k in range(2):
                sp.wait_ge(s.idx_in[k], 16 * half + 16)

        @block.gpsimd
        def _(pool):
            def edges(p):
                for k in range(2):
                    pool.wait_ge(s.idx_in[k], 16 * p + 16)
                    pool.sem_inc(s.idle, 1)
                    pool.wait_ge(s.scaled, freed(2 * p + k))
                    pool.sem_inc(s.idle, 1)
                    for j in range(TILES):
                        nc.gpsimd.indirect_dma_start(
                            dsrc[k][:, j:j + 1], None, c.dinv_d[:, :],
                            bass.IndirectOffsetOnAxis(ap=idx[k][:, j:j + 1], axis=0)).then_inc(s.gathered[k], 16)
            pairs(pool, 0, half, edges)

        @block.tensor
        def _(pe):
            credit(pe, s.agg_done, s.projected)
            ex.start(pe)

            def nodes(p, general):
                for k in range(2):
                    g = 2 * p + k
                    pe.wait_ge(s.prepared, done(g))
                    pe.wait_ge(s.win_in[k], LOADS * p + LOADS)
                    pe.wait_ge(s.sum_copied, freed(g))
                    aggregate(nc, pe, ex, g, p_sum[k], rows[k], [diag[k][:, q, :] for q in range(TILES)], win[k], hot[k],
                              general).then_inc(s.agg_done, 1)
                for k in range(2):
                    g = 2 * p + k
                    pe.wait_ge(s.sum_copied, done(g))
                    pe.wait_ge(ln.y_done, freed(g))
                    for q in range(TILES):
                        mm = nc.tensor.matmul(p_out[k][:, q * P:(q + 1) * P], summed[k][:, q * P:(q + 1) * P],
                                              c.conv_w[:, :], start=True, stop=True)
                    mm.then_inc(s.projected, 1)
            interleave(pe, c, None, nodes)

        @block.scalar
        def _(act):
            credit(act, s.sum_copied)
            credit(act, *s.edges_out, by=16)
            ln.start_scalar(act)
            act.preload_act_table(ACT.Sqrt)

            def edges(p):
                for k in range(2):
                    n = 2 * p + k
                    act.wait_ge(s.scaled, done(n))
                    act.dma_start(edge_rows(c.edge_val[0:c.E, :], n), val[k][:, :, :]).then_inc(s.edges_out[k], 16)

            def nodes(p, general):
                for k in range(2):
                    g = 2 * p + k
                    act.wait_ge(s.agg_done, done(g))
                    act.wait_ge(s.projected, freed(g))
                    nc.scalar.activation(summed[k][:, :], p_sum[k][:, :], ACT.Copy).then_inc(s.sum_copied, 1)
                for k in range(2):
                    ln.root(act, 2 * p + k, k)
                for k in range(2):
                    ln.apply(act, 2 * p + k, k, p, node_rows(c.x1, 2 * p + k))
            interleave(act, c, edges, nodes)
            for k in range(2):
                act.wait_ge(s.edges_out[k], 16 * half + 16)
            ln.finish(act, half)

        @block.vector
        def _(dve):
            v = nc.vector
            credit(dve, s.scaled, s.placed, s.prepared)
            ln.start_vector(dve)

            def edges(p):
                for k in range(2):
                    n = 2 * p + k
                    dve.wait_ge(s.gathered[k], 64 * p + 64)
                    dve.wait_ge(s.edges_out[k], 16 * p + 16)
                    v.tensor_tensor(val[k][:, :, 0], dsrc[k][:, :], c.w_all[:, ds(TILES * n, TILES)], ALU.mult)
                    v.tensor_copy(val[k][:, :, 1], c.dst_f[:, ds(TILES * n, TILES)]).then_inc(s.scaled, 1)

            def nodes(p, general):
                for k in range(2):
                    g = 2 * p + k
                    dve.wait_ge(s.win_in[k], LOADS * p + LOADS)
                    dve.wait_ge(s.agg_done, freed(g))
                    v.tensor_tensor(place[k][:, :], wval[k][:, :, 1], c.base[:, ds(g * TILES * WJ, TILES * WJ)],
                                    ALU.subtract).then_inc(s.placed, 1)
                    v.tensor_tensor(resid[k][:, :, :], rows[k][:, :, :], over_rows(c.conv_b[:, :], TILES), ALU.add)
                    for q in range(TILES):
                        v.tensor_scalar(diag[k][:, q, :], c.ident[:, :], c.dinv[:, ds(g * TILES + q, 1)], None, ALU.mult)
                    dve.wait_ge(s.placed, done(g))
                    v.tensor_copy(c.place[:, ds(g * TILES * WJ, TILES * WJ)], place[k][:, :])
                    for n in range(TILES * WJ):
                        ins = v.tensor_scalar(hot[k][:, n, :], c.iota[0:WP, :], place[k][:, n:n + 1],
                                              wval[k][:, n, 0:1], ALU.is_equal, ALU.mult)
                    ins.then_inc(s.prepared, 1)
                    if general:
                        for q in range(TILES):
                            ex.one_hot(dve, g * TILES + q, weigh=True)
                for k in range(2):
                    g = 2 * p + k
                    dve.wait_ge(s.projected, done(g))
                    dve.wait_ge(s.prepared, done(g))
                    dve.wait_ge(ln.normed, freed(g))
                    for q in range(TILES):
                        ins = v.scalar_tensor_tensor(ln.y[k][:, q, :], p_out[k][:, q * P:(q + 1) * P],
                                                     c.dinv[:, ds(g * TILES + q, 1)], resid[k][:, q, :], ALU.mult, ALU.add)
                    ins.then_inc(ln.y_done, 1)
                    ln.statistics(dve, g, k)
                for k in range(2):
                    ln.scales(dve, 2 * p + k, k)
            interleave(dve, c, edges, nodes)


def build_gine(nc, c, a, layer, h_in):
    last = layer == 1
    with ExitStack() as ctx:
        tag = "cd"[layer]
        sb = lambda name, shape, dt=F32: ctx.enter_context(nc.sbuf_tensor(f"{tag}_{name}", shape, dt))
        sem = lambda name: ctx.enter_context(nc.semaphore(f"{tag}_{name}"))
        two = lambda make, name, *args: [make(f"{name}{k}", *args) for k in range(2)]
        psum = lambda name, shape: ctx.enter_context(nc.psum_tensor(f"{tag}p_{name}", shape, F32))
        idx = two(sb, "idx", [P, 2 * TILES], I32)
        attr = two(sb, "attr", [c.K + 1, G])
        src_rows = two(sb, "src_rows", [P, TILES, D])
        msg = two(sb, "msg", [P, TILES, D])
        win = two(sb, "win", [WP, TILES, WJ * D])
        hot = two(sb, "hot", [WP, TILES * WJ, P])
        rows = two(sb, "rows", [P, TILES, D])
        summed = two(sb, "summed", [P, G])
        hid = two(sb, "hid", [P, G])
        out = two(sb, "out", [P, TILES, D])
        bn = sb("bn", [P, c.groups, 6])
        mv = sb("mv", [P, 2])
        p_edge, p_sum, p_hid, p_out = (two(psum, n, [P, G]) for n in ("edge", "sum", "hid", "out"))
        ex = Extras(nc, c, sb, sem, "x")
        s = Names(**{n: sem(n) for n in (
            "idle", "lifted", "added", "msg_done", "prepared", "agg_done", "sum_copied", "hidden", "hid_done",
            "projected", "biased", "out_done", "bn_done")})
        s.idx_in, s.attr_in, s.gathered, s.edges_out, s.win_in, s.stored = (
            two(sem, n) for n in ("idx_in", "attr_in", "gathered", "edges_out", "win_in", "stored"))
        half = c.batches // 2
        LOADS = 16 * (TILES + 1)
        block = ctx.enter_context(nc.Block())

        @block.sync
        def _(sp):
            for k in range(2):
                sp.dma_start(idx[k][:, :], a.edge_idx[k * P:(k + 1) * P, :]).then_inc(s.idx_in[k], 16)

            def edges(p):
                for k in range(2):
                    n = 2 * p + k
                    sp.wait_ge(s.gathered[k], 64 * p + 64)
                    sp.sem_inc(s.idle, 1)
                    sp.dma_start(idx[k][:, :], a.edge_idx[ds((n + 2) * P, P), :]).then_inc(s.idx_in[k], 16)
                    sp.wait_ge(s.lifted, freed(n))
                    sp.sem_inc(s.idle, 1)
                    sp.dma_start(attr[k][:, :], a.edge_attr[:, ds(n * G, G)]).then_inc(s.attr_in[k], 16)

            def nodes(p, general):
                for k in range(2):
                    load_windows(sp, c, s, ex, p, k, c.rec1, h_in, rows, win, None, general)
            interleave(sp, c, edges, nodes)
            for k in range(2):
                sp.wait_ge(s.idx_in[k], 16 * half + 16)

        @block.gpsimd
        def _(pool):
            def edges(p):
                for k in range(2):
                    pool.wait_ge(s.idx_in[k], 16 * p + 16)
                    pool.sem_inc(s.idle, 1)
                    pool.wait_ge(s.added, freed(2 * p + k))
                    pool.sem_inc(s.idle, 1)
                    for j in range(TILES):
                        nc.gpsimd.indirect_dma_start(
                            src_rows[k][:, j, :], None, h_in,
                            bass.IndirectOffsetOnAxis(ap=idx[k][:, j:j + 1], axis=0)).then_inc(s.gathered[k], 16)
            pairs(pool, 0, half, edges)

        @block.tensor
        def _(pe):
            credit(pe, s.lifted, s.agg_done, s.hidden, s.projected)
            ex.start(pe)

            def edges(p):
                for k in range(2):
                    n = 2 * p + k
                    pe.wait_ge(s.attr_in[k], 16 * p + 16)
                    pe.wait_ge(s.added, freed(n))
                    for j in range(TILES):
                        mm = nc.tensor.matmul(p_edge[k][:, j * P:(j + 1) * P], attr[k][:, j * P:(j + 1) * P],
                                              c.We[:, layer, :], start=True, stop=True)
                    mm.then_inc(s.lifted, 1)

            def nodes(p, general):
                for k in range(2):
                    g = 2 * p + k
                    pe.wait_ge(s.prepared, done(g))
                    pe.wait_ge(s.win_in[k], LOADS * p + LOADS)
                    pe.wait_ge(s.sum_copied, freed(g))
                    aggregate(nc, pe, ex, g, p_sum[k], rows[k], [c.ident[:, :]] * TILES, win[k], hot[k],
                              general).then_inc(s.agg_done, 1)
                for k in range(2):
                    g = 2 * p + k
                    pe.wait_ge(s.sum_copied, done(g))
                    pe.wait_ge(s.hid_done, freed(g))
                    nc.tensor.matmul(p_hid[k][:, :], c.Wa[:, layer, :], summed[k][:, :], start=True, stop=True)\
                        .then_inc(s.hidden, 1)
                for k in range(2):
                    g = 2 * p + k
                    pe.wait_ge(s.hid_done, done(g))
                    pe.wait_ge(s.biased, freed(g))
                    if last:
                        mm = nc.tensor.matmul(p_out[k][:, :], c.Wb[:, layer, :], hid[k][:, :], start=True, stop=True)
                    else:
                        for q in range(TILES):
                            mm = nc.tensor.matmul(p_out[k][:, q * P:(q + 1) * P], hid[k][:, q * P:(q + 1) * P],
                                                  c.Wb[:, layer, :], start=True, stop=True)
                    mm.then_inc(s.projected, 1)
            interleave(pe, c, edges, nodes)

        @block.scalar
        def _(act):
            credit(act, s.msg_done, s.sum_copied, s.hid_done, s.out_done)
            credit(act, *s.edges_out, *s.stored, by=16)
            act.preload_act_table(ACT.Relu)

            def edges(p):
                for k in range(2):
                    n = 2 * p + k
                    act.wait_ge(s.added, done(n))
                    nc.scalar.activation(msg[k][:, :, :], msg[k][:, :, :], ACT.Relu).then_inc(s.msg_done, 1)
                for k in range(2):
                    n = 2 * p + k
                    act.wait_ge(s.msg_done, done(n))
                    act.dma_start(edge_rows(c.rec1[0:c.E, :], n), msg[k][:, :, :]).then_inc(s.edges_out[k], 16)

            def nodes(p, general):
                for k in range(2):
                    g = 2 * p + k
                    act.wait_ge(s.agg_done, done(g))
                    act.wait_ge(s.hidden, freed(g))
                    nc.scalar.activation(summed[k][:, :], p_sum[k][:, :], ACT.Copy).then_inc(s.sum_copied, 1)
                for k in range(2):
                    g = 2 * p + k
                    act.wait_ge(s.hidden, done(g))
                    act.wait_ge(s.projected, freed(g))
                    if last:
                        act.wait_ge(s.stored[k], 16 * p + 16)
                    nc.scalar.activation(hid[k][:, :], p_hid[k][:, :], ACT.Relu, bias=c.ba[:, layer:layer + 1])\
                        .then_inc(s.hid_done, 1)
                for k in range(2):
                    g = 2 * p + k
                    if last:
                        act.wait_ge(s.hid_done, done(g))
                        act.dma_start(c.hid_d[:, ds(g * G, G)], hid[k][:, :]).then_inc(s.stored[k], 16)
                    else:
                        act.wait_ge(s.biased, done(g))
                        nc.scalar.activation(out[k][:, :, :], out[k][:, :, :], ACT.Relu).then_inc(s.out_done, 1)
                        act.wait_ge(s.out_done, done(g))
                        act.dma_start(node_rows(c.h1, g), out[k][:, :, :]).then_inc(s.stored[k], 16)
            interleave(act, c, edges, nodes)
            for k in range(2):
                act.wait_ge(s.edges_out[k], 16 * half + 16)
                act.wait_ge(s.stored[k], 16 * half + 16)

        @block.vector
        def _(dve):
            v = nc.vector
            credit(dve, s.added, s.prepared, s.biased)

            def edges(p):
                for k in range(2):
                    n = 2 * p + k
                    dve.wait_ge(s.gathered[k], 64 * p + 64)
                    dve.wait_ge(s.lifted, done(n))
                    dve.wait_ge(s.edges_out[k], 16 * p + 16)
                    v.tensor_tensor(msg[k][:, :, :], p_edge[k][:, :].rearrange("p (j f) -> p j f", j=TILES),
                                    src_rows[k][:, :, :], ALU.add).then_inc(s.added, 1)

            def nodes(p, general):
                for k in range(2):
                    g = 2 * p + k
                    dve.wait_ge(s.agg_done, freed(g))
                    v.tensor_tensor(hot[k][:, :, :], over_cols(c.place[:, ds(g * TILES * WJ, TILES * WJ)], P),
                                    over_rows(c.iota[0:WP, :], TILES * WJ), ALU.is_equal).then_inc(s.prepared, 1)
                    if general:
                        for q in range(TILES):
                            ex.one_hot(dve, g * TILES + q, weigh=False)
                for k in range(2):
                    g = 2 * p + k
                    dve.wait_ge(s.projected, done(g))
                    if last:
                        cols = min(G, c.n_nodes - g * G) if isinstance(g, int) else G
                        v.bn_stats(bn[:, ds(g, 1), :].rearrange("p a s -> p (a s)"), p_out[k][:, 0:cols]).then_inc(s.biased, 1)
                    else:
                        dve.wait_ge(s.stored[k], 16 * p + 16)
                        v.tensor_tensor(out[k][:, :, :], p_out[k][:, :].rearrange("p (q f) -> p q f", q=TILES),
                                        over_rows(c.bb[:, :], TILES), ALU.add).then_inc(s.biased, 1)
            interleave(dve, c, edges, nodes)
            if last:
                dve.wait_ge(s.biased, done(c.groups - 1))
                v.bn_aggr(mv[:, :], bn[:, :, :].rearrange("p g s -> p (g s)")).then_inc(s.bn_done, 1)
                dve.wait_ge(s.bn_done, 1)
                v.tensor_tensor(c.bn_mean[:, :], mv[:, 0:1], c.b4[:, :], ALU.add)
                v.tensor_scalar(c.bn_var[:, :], mv[:, 1:2], EPS, None, ALU.add)


def build_final(nc, c, a):
    with ExitStack() as ctx:
        sb = lambda name, shape, dt=F32: ctx.enter_context(nc.sbuf_tensor(name, shape, dt))
        sem = lambda name: ctx.enter_context(nc.semaphore(name))
        two = lambda make, name, *args: [make(f"{name}{k}", *args) for k in range(2)]
        psum = lambda name, shape: ctx.enter_context(nc.psum_tensor(name, shape, F32))
        col = sb("e_col", [P, 4])
        diag = sb("e_diag", [P, 2, P])
        ones = sb("e_ones", [P, P])
        row = sb("e_row", [P, 2, P])
        Wn = sb("e_Wn", [P, D])
        hid = two(sb, "e_hid", [P, G])
        rows = two(sb, "e_rows", [P, TILES, D])
        p_out = two(psum, "ep_out", [P, G])
        p_row = psum("ep_row", [P, 2 * P])
        ln = LayerNorm(nc, sb, sem, "e_ln")
        idle, step, projected, p_done = sem("e_idle"), sem("e_step"), sem("e_projected"), sem("e_row_done")
        loaded = two(sem, "e_loaded")
        half = c.batches // 2
        STEPS = 9
        block = ctx.enter_context(nc.Block())

        @block.sync
        def _(sp):
            def pair(p):
                for k in range(2):
                    g = 2 * p + k
                    sp.wait_ge(projected, freed(g))
                    sp.sem_inc(idle, 1)
                    sp.wait_ge(ln.y_done, freed(g))
                    sp.sem_inc(idle, 1)
                    sp.dma_start(hid[k][:, :], c.hid_d[:, ds(g * G, G)]).then_inc(loaded[k], 16)
                    sp.dma_start(rows[k][:, :, :], node_rows(c.x1, g)).then_inc(loaded[k], 16)
            pairs(sp, 0, half, pair)

        @block.tensor
        def _(pe):
            credit(pe, projected)
            pe.wait_ge(step, 7)
            nc.tensor.matmul(p_row[:, :], ones[:, :], diag[:, :, :].rearrange("p a f -> p (a f)"), start=True,
                             stop=True).then_inc(p_done, 1)
            pe.wait_ge(step, STEPS)

            def pair(p):
                for k in range(2):
                    g = 2 * p + k
                    pe.wait_ge(loaded[k], 32 * p + 32)
                    pe.wait_ge(ln.y_done, freed(g))
                    for q in range(TILES):
                        cols = slice(q * P, (q + 1) * P)
                        nc.tensor.matmul(p_out[k][:, cols], hid[k][:, cols], Wn[:, :], start=True, stop=False,
                                         skip_group_check=True)
                        mm = nc.tensor.matmul(p_out[k][:, cols], c.ones_row[0:1, :], row[0:1, 1, :], start=False,
                                              stop=True, skip_group_check=True)
                    mm.then_inc(projected, 1)
            pairs(pe, 0, half, pair)

        @block.scalar
        def _(act):
            ln.start_scalar(act)
            act.preload_act_table(ACT.Sqrt)
            nc.scalar.activation(col[:, 0:1], c.bn_var[:, :], ACT.Sqrt).then_inc(step, 1)

            def pair(p):
                for k in range(2):
                    ln.root(act, 2 * p + k, k)
                for k in range(2):
                    ln.apply(act, 2 * p + k, k, p, node_rows(a.out, 2 * p + k))
            pairs(act, 0, half, pair)
            ln.finish(act, half)

        @block.vector
        def _(dve):
            v = nc.vector
            ln.start_vector(dve)
            n = [1]

            def link(ins):
                n[0] += 1
                ins.then_inc(step, 1)
                dve.wait_ge(step, n[0])

            v.memset(ones[:, :], 1.0)
            dve.wait_ge(step, 1)
            link(v.reciprocal(col[:, 1:2], col[:, 0:1]))
            link(v.tensor_tensor(col[:, 2:3], col[:, 1:2], c.gamma[:, :], ALU.mult))
            link(v.tensor_tensor(col[:, 3:4], c.b4[:, :], c.bn_mean[:, :], ALU.subtract))
            link(v.scalar_tensor_tensor(col[:, 3:4], col[:, 3:4], col[:, 2:3], c.beta[:, :], ALU.mult, ALU.add))
            link(v.tensor_scalar(diag[:, 0, :], c.ident[:, :], col[:, 2:3], None, ALU.mult))
            link(v.tensor_scalar(diag[:, 1, :], c.ident[:, :], col[:, 3:4], None, ALU.mult))
            dve.wait_ge(p_done, 1)
            link(v.tensor_copy(row[:, :, :], p_row[:, :].rearrange("p (a f) -> p a f", a=2)))
            link(v.tensor_tensor(Wn[:, :], c.Wb[:, 1, :], row[:, 0, :], ALU.mult))
            assert n[0] == STEPS

            def pair(p):
                for k in range(2):
                    g = 2 * p + k
                    dve.wait_ge(projected, done(g))
                    dve.wait_ge(loaded[k], 32 * p + 32)
                    dve.wait_ge(ln.normed, freed(g))
                    v.tensor_tensor(ln.y[k][:, :, :], p_out[k][:, :].rearrange("p (q f) -> p q f", q=TILES),
                                    rows[k][:, :, :], ALU.add).then_inc(ln.y_done, 1)
                    ln.statistics(dve, g, k)
                for k in range(2):
                    ln.scales(dve, 2 * p + k, k)
            pairs(dve, 0, half, pair)


def build(nc, a, n_nodes):
    c = Names(nc=nc, n_nodes=n_nodes)
    c.N = a.x.shape[0]
    c.E = a.edge_attr.shape[1]
    c.K = a.edge_attr.shape[0] - 1
    c.M = a.mlp_b1.shape[0]
    c.tiles, c.groups, c.batches, c.cols = c.N // P, c.N // G, c.E // G, c.E // P
    assert c.groups == c.batches and c.batches % 2 == 0 and c.tiles <= min(SPREAD, 512)
    dram = lambda name, shape, dt=F32: nc.dram_tensor(f"t_{name}", shape, dt).ap()
    c.rec0, c.rec1 = dram("rec0", [c.E + W, D]), dram("rec1", [c.E + W, D])
    c.edge_val = dram("edge_val", [c.E + W, 2])
    c.x1, c.h1, c.hid_d = dram("x1", [c.N, D]), dram("h1", [c.N, D]), dram("hid_d", [D, c.N])
    c.dinv_d, c.spread_idx = dram("dinv_d", [P * SPREAD, 1]), dram("spread_idx", [(c.batches + 2) * P, TILES], I32)
    c.hist_d = dram("hist_d", [16 * (c.tiles // 16 + 1)])
    with ExitStack() as ctx:
        sb = lambda name, shape, dt=F32: ctx.enter_context(nc.sbuf_tensor(f"c_{name}", shape, dt))
        c.none = ctx.enter_context(nc.semaphore("none"))
        c.ident, c.iota, c.iota_t = sb("ident", [P, P]), sb("iota", [P, P]), sb("iota_t", [P, c.tiles])
        c.iota_t_i = sb("iota_t_i", [P, c.tiles], I32)
        c.ones_row = sb("ones_row", [1, P])
        c.W1, c.b1, c.w2, c.b2 = sb("W1", [D, 2, c.M]), sb("b1", [c.M, 1]), sb("w2", [c.M, 1]), sb("b2", [P, 1])
        c.conv_w, c.conv_b = sb("conv_w", [D, D]), sb("conv_b", [P, D])
        c.Wa, c.Wb, c.We = sb("Wa", [D, 2, D]), sb("Wb", [D, 2, D]), sb("We", [c.K + 1, 2, D])
        c.ba, c.bb, c.b4 = sb("ba", [D, 2]), sb("bb", [P, D]), sb("b4", [D, 1])
        c.gamma, c.beta, c.bn_mean, c.bn_var = (sb(n, [D, 1]) for n in ("gamma", "beta", "bn_mean", "bn_var"))
        c.w_all, c.dst_f, c.dst_lo, c.dst_hi = (sb(n, [P, c.cols]) for n in ("w_all", "dst_f", "dst_lo", "dst_hi"))
        c.dinv = sb("dinv", [P, SPREAD])
        c.base, c.place = sb("base", [WP, c.tiles * WJ]), sb("place", [WP, c.tiles * WJ])
        c.starts, c.extra, c.flag = sb("starts", [1, c.tiles], I32), sb("extra", [1, c.tiles], I32), sb("flag", [1, 1], I32)
        build_setup(nc, c, a)
        build_edge_weights(nc, c, a)
        build_gcn(nc, c, a)
        build_gine(nc, c, a, 0, c.x1)
        build_gine(nc, c, a, 1, c.h1)
        build_final(nc, c, a)


def arrays_of(x, src, dst, edge_attr_64, L0_gnn_mlp_w1, L0_gnn_mlp_b1, L0_gnn_mlp_w2, L0_gnn_mlp_b2, L0_gnn_conv_w,
              L0_gnn_conv_b, L1_gnn_We1, L1_gnn_be1, L1_gnn_W1, L1_gnn_b1, L1_gnn_W2, L1_gnn_b2, L1_gnn_We2, L1_gnn_be2,
              L1_gnn_W3, L1_gnn_b3, L1_gnn_W4, L1_gnn_b4, L1_gnn_gamma, L1_gnn_beta):
    import numpy as np
    n, e = x.shape[0], src.shape[0]
    size = -(-max(n + 1, e + 1) // (2 * G)) * 2 * G
    size = max(size, 2 * LAG * G)

    def pad(arr, rows, fill=0):
        out = np.full((rows,) + tuple(arr.shape[1:]), fill, arr.dtype)
        out[:arr.shape[0]] = arr
        return out
    src_p, dst_p = pad(np.asarray(src), size, size - 1), pad(np.asarray(dst), size, size - 1)
    batches = size // G
    by_batch = lambda v: v.reshape(batches, P, TILES)
    edge_idx = np.concatenate([by_batch(src_p), by_batch(dst_p)], axis=2)
    attr = pad(np.asarray(edge_attr_64), size).reshape(batches, P, TILES, -1)
    attr = attr.transpose(3, 0, 2, 1).reshape(attr.shape[3], size)
    return {
        "x": pad(np.asarray(x), size),
        "dst_order": pad(dst_p, size + 1, size - 1),
        "src_cols": by_batch(src_p).transpose(1, 0, 2).reshape(P, -1),
        "dst_cols": by_batch(dst_p).transpose(1, 0, 2).reshape(P, -1),
        "edge_idx": pad(edge_idx, batches + 2).reshape(-1, 2 * TILES),
        "edge_attr": np.concatenate([attr, np.ones((1, size), attr.dtype)]),
        "mlp_w1": L0_gnn_mlp_w1, "mlp_b1": L0_gnn_mlp_b1, "mlp_w2": L0_gnn_mlp_w2, "mlp_b2": L0_gnn_mlp_b2,
        "conv_w": L0_gnn_conv_w, "conv_b": L0_gnn_conv_b, "We1": L1_gnn_We1, "be1": L1_gnn_be1, "W1": L1_gnn_W1,
        "b1": L1_gnn_b1, "W2": L1_gnn_W2, "b2": L1_gnn_b2, "We2": L1_gnn_We2, "be2": L1_gnn_be2, "W3": L1_gnn_W3,
        "b3": L1_gnn_b3, "W4": L1_gnn_W4, "b4": L1_gnn_b4, "gamma": L1_gnn_gamma, "beta": L1_gnn_beta,
    }


def kernel(**inputs):
    import numpy as np
    import concourse.bacc as bacc
    from concourse.bass_utils import run_bass_kernel_spmd

    arrays = {f"in_{k}": np.ascontiguousarray(v) for k, v in arrays_of(**inputs).items()}
    nc = bacc.Bacc("TRN2", target_bir_lowering=False, num_devices=1)
    a = Names(**{k[3:]: nc.dram_tensor(k, v.shape, mybir.dt.from_np(v.dtype), kind="ExternalInput").ap()
                           for k, v in arrays.items()})
    a.out = nc.dram_tensor("out_rows", a.x.shape, F32, kind="ExternalOutput").ap()
    n_nodes = inputs["x"].shape[0]
    build(nc, a, n_nodes)
    r = run_bass_kernel_spmd(nc, [arrays], core_ids=[0])
    return r.results[0]["out_rows"][:n_nodes]
```

```python
from contextlib import ExitStack, contextmanager

import concourse.bass as bass
from concourse import mybir
from concourse.alu_op_type import AluOpType as ALU

P = 128
TILES = 4
G = TILES * P
CHUNKS = TILES + 1
PAIRS = 2 * TILES
WIN = CHUNKS * P
EDGE = WIN // 2
XJ = 2
XW = P * XJ
D = 128
SLOTS = 4
LAG = 2
RW = D + 2
SPREAD = 512
EPS = 1e-5

F32 = mybir.dt.float32
BF16 = mybir.dt.bfloat16
I32 = mybir.dt.int32
ACT = mybir.ActivationFunctionType
AX = mybir.AxisListType


class Names(dict):

    def __getattr__(self, name):
        return self[name]

    def __setattr__(self, name, value):
        self[name] = value


def ds(start, size):
    return bass.ds(start, size)


def over_rows(ap, rows):
    return ap.unsqueeze(1).broadcast_to([ap.shape[0], rows, ap.shape[1]])


def over_cols(ap, cols):
    return ap.unsqueeze(2).broadcast_to([ap.shape[0], ap.shape[1], cols])


def window(table, start):
    return table[ds(start, WIN), :].rearrange("(i p) f -> p i f", p=P)


def kept_rows(c, table):
    return table[EDGE:EDGE + c.E, :]


def node_rows(dram, group):
    return dram[ds(group * G, G), :].rearrange("(q p) f -> p q f", p=P)


def edge_rows(dram, batch):
    return dram[ds(batch * G, G), :].rearrange("(p j) f -> p j f", j=TILES)


def done(n):
    return n + 1 + SLOTS


def freed(n):
    return n + 1


def credit(eng, *sems, by=SLOTS):
    for s in sems:
        eng.sem_inc(s, by)


@contextmanager
def semaphores(nc, tag):
    made = []
    with ExitStack() as held:
        def sem(name):
            made.append(held.enter_context(nc.semaphore(f"{tag}_{name}")))
            return made[-1]
        yield sem
        with nc.Block() as block:
            @block.vector
            def _(dve):
                for s in made:
                    dve.sem_clear(s)


def pipeline(eng, c, order, steps):
    stages = [(steps[name[0]], int(name[1:])) for name in order.split() if name[0] in steps]
    if not stages:
        return
    lag = max(lag for _, lag in stages)

    def turn(q):
        for k in range(SLOTS):
            for step, back in stages:
                slot, item_turn = (k - back) % SLOTS, q + (k - back) // SLOTS
                n = SLOTS * item_turn + slot
                if not isinstance(q, int) or 0 <= n < c.batches:
                    step(n, slot, item_turn)
    first = min(-(-lag // SLOTS), c.full)
    for q in range(first):
        turn(q)
    if first < c.full:
        with eng.Fori(first, c.full) as q:
            turn(q)
    for q in range(c.full, -(-(c.batches + lag) // SLOTS)):
        turn(q)


def one_by_one(order):
    return " ".join(name[0] + "0" for name in sorted(order.split(), key=lambda name: int(name[1:])))


def interleave(eng, c, order, edges, nodes, nodes_general=None):
    regular = eng.value_load(c.flag[0:1, 0:1], min_val=0, max_val=1)
    with eng.If(regular == 1):
        pipeline(eng, c, order, {**edges, **nodes})
    with eng.Else():
        pipeline(eng, c, one_by_one(order), edges)
        pipeline(eng, c, one_by_one(order), nodes_general or nodes)


def build_setup(nc, c, a):
    A_ROWS = c.tiles // 16 + 1
    assert EDGE % (P // 2) == 0 and EDGE >= XW
    with semaphores(nc, "s0") as sem, ExitStack() as ctx:
        sb = lambda name, shape, dt=F32: ctx.enter_context(nc.sbuf_tensor(name, shape, dt))
        iota_i = sb("iota_i", [P, P], I32)
        zeros = sb("zeros", [P, EDGE * RW // P])
        dst_nat = sb("dst_nat", [P, c.cols], I32)
        dst_next = sb("dst_next", [P, c.cols], I32)
        part = sb("part", [P, 2, c.cols], I32)
        part_f = sb("part_f", [P, 2, c.cols])
        hot_a = sb("hot_a", [P, c.cols, A_ROWS], BF16)
        hot_b = sb("hot_b", [P, c.cols, 16], BF16)
        disorder = sb("disorder", [P, c.cols])
        disorder_sum = sb("disorder_sum", [P, 1])
        ones_col = sb("ones_col", [P, 1])
        hist = sb("hist", [A_ROWS, 16])
        row = sb("row", [1, 8, A_ROWS * 16])
        row_i = sb("row_i", [1, A_ROWS * 16], I32)
        late = sb("late", [1, 4])
        base_i = sb("base_i", [P, c.tiles], I32)
        off_i = sb("off_i", [1, c.tiles], I32)
        off = sb("off", [1, c.tiles])
        src_i = sb("src_i", [P, c.cols], I32)
        dst_i = sb("dst_i", [P, c.cols], I32)
        bits = sb("bits", [P, 4, c.cols], I32)
        p_hist = ctx.enter_context(nc.psum_tensor("p_hist", [A_ROWS, 16], F32))
        p_dis = ctx.enter_context(nc.psum_tensor("p_dis", [1, 1], F32))
        loaded, consts, made, step, one_hots, counted, hist_done, hist_out, hist_in, pads, kept = (sem(n) for n in (
            "loaded", "consts", "made", "step", "one_hots", "counted", "hist_done", "hist_out", "hist_in", "pads", "kept"))
        block = ctx.enter_context(nc.Block())
        t_used = c.tiles
        loads = [
            (c.W1[:, 0, :], a.mlp_w1[0:D, :]), (c.W1[:, 1, :], a.mlp_w1[D:2 * D, :]),
            (c.b1[:, :], a.mlp_b1.unsqueeze(1)), (c.w2[:, :], a.mlp_w2),
            (c.b2[:, :], a.mlp_b2.unsqueeze(0).to_broadcast([P, 1])),
            (c.conv_w[:, :], a.conv_w),
            (c.conv_b[:, :], a.conv_b.unsqueeze(0).to_broadcast([P, D])),
            (c.Wa[:, 0, :], a.W1), (c.Wb[:, 0, :], a.W2), (c.Wa[:, 1, :], a.W3), (c.Wb[:, 1, :], a.W4),
            (c.We[0:c.K, 0, :], a.We1), (c.We[0:c.K, 1, :], a.We2),
            (c.We[c.K:c.K + 1, 0, :], a.be1.unsqueeze(0)), (c.We[c.K:c.K + 1, 1, :], a.be2.unsqueeze(0)),
            (c.ba[:, 0:1], a.b1.unsqueeze(1)), (c.ba[:, 1:2], a.b3.unsqueeze(1)),
            (c.bb[:, :], a.b2.unsqueeze(0).to_broadcast([P, D])),
            (c.b4[:, :], a.b4.unsqueeze(1)), (c.gamma[:, :], a.gamma.unsqueeze(1)),
            (c.beta[:, :], a.beta.unsqueeze(1)),
        ]

        @block.sync
        def _(sp):
            sp.dma_start(dst_nat[:, :], a.dst_order[0:c.E].rearrange("(p n) -> p n", p=P)).then_inc(loaded, 16)
            sp.dma_start(dst_next[:, :], a.dst_order[1:c.E + 1].rearrange("(p n) -> p n", p=P)).then_inc(loaded, 16)
            sp.dma_start(src_i[:, :], a.src_cols).then_inc(loaded, 16)
            sp.dma_start(dst_i[:, :], a.dst_cols).then_inc(loaded, 16)
            for to, of in loads:
                sp.dma_start(to, of).then_inc(consts, 16)
            sp.wait_ge(made, 2)
            for table in (c.rec0, c.rec1):
                for start in (0, EDGE + c.E):
                    rows = table[start:start + EDGE, :]
                    sp.dma_start(rows.rearrange("r f -> (r f)").rearrange("(p n) -> p n", p=P),
                                 zeros[:, 0:EDGE * table.shape[1] // P]).then_inc(pads, 16)
            sp.wait_ge(hist_done, 1)
            sp.dma_start(c.hist_d[:].rearrange("(r n) -> r n", n=16), hist[:, :]).then_inc(hist_out, 16)
            sp.wait_ge(hist_out, 16)
            sp.dma_start(row[:, 0, :], c.hist_d[:].unsqueeze(0)).then_inc(hist_in, 16)
            sp.wait_ge(kept, 1)
            by_batch = c.spread_idx[:, :].rearrange("(b p) j -> p b j", p=P)
            idx_now = bits[:, 3, :].rearrange("p (b j) -> p b j", j=TILES)
            sp.dma_start(by_batch[:, 0:c.batches, :], idx_now).then_inc(pads, 16)
            sp.dma_start(by_batch[:, c.batches:, :], idx_now[:, 0:SLOTS, :]).then_inc(pads, 16)
            sp.wait_ge(pads, 16 * 6)
            sp.wait_ge(consts, 16 * len(loads))

        @block.gpsimd
        def _(pool):
            nc.gpsimd.memset(c.ident[:, :], 0.0).then_inc(made, 1)
            nc.gpsimd.memset(zeros[:, :], 0.0).then_inc(made, 1)
            pool.wait_ge(made, 2)
            nc.gpsimd.affine_select(out=c.ident[:, :], in_=c.ident[:, :], compare_op=ALU.not_equal, fill=1.0, base=0,
                                    pattern=[[-1, P]], channel_multiplier=1).then_inc(made, 1)
            nc.gpsimd.iota(iota_i[:, :], pattern=[[1, P]], base=0, channel_multiplier=0).then_inc(made, 1)
            nc.gpsimd.iota(base_i[:, :], pattern=[[P, c.tiles]], base=0, channel_multiplier=0).then_inc(made, 1)
            nc.gpsimd.iota(off_i[:, :], pattern=[[0, c.groups], [P, TILES]], base=-EDGE, channel_multiplier=0).then_inc(made, 1)
            nc.gpsimd.iota(c.iota_t_i[:, :], pattern=[[1, c.tiles]], base=0, channel_multiplier=0).then_inc(made, 1)

        @block.vector
        def _(dve):
            n = [0]

            def link(ins):
                n[0] += 1
                ins.then_inc(step, 1)
                dve.wait_ge(step, n[0])

            v = nc.vector
            v.memset(c.ones_row[:, :], 1.0)
            v.memset(c.none_row[:, :], 0.0)
            v.memset(c.dinv[:, :], 0.0)
            link(v.memset(ones_col[:, :], 1.0))
            dve.wait_ge(made, 7)
            v.tensor_copy(c.iota[:, :], iota_i[:, :])
            v.tensor_copy(c.iota_t[:, :], c.iota_t_i[:, :])
            v.tensor_copy(off[:, :], off_i[:, :])
            link(v.tensor_copy(c.base[:, :], base_i[:, :]))
            dve.wait_ge(loaded, 64)
            v.tensor_scalar(part[:, 0, :], dst_nat[:, :], 11, None, ALU.logical_shift_right)
            link(v.tensor_scalar(part[:, 1, :], dst_nat[:, :], 7, 15, ALU.logical_shift_right, ALU.bitwise_and))
            link(v.tensor_copy(part_f[:, :, :], part[:, :, :]))
            v.tensor_tensor(hot_a[:, :, :], over_cols(part_f[:, 0, :], A_ROWS), over_rows(c.iota[:, 0:A_ROWS], c.cols),
                            ALU.is_equal)
            v.tensor_tensor(hot_b[:, :, :], over_cols(part_f[:, 1, :], 16), over_rows(c.iota[:, 0:16], c.cols),
                            ALU.is_equal)
            link(v.tensor_tensor(disorder[:, :], dst_nat[:, :], dst_next[:, :], ALU.is_gt))
            link(v.tensor_reduce(disorder_sum[:, :], disorder[:, :], AX.X, ALU.add))
            link(v.memset(late[:, :], 0.0))
            dve.sem_inc(one_hots, 1)
            v.tensor_scalar(bits[:, 0, :], src_i[:, :], P - 1, 9, ALU.bitwise_and, ALU.logical_shift_left)
            v.tensor_scalar(bits[:, 1, :], src_i[:, :], 7, None, ALU.logical_shift_right)
            link(v.tensor_scalar(bits[:, 2, :], dst_i[:, :], P - 1, None, ALU.bitwise_and))
            v.tensor_tensor(bits[:, 3, :], bits[:, 0, :], bits[:, 1, :], ALU.bitwise_or).then_inc(kept, 1)
            v.tensor_copy(c.dst_f[:, :], dst_i[:, :])
            v.tensor_copy(c.dst_lo[:, :], bits[:, 2, :])
            link(v.tensor_scalar(part[:, 0, :], dst_i[:, :], 7, None, ALU.logical_shift_right))
            link(v.tensor_copy(c.dst_hi[:, :], part[:, 0, :]))
            dve.wait_ge(counted, 2)
            v.tensor_copy(late[:, 0:1], p_dis[:, :]).then_inc(step, 1)
            n[0] += 1
            v.tensor_copy(hist[:, :], p_hist[:, :]).then_inc(hist_done, 1)
            dve.wait_ge(step, n[0])
            link(v.tensor_scalar(late[:, 1:2], late[:, 0:1], 1.0, None, ALU.min))
            link(v.tensor_scalar(late[:, 2:3], late[:, 1:2], -1.0, 1.0, ALU.mult, ALU.add))
            link(v.tensor_scalar(late[:, 3:4], late[:, 1:2], float(c.E), None, ALU.mult))
            dve.wait_ge(hist_in, 16)
            link(v.memset(row[:, 7, :], 1.0))
            link(v.tensor_tensor_scan(row[:, 1, :], row[:, 7, :], row[:, 0, :], 0.0, ALU.mult, ALU.add))
            link(v.tensor_tensor(row[:, 2, :], row[:, 1, :], row[:, 0, :], ALU.subtract))
            link(v.tensor_scalar(row[:, 3, :], row[:, 2, :], late[:, 2:3], None, ALU.mult))
            link(v.tensor_scalar(row[:, 4, :], row[:, 1, :], late[:, 2:3], late[:, 3:4], ALU.mult, ALU.add))
            v.tensor_copy(c.starts[:, :], row[:, 3, 0:t_used])
            link(v.tensor_tensor(row[:, 5, :], row[:, 4, :], row[:, 3, :], ALU.subtract))
            link(v.tensor_scalar(row[:, 6, :], row[:, 5, :], -0.5, 1.0 / XW, ALU.add, ALU.mult))
            link(v.tensor_scalar(row[:, 5, :], row[:, 6, :], 0.5, 0.0, ALU.add, ALU.max))
            link(v.tensor_copy(row_i[:, :], row[:, 5, :]))
            v.tensor_copy(c.extra[:, :], row_i[:, 0:t_used])
            middle = over_cols(row[:, 3, 0:t_used].rearrange("o (g t) -> o g t", t=TILES)[:, :, TILES // 2], TILES)
            link(v.tensor_copy(row[:, 5, 0:t_used].rearrange("o (g t) -> o g t", t=TILES), middle))
            link(v.tensor_tensor(row[:, 6, 0:t_used], row[:, 5, 0:t_used], off[:, :], ALU.add))
            link(v.tensor_tensor(row[:, 7, 0:t_used], row[:, 6, 0:t_used], row[:, 3, 0:t_used], ALU.subtract))
            link(v.scalar_tensor_tensor(row[:, 2, 0:t_used], row[:, 4, 0:t_used], -float(2 * P), row[:, 6, 0:t_used],
                                        ALU.add, ALU.subtract))
            link(v.tensor_tensor(row[:, 7, 0:t_used], row[:, 7, 0:t_used], row[:, 2, 0:t_used], ALU.max))
            link(v.tensor_scalar(row[:, 6, 0:t_used], row[:, 5, 0:t_used], float(EDGE), float(c.E), ALU.add, ALU.min))
            link(v.scalar_tensor_tensor(row[:, 6, 0:t_used], c.iota_t[0:1, :], -float(P), row[:, 6, 0:t_used],
                                        ALU.mult, ALU.add))
            link(v.scalar_tensor_tensor(row[:, 6, 0:t_used], off[:, :], float(EDGE - LAG * G), row[:, 6, 0:t_used],
                                        ALU.add, ALU.add))
            link(v.tensor_tensor(row[:, 7, 0:t_used], row[:, 7, 0:t_used], row[:, 6, 0:t_used], ALU.max))
            link(v.tensor_reduce(late[:, 0:1], row[:, 7, 0:t_used], AX.X, ALU.max))
            link(v.tensor_scalar(c.flag[:, :], late[:, 0:1], 0.5, None, ALU.is_lt))
            dve.wait_ge(consts, 16 * len(loads))
            link(v.tensor_scalar(c.b2[:, :], c.b2[:, :], 0.5, None, ALU.mult))

        @block.tensor
        def _(pe):
            pe.wait_ge(one_hots, 1)
            for n in range(c.cols):
                mm = nc.tensor.matmul(p_hist[:, :], hot_a[:, n, :], hot_b[:, n, :], start=(n == 0), stop=(n == c.cols - 1))
            mm.then_inc(counted, 1)
            nc.tensor.matmul(p_dis[:, :], disorder_sum[:, :], ones_col[:, :], start=True, stop=True).then_inc(counted, 1)


def build_edge_weights(nc, c, a):
    with semaphores(nc, "a") as sem, ExitStack() as ctx:
        sb = lambda name, shape, dt=F32: ctx.enter_context(nc.sbuf_tensor(name, shape, dt))
        slots = lambda make, name, *args: [make(f"{name}{k}", *args) for k in range(SLOTS)]
        psum = lambda name, shape: ctx.enter_context(nc.psum_tensor(name, shape, F32))
        idx = slots(sb, "a_idx", [P, 2 * TILES], I32)
        src_rows, dst_rows = slots(sb, "a_src_rows", [P, TILES, RW]), slots(sb, "a_dst_rows", [P, TILES, D])
        src_t, dst_t = slots(sb, "a_src_t", [P, G]), slots(sb, "a_dst_t", [P, G])
        hid = slots(sb, "a_hid", [c.M, G])
        tanh = slots(sb, "a_tanh", [P, TILES])
        wk = slots(sb, "a_wk", [P, TILES])
        hot_lo = slots(sb, "a_hot_lo", [P, TILES, P])
        hot_hi = slots(sb, "a_hot_hi", [P, TILES, c.tiles])
        zero = sb("a_zero", [1, max(P, c.tiles)])
        root = sb("a_root", [P, c.tiles])
        p_src, p_dst = ([psum(f"ap_{side}{k}", [P, G]) for k in range(2)] for side in ("src", "dst"))
        p_h = psum("ap_h", [c.M, G])
        p_w = psum("ap_w", [P, SLOTS, TILES])
        p_deg = psum("ap_deg", [P, c.tiles])
        idx_in, gathered, kept = slots(sem, "idx_in"), c.gathered[0], slots(sem, "kept")
        marked, turned, src_copied, dst_copied, hidden, gelu_done, logits, tanh_done, w_done, hot, deg_added = (
            sem(n) for n in ("marked", "turned", "src_copied", "dst_copied", "hidden", "gelu_done",
                                    "logits", "tanh_done", "w_done", "hot", "deg_added"))
        cleared, root_done, table_out = sem("cleared"), sem("root_done"), sem("table_out")
        ROWS = 16 * 2 * TILES
        block = ctx.enter_context(nc.Block())

        @block.sync
        def _(sp):
            credit(sp, *kept, by=16)
            for k in range(SLOTS):
                sp.dma_start(idx[k][:, :], a.edge_idx[k * P:(k + 1) * P, :]).then_inc(idx_in[k], 16)

            def keep_and_fetch(n, k, q):
                sp.wait_ge(gathered[k], ROWS * q + ROWS)
                sp.sem_inc(c.none, 1)
                sp.wait_ge(marked, done(n))
                sp.sem_inc(c.none, 1)
                sp.dma_start(edge_rows(kept_rows(c, c.rec0), n), src_rows[k][:, :, :]).then_inc(kept[k], 16)
                sp.dma_start(idx[k][:, :], a.edge_idx[ds((n + SLOTS) * P, P), :]).then_inc(idx_in[k], 16)
            pipeline(sp, c, "K2", {"K": keep_and_fetch})
            for k in range(SLOTS):
                sp.wait_ge(idx_in[k], 16 * c.uses(k) + 16)
                sp.wait_ge(kept[k], 16 * c.uses(k) + 16)
            sp.wait_ge(root_done, 3)
            sp.dma_start(c.dinv_d[:, :].rearrange("(p n) o -> p (n o)", n=SPREAD), c.dinv[:, :]).then_inc(table_out, 16)
            sp.wait_ge(table_out, 16)

        @block.gpsimd
        def _(pool):
            def gather(n, k, q):
                pool.wait_ge(idx_in[k], 16 * q + 16)
                pool.sem_inc(c.none, 1)
                pool.wait_ge(turned, freed(n))
                pool.sem_inc(c.none, 1)
                pool.wait_ge(kept[k], 16 * q + 16)
                pool.sem_inc(c.none, 1)
                for side, rows in enumerate((src_rows, dst_rows)):
                    for j in range(TILES):
                        col = side * TILES + j
                        nc.gpsimd.indirect_dma_start(
                            rows[k][:, j, 0:D], None, a.x,
                            bass.IndirectOffsetOnAxis(ap=idx[k][:, col:col + 1], axis=0)).then_inc(gathered[k], 16)
            pipeline(pool, c, "G0", {"G": gather})

        @block.tensor
        def _(pe):
            credit(pe, turned, hidden, logits, deg_added)
            pe.wait_ge(cleared, 1)
            nc.tensor.matmul(p_deg[:, :], zero[0:1, 0:P], zero[:, 0:c.tiles], start=True, stop=False, skip_group_check=True)

            def transpose_rows(n, k, q):
                pe.wait_ge(gathered[k], ROWS * q + ROWS)
                pe.wait_ge(src_copied, done(n - 2))
                pe.wait_ge(dst_copied, done(n - 2))
                for rows, out in ((src_rows, p_src), (dst_rows, p_dst)):
                    for j in range(TILES):
                        mm = nc.tensor.transpose(out[k % 2][:, j * P:(j + 1) * P], rows[k][:, j, 0:D], c.ident[:, :])
                mm.then_inc(turned, 1)

            def hidden_layer(n, k, q):
                pe.wait_ge(src_copied, done(n))
                pe.wait_ge(dst_copied, done(n))
                pe.wait_ge(gelu_done, done(n - 1))
                nc.tensor.matmul(p_h[:, :], c.W1[:, 0, :], src_t[k][:, :], start=True, stop=False)
                nc.tensor.matmul(p_h[:, :], c.W1[:, 1, :], dst_t[k][:, :], start=False, stop=True).then_inc(hidden, 1)

            def logit(n, k, q):
                pe.wait_ge(tanh_done, done(n - 1))
                pe.wait_ge(gelu_done, done(n))
                for j in range(TILES):
                    mm = nc.tensor.matmul(p_w[:, k, j:j + 1], hid[k][:, j * P:(j + 1) * P], c.w2[:, :],
                                          start=True, stop=True)
                mm.then_inc(logits, 1)

            def degrees(n, k, q):
                pe.wait_ge(hot, n + 1)
                for j in range(TILES):
                    mm = nc.tensor.matmul(p_deg[:, :], hot_lo[k][:, j, :], hot_hi[k][:, j, :], start=False, stop=False,
                                          skip_group_check=True)
                mm.then_inc(deg_added, 1)
            pipeline(pe, c, "D5 L3 H2 T1",
                  {"T": transpose_rows, "H": hidden_layer, "L": logit, "D": degrees})

        @block.scalar
        def _(act):
            credit(act, src_copied, gelu_done, tanh_done)
            act.preload_act_table(ACT.Gelu)

            def copy_src(n, k, q):
                act.wait_ge(turned, done(n))
                act.wait_ge(hidden, freed(n))
                nc.scalar.activation(src_t[k][:, :], p_src[k % 2][:, :], ACT.Copy).then_inc(src_copied, 1)

            def gelu(n, k, q):
                act.wait_ge(hidden, done(n))
                act.wait_ge(logits, freed(n))
                nc.scalar.activation(hid[k][:, :], p_h[:, :], ACT.Gelu, bias=c.b1[:, 0:1]).then_inc(gelu_done, 1)

            def half_sigmoid(n, k, q):
                act.wait_ge(logits, done(n))
                act.wait_ge(w_done, freed(n))
                nc.scalar.activation(tanh[k][:, :], p_w[:, k, :], ACT.Tanh, bias=c.b2[:, 0:1], scale=0.5)\
                    .then_inc(tanh_done, 1)
            pipeline(act, c, "S3 G2 C1", {"C": copy_src, "G": gelu, "S": half_sigmoid})
            act.wait_ge(root_done, 1)
            nc.scalar.activation(root[:, :], root[:, :], ACT.Sqrt).then_inc(root_done, 1)

        @block.vector
        def _(dve):
            v = nc.vector
            credit(dve, dst_copied, w_done, marked)
            for k in range(SLOTS):
                v.memset(src_rows[k][:, :, D + 1:RW], 0.0)
            v.memset(zero[:, :], 0.0).then_inc(cleared, 1)

            def mark(n, k, q):
                dve.wait_ge(kept[k], 16 * q + 16)
                v.tensor_copy(src_rows[k][:, :, D], c.dst_f[:, ds(TILES * n, TILES)]).then_inc(marked, 1)

            def high(n, k, q):
                dve.wait_ge(deg_added, freed(n))
                v.tensor_tensor(hot_hi[k][:, :, :], over_cols(c.dst_hi[:, ds(TILES * n, TILES)], c.tiles),
                                over_rows(c.iota_t[:, :], TILES), ALU.is_equal)

            def copy_dst(n, k, q):
                dve.wait_ge(turned, done(n))
                dve.wait_ge(hidden, freed(n))
                v.tensor_copy(dst_t[k][:, :], p_dst[k % 2][:, :]).then_inc(dst_copied, 1)

            def weights(n, k, q):
                dve.wait_ge(tanh_done, done(n))
                v.tensor_scalar(wk[k][:, :], tanh[k][:, :], 0.5, 0.5, ALU.mult, ALU.add).then_inc(w_done, 1)
                dve.wait_ge(w_done, done(n))
                v.tensor_copy(c.w_all[:, ds(TILES * n, TILES)], wk[k][:, :])
                for j in range(TILES):
                    ins = v.tensor_scalar(hot_lo[k][:, j, :], c.iota[:, :], c.dst_lo[:, ds(TILES * n + j, 1)],
                                          wk[k][:, j:j + 1], ALU.is_equal, ALU.mult)
                ins.then_inc(hot, 1)
            pipeline(dve, c, "M1 X4 W4 C1", {"M": mark, "C": copy_dst, "X": high, "W": weights})
            dve.wait_ge(deg_added, done(c.batches - 1))
            v.tensor_scalar(root[:, :], p_deg[:, :], 1.0, None, ALU.add).then_inc(root_done, 1)
            dve.wait_ge(root_done, 2)
            v.reciprocal(c.dinv[:, 0:c.tiles], root[:, :]).then_inc(root_done, 1)


class Extras:

    def __init__(self, nc, c, sb, sem, name):
        self.nc, self.c = nc, c
        self.rows = sb(f"{name}_rows", [P, XJ, D])
        self.val = sb(f"{name}_val", [P, XJ, 2])
        self.place = sb(f"{name}_place", [P, XJ])
        self.hot = sb(f"{name}_hot", [P, XJ, P])
        self.free, self.loaded, self.hot_done, self.place_done = (
            sem(f"{name}_{n}") for n in ("free", "loaded", "hot_done", "place_done"))

    def start(self, pe):
        pe.sem_inc(self.free, 1)

    def _each(self, eng, tile, body):
        count = eng.value_load(self.c.extra[0:1, ds(tile, 1)], min_val=0, max_val=self.c.E // XW + 1)
        with eng.If(count > 0):
            with eng.Fori(0, count) as i:
                body(i)
        with eng.Else():
            eng.sem_inc(self.c.none, 1)

    def load(self, sp, tile, table):
        start = sp.value_load(self.c.starts[0:1, ds(tile, 1)], min_val=0, max_val=self.c.E)

        def one(i):
            sp.wait_ge(self.free, 1)
            sp.sem_clear(self.free)
            at = self.nc.s_assert_within(start + EDGE + i * XW, 0, EDGE + self.c.E,
                                         skip_runtime_bounds_check_because="a further window starts before its tile's last edge")
            sp.dma_start(self.rows[:, :, :], table[ds(at, XW), 0:D].rearrange("(p j) f -> p j f", j=XJ))\
                .then_inc(self.loaded, 16)
            sp.dma_start(self.val[:, :, :], self.c.rec0[ds(at, XW), D:RW].rearrange("(p j) f -> p j f", j=XJ))\
                .then_inc(self.loaded, 16)
        self._each(sp, tile, one)

    def one_hot(self, dve, tile, weigh):
        v = self.nc.vector

        def one(i):
            dve.wait_ge(self.loaded, 32)
            dve.sem_clear(self.loaded)
            v.tensor_scalar(self.place[:, :], self.val[:, :, 0], self.c.base[:, ds(tile, 1)], None,
                            ALU.subtract).then_inc(self.place_done, 1)
            dve.wait_ge(self.place_done, 1)
            dve.sem_clear(self.place_done)
            for j in range(XJ):
                if weigh:
                    ins = v.tensor_scalar(self.hot[:, j, :], self.c.iota[:, :], self.place[:, j:j + 1],
                                          self.val[:, j, 1:2], ALU.is_equal, ALU.mult)
                else:
                    ins = v.tensor_scalar(self.hot[:, j, :], self.c.iota[:, :], self.place[:, j:j + 1], None,
                                          ALU.is_equal)
            ins.then_inc(self.hot_done, 1)
        self._each(dve, tile, one)

    def add(self, pe, tile, out):
        def one(i):
            pe.wait_ge(self.hot_done, 1)
            pe.sem_clear(self.hot_done)
            for j in range(XJ):
                mm = self.nc.tensor.matmul(out, self.rows[:, j, :], self.hot[:, j, :], start=False,
                                             stop=False, skip_group_check=True)
            mm.then_inc(self.free, 1)
        self._each(pe, tile, one)


def aggregate(nc, c, pe, ex, g, out, rows, win, hot, general):
    for q in range(TILES):
        cols = slice(q * P, (q + 1) * P)
        mm = nc.tensor.matmul(out[:, cols], rows[:, q, :], c.ident[:, :], start=True, stop=False, skip_group_check=True)
        if general:
            ex.add(pe, g * TILES + q, out[:, cols])
        else:
            for j in range(2):
                mm = nc.tensor.matmul(out[:, cols], win[:, q + j, 0:D], hot[:, 2 * q + j, :],
                                      start=False, stop=(j == 1), skip_group_check=True)
    if general:
        mm = nc.tensor.matmul(out[:, cols], c.none_row[0:1, 0:P], c.ones_row[0:1, :], start=False, stop=True,
                              skip_group_check=True)
    return mm


class LayerNorm:

    def __init__(self, nc, c, sb, sem, name):
        slots = lambda make, what, *args: [make(f"{name}_{what}{k}", *args) for k in range(SLOTS)]
        self.nc = nc
        self.y = slots(sb, "y", [P, TILES, D])
        self.out = slots(sb, "out", [P, TILES, D])
        self.stats = slots(sb, "stats", [P, TILES, 6])
        self.mv = slots(sb, "mv", [P, TILES, 2])
        self.std = slots(sb, "std", [P, TILES])
        self.rstd = slots(sb, "rstd", [P, TILES])
        self.shift = slots(sb, "shift", [P, TILES])
        self.y_done, self.stats_done, self.mean_done, self.var_done, self.root_done, self.rstd_done, self.shift_done, self.normed = (
            sem(f"{name}_{n}") for n in ("y_done", "stats_done", "mean_done", "var_done", "root_done", "rstd_done",
                                         "shift_done", "normed"))
        self.stored, self.none = slots(sem, "stored"), c.none

    def start_vector(self, dve):
        credit(dve, self.y_done, self.stats_done, self.mean_done, self.var_done, self.rstd_done, self.shift_done)

    def start_scalar(self, act):
        credit(act, self.root_done, self.normed)
        credit(act, *self.stored, by=16)

    def statistics(self, dve, n, k):
        v = self.nc.vector
        dve.wait_ge(self.y_done, done(n))
        for q in range(TILES):
            ins = v.bn_stats(self.stats[k][:, q, :], self.y[k][:, q, :])
        ins.then_inc(self.stats_done, 1)
        dve.wait_ge(self.stats_done, done(n))
        dve.sem_inc(self.none, 1)
        for q in range(TILES):
            ins = v.bn_aggr(self.mv[k][:, q, :], self.stats[k][:, q, :])
        ins.then_inc(self.mean_done, 1)
        dve.wait_ge(self.mean_done, done(n))
        v.tensor_scalar(self.std[k][:, :], self.mv[k][:, :, 1], EPS, None, ALU.add).then_inc(self.var_done, 1)

    def root(self, act, n, k):
        act.wait_ge(self.var_done, done(n))
        self.nc.scalar.activation(self.std[k][:, :], self.std[k][:, :], ACT.Sqrt).then_inc(self.root_done, 1)

    def scales(self, dve, n, k):
        v = self.nc.vector
        dve.wait_ge(self.root_done, done(n))
        dve.wait_ge(self.normed, freed(n))
        v.reciprocal(self.rstd[k][:, :], self.std[k][:, :]).then_inc(self.rstd_done, 1)
        dve.wait_ge(self.rstd_done, done(n))
        v.scalar_tensor_tensor(self.shift[k][:, :], self.mv[k][:, :, 0], -1.0, self.rstd[k][:, :], ALU.mult,
                               ALU.mult).then_inc(self.shift_done, 1)

    def apply(self, act, n, k, q, to):
        act.wait_ge(self.shift_done, done(n))
        act.wait_ge(self.stored[k], 16 * q + 16)
        for t in range(TILES):
            ins = self.nc.scalar.activation(self.out[k][:, t, :], self.y[k][:, t, :], ACT.Identity,
                                            bias=self.shift[k][:, t:t + 1], scale=self.rstd[k][:, t:t + 1])
        ins.then_inc(self.normed, 1)
        act.wait_ge(self.normed, done(n))
        act.dma_start(to, self.out[k][:, :, :]).then_inc(self.stored[k], 16)

    def finish(self, act, c):
        for k in range(SLOTS):
            act.wait_ge(self.stored[k], 16 * c.uses(k) + 16)


def load_windows(sp, c, s, ex, g, k, q, table, rows_of, rows, win, general):
    for slot in range(SLOTS):
        if general:
            upto = c.uses(slot)
        else:
            upto = q + 1 + (k + LAG - 1 - slot) // SLOTS
            upto = min(upto, c.uses(slot)) if isinstance(q, int) else upto
        sp.wait_ge(s.edges_out[slot], 16 * upto + 16)
        sp.sem_inc(c.none, 1)
    sp.wait_ge(s.agg_done, freed(g))
    sp.sem_inc(c.none, 1)
    sp.wait_ge(s.prepared, freed(g))
    sp.sem_inc(c.none, 1)
    sp.dma_start(rows[k][:, :, :], node_rows(rows_of, g)).then_inc(s.win_in[k], 16)
    middle = sp.value_load(c.starts[0:1, ds(g * TILES + TILES // 2, 1)], min_val=0, max_val=c.E)
    sp.dma_start(win[k][:, :, :], window(table, middle)).then_inc(s.win_in[k], 16)
    if general:
        for t in range(TILES):
            ex.load(sp, g * TILES + t, table)


def build_gcn(nc, c, a):
    with semaphores(nc, "b") as sem, ExitStack() as ctx:
        sb = lambda name, shape, dt=F32: ctx.enter_context(nc.sbuf_tensor(f"b_{name}", shape, dt))
        slots = lambda make, name, *args: [make(f"{name}{k}", *args) for k in range(SLOTS)]
        psum = lambda name, shape: ctx.enter_context(nc.psum_tensor(f"bp_{name}", shape, F32))
        idx = slots(sb, "idx", [P, TILES], I32)
        dsrc = slots(sb, "dsrc", [P, TILES])
        scale = slots(sb, "scale", [P, TILES, 1])
        win = slots(sb, "win", [P, CHUNKS, RW])
        place = slots(sb, "place", [P, TILES, 2])
        hot = slots(sb, "hot", [P, PAIRS, P])
        rows = slots(sb, "rows", [P, TILES, D])
        own = slots(sb, "own", [P, TILES, D])
        resid = slots(sb, "resid", [P, TILES, D])
        summed = slots(sb, "summed", [P, G])
        p_sum, p_out = ([psum(f"{n}{k}", [P, G]) for k in range(4)] for n in ("sum", "out"))
        ex = Extras(nc, c, sb, sem, "x")
        ln = LayerNorm(nc, c, sb, sem, "ln")
        s = Names(**{n: sem(n) for n in (
            "scaled", "placed", "prepared", "own_done", "agg_done", "sum_copied", "projected")})
        s.idx_in, s.edges_out, s.win_in = (slots(sem, n) for n in ("idx_in", "edges_out", "win_in"))
        s.gathered = c.gathered[1]
        LOADS = 16 * 2
        ROWS = 16 * TILES
        block = ctx.enter_context(nc.Block())

        @block.sync
        def _(sp):
            for k in range(SLOTS):
                sp.dma_start(idx[k][:, :], c.spread_idx[k * P:(k + 1) * P, :]).then_inc(s.idx_in[k], 16)

            def fetch(n, k, q):
                sp.wait_ge(s.gathered[k], ROWS * q + ROWS)
                sp.sem_inc(c.none, 1)
                sp.dma_start(idx[k][:, :], c.spread_idx[ds((n + SLOTS) * P, P), :]).then_inc(s.idx_in[k], 16)

            def windows(general):
                return {"W": lambda g, k, q: load_windows(sp, c, s, ex, g, k, q, c.rec0, a.x, rows, win, general)}
            interleave(sp, c, "F0 W5", {"F": fetch}, windows(False), windows(True))
            for k in range(SLOTS):
                sp.wait_ge(s.idx_in[k], 16 * c.uses(k) + 16)

        @block.gpsimd
        def _(pool):
            def gather(n, k, q):
                pool.wait_ge(s.idx_in[k], 16 * q + 16)
                pool.sem_inc(c.none, 1)
                pool.wait_ge(s.scaled, freed(n))
                pool.sem_inc(c.none, 1)
                for j in range(TILES):
                    nc.gpsimd.indirect_dma_start(
                        dsrc[k][:, j:j + 1], None, c.dinv_d[:, :],
                        bass.IndirectOffsetOnAxis(ap=idx[k][:, j:j + 1], axis=0)).then_inc(s.gathered[k], 16)
            pipeline(pool, c, "G0", {"G": gather})

        @block.tensor
        def _(pe):
            credit(pe, s.agg_done, s.projected)
            ex.start(pe)

            def sums(general):
                def step(g, k, q):
                    pe.wait_ge(s.prepared, done(g))
                    pe.wait_ge(s.own_done, done(g))
                    pe.wait_ge(s.win_in[k], LOADS * q + LOADS)
                    pe.wait_ge(s.sum_copied, freed(g))
                    aggregate(nc, c, pe, ex, g, p_sum[k], own[k], win[k], hot[k], general).then_inc(s.agg_done, 1)
                return step

            def project(g, k, q):
                pe.wait_ge(s.sum_copied, done(g))
                pe.wait_ge(ln.y_done, freed(g))
                for t in range(TILES):
                    mm = nc.tensor.matmul(p_out[k][:, t * P:(t + 1) * P], summed[k][:, t * P:(t + 1) * P],
                                          c.conv_w[:, :], start=True, stop=True)
                mm.then_inc(s.projected, 1)
            interleave(pe, c, "O8 A7", {}, {"A": sums(False), "O": project},
                       {"A": sums(True), "O": project})

        @block.scalar
        def _(act):
            credit(act, s.sum_copied, s.own_done)
            credit(act, *s.edges_out, by=16)
            ln.start_scalar(act)
            act.preload_act_table(ACT.Sqrt)

            def store_scales(n, k, q):
                act.wait_ge(s.scaled, done(n))
                with nc.allow_non_contiguous_dma(reason="one value of each kept row"):
                    act.dma_start(edge_rows(kept_rows(c, c.rec0), n)[:, :, D + 1:RW], scale[k][:, :, :])\
                        .then_inc(s.edges_out[k], 16)

            def own_rows(g, k, q):
                act.wait_ge(s.win_in[k], LOADS * q + LOADS)
                act.wait_ge(s.agg_done, freed(g))
                for t in range(TILES):
                    ins = nc.scalar.activation(own[k][:, t, :], rows[k][:, t, :], ACT.Copy,
                                               scale=c.dinv[:, ds(g * TILES + t, 1)])
                ins.then_inc(s.own_done, 1)

            def copy_sums(g, k, q):
                act.wait_ge(s.agg_done, done(g))
                act.wait_ge(s.projected, freed(g))
                nc.scalar.activation(summed[k][:, :], p_sum[k][:, :], ACT.Copy).then_inc(s.sum_copied, 1)
            interleave(act, c, "E0 X6 C7 N10 R9",
                       {"E": store_scales},
                       {"X": own_rows, "C": copy_sums, "R": lambda g, k, q: ln.root(act, g, k),
                        "N": lambda g, k, q: ln.apply(act, g, k, q, node_rows(c.x1, g))})
            for k in range(SLOTS):
                act.wait_ge(s.edges_out[k], 16 * c.uses(k) + 16)
            ln.finish(act, c)

        @block.vector
        def _(dve):
            v = nc.vector
            credit(dve, s.scaled, s.placed, s.prepared)
            ln.start_vector(dve)

            def scales(n, k, q):
                dve.wait_ge(s.gathered[k], ROWS * q + ROWS)
                dve.wait_ge(s.edges_out[k], 16 * q + 16)
                v.tensor_tensor(scale[k][:, :, 0], dsrc[k][:, :], c.w_all[:, ds(TILES * n, TILES)], ALU.mult)\
                    .then_inc(s.scaled, 1)

            def prepare(general):
                def step(g, k, q):
                    dve.wait_ge(s.win_in[k], LOADS * q + LOADS)
                    dve.wait_ge(s.agg_done, freed(g))
                    for j in range(2):
                        ins = v.tensor_tensor(place[k][:, :, j], win[k][:, j:j + TILES, D],
                                              c.base[:, ds(g * TILES, TILES)], ALU.subtract)
                    ins.then_inc(s.placed, 1)
                    v.tensor_tensor(resid[k][:, :, :], rows[k][:, :, :], over_rows(c.conv_b[:, :], TILES), ALU.add)
                    dve.wait_ge(s.placed, done(g))
                    v.tensor_copy(c.place[:, ds(g * PAIRS, PAIRS)], place[k][:, :, :].rearrange("p t j -> p (t j)"))
                    for t in range(TILES):
                        for j in range(2):
                            ins = v.tensor_scalar(hot[k][:, 2 * t + j, :], c.iota[:, :], place[k][:, t, j:j + 1],
                                                  win[k][:, t + j, D + 1:RW], ALU.is_equal, ALU.mult)
                    ins.then_inc(s.prepared, 1)
                    if general:
                        for t in range(TILES):
                            ex.one_hot(dve, g * TILES + t, weigh=True)
                return step

            def residual(g, k, q):
                dve.wait_ge(s.projected, done(g))
                dve.wait_ge(s.prepared, done(g))
                dve.wait_ge(ln.normed, freed(g))
                for t in range(TILES):
                    ins = v.scalar_tensor_tensor(ln.y[k][:, t, :], p_out[k][:, t * P:(t + 1) * P],
                                                 c.dinv[:, ds(g * TILES + t, 1)], resid[k][:, t, :], ALU.mult, ALU.add)
                ins.then_inc(ln.y_done, 1)
                ln.statistics(dve, g, k)
            common = {"Y": residual, "S": lambda g, k, q: ln.scales(dve, g, k)}
            interleave(dve, c, "E0 P6 S10 Y9", {"E": scales},
                       {"P": prepare(False), **common}, {"P": prepare(True), **common})


def build_gine(nc, c, a, layer, h_in):
    last = layer == 1
    with semaphores(nc, "cd"[layer]) as sem, ExitStack() as ctx:
        tag = "cd"[layer]
        sb = lambda name, shape, dt=F32: ctx.enter_context(nc.sbuf_tensor(f"{tag}_{name}", shape, dt))
        slots = lambda make, name, *args: [make(f"{name}{k}", *args) for k in range(SLOTS)]
        psum = lambda name, shape: ctx.enter_context(nc.psum_tensor(f"{tag}p_{name}", shape, F32))
        idx = slots(sb, "idx", [P, 2 * TILES], I32)
        attr = slots(sb, "attr", [c.K + 1, G])
        src_rows = slots(sb, "src_rows", [P, TILES, D])
        msg = slots(sb, "msg", [P, TILES, D])
        win = slots(sb, "win", [P, CHUNKS, D])
        hot = slots(sb, "hot", [P, PAIRS, P])
        rows = slots(sb, "rows", [P, TILES, D])
        summed = slots(sb, "summed", [P, G])
        hid = slots(sb, "hid", [P, G])
        out = slots(sb, "out", [P, TILES, D])
        bn = sb("bn", [P, c.groups, 6])
        mv = sb("mv", [P, 2])
        p_edge, p_sum, p_hid, p_out = ([psum(f"{n}{k}", [P, G]) for k in range(2)] for n in ("edge", "sum", "hid", "out"))
        ex = Extras(nc, c, sb, sem, "x")
        s = Names(**{n: sem(n) for n in (
            "lifted", "added", "msg_done", "prepared", "agg_done", "sum_copied", "hidden", "hid_done",
            "projected", "read", "out_done", "bn_done")})
        s.idx_in, s.attr_in, s.edges_out, s.win_in, s.stored = (
            slots(sem, n) for n in ("idx_in", "attr_in", "edges_out", "win_in", "stored"))
        s.gathered = c.gathered[2 + layer]
        LOADS = 16 * 2
        ROWS = 16 * TILES
        block = ctx.enter_context(nc.Block())

        @block.sync
        def _(sp):
            for k in range(SLOTS):
                sp.dma_start(idx[k][:, :], a.edge_idx[k * P:(k + 1) * P, :]).then_inc(s.idx_in[k], 16)

            def attributes(n, k, q):
                sp.wait_ge(s.lifted, freed(n))
                sp.sem_inc(c.none, 1)
                sp.dma_start(attr[k][:, :], a.edge_attr[:, ds(n * G, G)]).then_inc(s.attr_in[k], 16)

            def fetch(n, k, q):
                sp.wait_ge(s.gathered[k], ROWS * q + ROWS)
                sp.sem_inc(c.none, 1)
                sp.dma_start(idx[k][:, :], a.edge_idx[ds((n + SLOTS) * P, P), :]).then_inc(s.idx_in[k], 16)

            def windows(general):
                return {"W": lambda g, k, q: load_windows(sp, c, s, ex, g, k, q, c.rec1, h_in, rows, win, general)}
            interleave(sp, c, "B0 F0 W6", {"B": attributes, "F": fetch},
                       windows(False), windows(True))
            for k in range(SLOTS):
                sp.wait_ge(s.idx_in[k], 16 * c.uses(k) + 16)

        @block.gpsimd
        def _(pool):
            def gather(n, k, q):
                pool.wait_ge(s.idx_in[k], 16 * q + 16)
                pool.sem_inc(c.none, 1)
                pool.wait_ge(s.added, freed(n))
                pool.sem_inc(c.none, 1)
                for j in range(TILES):
                    nc.gpsimd.indirect_dma_start(
                        src_rows[k][:, j, :], None, h_in,
                        bass.IndirectOffsetOnAxis(ap=idx[k][:, j:j + 1], axis=0)).then_inc(s.gathered[k], 16)
            pipeline(pool, c, "G0", {"G": gather})

        @block.tensor
        def _(pe):
            credit(pe, s.lifted, s.agg_done, s.hidden, s.projected)
            ex.start(pe)

            def lift(n, k, q):
                pe.wait_ge(s.attr_in[k], 16 * q + 16)
                pe.wait_ge(s.added, done(n - 2))
                for j in range(TILES):
                    mm = nc.tensor.matmul(p_edge[k % 2][:, j * P:(j + 1) * P], attr[k][:, j * P:(j + 1) * P],
                                          c.We[:, layer, :], start=True, stop=True)
                mm.then_inc(s.lifted, 1)

            def sums(general):
                def step(g, k, q):
                    pe.wait_ge(s.prepared, done(g))
                    pe.wait_ge(s.win_in[k], LOADS * q + LOADS)
                    pe.wait_ge(s.sum_copied, done(g - 2))
                    aggregate(nc, c, pe, ex, g, p_sum[k % 2], rows[k], win[k], hot[k], general).then_inc(s.agg_done, 1)
                return step

            def hidden_layer(g, k, q):
                pe.wait_ge(s.sum_copied, done(g))
                pe.wait_ge(s.hid_done, done(g - 2))
                nc.tensor.matmul(p_hid[k % 2][:, :], c.Wa[:, layer, :], summed[k][:, :], start=True, stop=True)\
                    .then_inc(s.hidden, 1)

            def project(g, k, q):
                pe.wait_ge(s.hid_done, done(g))
                pe.wait_ge(s.read, done(g - 2))
                if last:
                    mm = nc.tensor.matmul(p_out[k % 2][:, :], c.Wb[:, layer, :], hid[k][:, :], start=True, stop=True)
                else:
                    for t in range(TILES):
                        mm = nc.tensor.matmul(p_out[k % 2][:, t * P:(t + 1) * P], hid[k][:, t * P:(t + 1) * P],
                                              c.Wb[:, layer, :], start=True, stop=True)
                mm.then_inc(s.projected, 1)
            common = {"H": hidden_layer, "O": project}
            interleave(pe, c, "E1 O9 H8 A7", {"E": lift},
                       {"A": sums(False), **common}, {"A": sums(True), **common})

        @block.scalar
        def _(act):
            credit(act, s.msg_done, s.sum_copied, s.hid_done, s.out_done)
            credit(act, *s.edges_out, *s.stored, by=16)
            act.preload_act_table(ACT.Relu)

            def messages(n, k, q):
                act.wait_ge(s.added, done(n))
                nc.scalar.activation(msg[k][:, :, :], msg[k][:, :, :], ACT.Relu).then_inc(s.msg_done, 1)
                act.wait_ge(s.msg_done, done(n))
                act.dma_start(edge_rows(kept_rows(c, c.rec1), n), msg[k][:, :, :]).then_inc(s.edges_out[k], 16)

            def copy_sums(g, k, q):
                act.wait_ge(s.agg_done, done(g))
                act.wait_ge(s.hidden, freed(g))
                nc.scalar.activation(summed[k][:, :], p_sum[k % 2][:, :], ACT.Copy).then_inc(s.sum_copied, 1)

            def relu_hidden(g, k, q):
                act.wait_ge(s.hidden, done(g))
                act.wait_ge(s.projected, freed(g))
                if last:
                    act.wait_ge(s.stored[k], 16 * q + 16)
                nc.scalar.activation(hid[k][:, :], p_hid[k % 2][:, :], ACT.Relu, bias=c.ba[:, layer:layer + 1])\
                    .then_inc(s.hid_done, 1)

            def store(g, k, q):
                if last:
                    act.wait_ge(s.hid_done, done(g))
                    act.dma_start(c.hid_d[:, ds(g * G, G)], hid[k][:, :]).then_inc(s.stored[k], 16)
                else:
                    act.wait_ge(s.read, done(g))
                    nc.scalar.activation(out[k][:, :, :], out[k][:, :, :], ACT.Relu).then_inc(s.out_done, 1)
                    act.wait_ge(s.out_done, done(g))
                    act.dma_start(node_rows(c.h1, g), out[k][:, :, :]).then_inc(s.stored[k], 16)
            interleave(act, c, "E1 S10 H8 C7", {"E": messages},
                       {"C": copy_sums, "H": relu_hidden, "S": store})
            for k in range(SLOTS):
                act.wait_ge(s.edges_out[k], 16 * c.uses(k) + 16)
                act.wait_ge(s.stored[k], 16 * c.uses(k) + 16)

        @block.vector
        def _(dve):
            v = nc.vector
            credit(dve, s.added, s.prepared, s.read)

            def add(n, k, q):
                dve.wait_ge(s.gathered[k], ROWS * q + ROWS)
                dve.wait_ge(s.lifted, done(n))
                dve.wait_ge(s.edges_out[k], 16 * q + 16)
                v.tensor_tensor(msg[k][:, :, :], p_edge[k % 2][:, :].rearrange("p (j f) -> p j f", j=TILES),
                                src_rows[k][:, :, :], ALU.add).then_inc(s.added, 1)

            def prepare(general):
                def step(g, k, q):
                    dve.wait_ge(s.agg_done, freed(g))
                    v.tensor_tensor(hot[k][:, :, :], over_cols(c.place[:, ds(g * PAIRS, PAIRS)], P),
                                    over_rows(c.iota[:, :], PAIRS), ALU.is_equal).then_inc(s.prepared, 1)
                    if general:
                        for t in range(TILES):
                            ex.one_hot(dve, g * TILES + t, weigh=False)
                return step

            def read(g, k, q):
                dve.wait_ge(s.projected, done(g))
                if last:
                    cols = min(G, c.n_nodes - g * G) if isinstance(g, int) else G
                    v.bn_stats(bn[:, ds(g, 1), :].rearrange("p a s -> p (a s)"), p_out[k % 2][:, 0:cols]).then_inc(s.read, 1)
                else:
                    dve.wait_ge(s.stored[k], 16 * q + 16)
                    v.tensor_tensor(out[k][:, :, :], p_out[k % 2][:, :].rearrange("p (t f) -> p t f", t=TILES),
                                    over_rows(c.bb[:, :], TILES), ALU.add).then_inc(s.read, 1)
            interleave(dve, c, "E1 P6 R10", {"E": add},
                       {"P": prepare(False), "R": read}, {"P": prepare(True), "R": read})
            if last:
                dve.wait_ge(s.read, done(c.groups - 1))
                v.bn_aggr(mv[:, :], bn[:, :, :].rearrange("p g s -> p (g s)")).then_inc(s.bn_done, 1)
                dve.wait_ge(s.bn_done, 1)
                v.tensor_tensor(c.bn_mean[:, :], mv[:, 0:1], c.b4[:, :], ALU.add)
                v.tensor_scalar(c.bn_var[:, :], mv[:, 1:2], EPS, None, ALU.add)


def build_final(nc, c, a):
    with semaphores(nc, "e") as sem, ExitStack() as ctx:
        sb = lambda name, shape, dt=F32: ctx.enter_context(nc.sbuf_tensor(name, shape, dt))
        slots = lambda make, name, *args: [make(f"{name}{k}", *args) for k in range(SLOTS)]
        psum = lambda name, shape: ctx.enter_context(nc.psum_tensor(name, shape, F32))
        col = sb("e_col", [P, 4])
        diag = sb("e_diag", [P, 2, P])
        ones = sb("e_ones", [P, P])
        row = sb("e_row", [P, 2, P])
        Wn = sb("e_Wn", [P, D])
        hid = slots(sb, "e_hid", [P, G])
        rows = slots(sb, "e_rows", [P, TILES, D])
        p_out = slots(psum, "ep_out", [P, G])
        p_row = psum("ep_row", [P, 2 * P])
        ln = LayerNorm(nc, c, sb, sem, "e_ln")
        step, projected, p_done = sem("step"), sem("projected"), sem("row_done")
        loaded = slots(sem, "loaded")
        STEPS = 9
        block = ctx.enter_context(nc.Block())

        @block.sync
        def _(sp):
            def load(g, k, q):
                sp.wait_ge(projected, freed(g))
                sp.sem_inc(c.none, 1)
                sp.wait_ge(ln.y_done, freed(g))
                sp.sem_inc(c.none, 1)
                sp.dma_start(hid[k][:, :], c.hid_d[:, ds(g * G, G)]).then_inc(loaded[k], 16)
                sp.dma_start(rows[k][:, :, :], node_rows(c.x1, g)).then_inc(loaded[k], 16)
            pipeline(sp, c, "L0", {"L": load})

        @block.tensor
        def _(pe):
            credit(pe, projected)
            pe.wait_ge(step, 7)
            nc.tensor.matmul(p_row[:, :], ones[:, :], diag[:, :, :].rearrange("p a f -> p (a f)"), start=True,
                             stop=True).then_inc(p_done, 1)
            pe.wait_ge(step, STEPS)

            def project(g, k, q):
                pe.wait_ge(loaded[k], 32 * q + 32)
                pe.wait_ge(ln.y_done, freed(g))
                for t in range(TILES):
                    cols = slice(t * P, (t + 1) * P)
                    nc.tensor.matmul(p_out[k][:, cols], hid[k][:, cols], Wn[:, :], start=True, stop=False,
                                     skip_group_check=True)
                    mm = nc.tensor.matmul(p_out[k][:, cols], c.ones_row[0:1, :], row[0:1, 1, :], start=False,
                                          stop=True, skip_group_check=True)
                mm.then_inc(projected, 1)
            pipeline(pe, c, "O1", {"O": project})

        @block.scalar
        def _(act):
            ln.start_scalar(act)
            act.preload_act_table(ACT.Sqrt)
            nc.scalar.activation(col[:, 0:1], c.bn_var[:, :], ACT.Sqrt).then_inc(step, 1)

            pipeline(act, c, "N3 R2",
                  {"R": lambda g, k, q: ln.root(act, g, k),
                   "N": lambda g, k, q: ln.apply(act, g, k, q, node_rows(a.out, g))})
            ln.finish(act, c)

        @block.vector
        def _(dve):
            v = nc.vector
            ln.start_vector(dve)
            n = [1]

            def link(ins):
                n[0] += 1
                ins.then_inc(step, 1)
                dve.wait_ge(step, n[0])

            v.memset(ones[:, :], 1.0)
            dve.wait_ge(step, 1)
            link(v.reciprocal(col[:, 1:2], col[:, 0:1]))
            link(v.tensor_tensor(col[:, 2:3], col[:, 1:2], c.gamma[:, :], ALU.mult))
            link(v.tensor_tensor(col[:, 3:4], c.b4[:, :], c.bn_mean[:, :], ALU.subtract))
            link(v.scalar_tensor_tensor(col[:, 3:4], col[:, 3:4], col[:, 2:3], c.beta[:, :], ALU.mult, ALU.add))
            link(v.tensor_scalar(diag[:, 0, :], c.ident[:, :], col[:, 2:3], None, ALU.mult))
            link(v.tensor_scalar(diag[:, 1, :], c.ident[:, :], col[:, 3:4], None, ALU.mult))
            dve.wait_ge(p_done, 1)
            link(v.tensor_copy(row[:, :, :], p_row[:, :].rearrange("p (a f) -> p a f", a=2)))
            link(v.tensor_tensor(Wn[:, :], c.Wb[:, 1, :], row[:, 0, :], ALU.mult))
            assert n[0] == STEPS

            def add(g, k, q):
                dve.wait_ge(projected, done(g))
                dve.wait_ge(loaded[k], 32 * q + 32)
                dve.wait_ge(ln.normed, freed(g))
                v.tensor_tensor(ln.y[k][:, :, :], p_out[k][:, :].rearrange("p (t f) -> p t f", t=TILES),
                                rows[k][:, :, :], ALU.add).then_inc(ln.y_done, 1)
                ln.statistics(dve, g, k)
            pipeline(dve, c, "S3 Y2", {"Y": add, "S": lambda g, k, q: ln.scales(dve, g, k)})


def build(nc, a, n_nodes):
    c = Names(nc=nc, n_nodes=n_nodes)
    c.N = a.x.shape[0]
    c.E = a.edge_attr.shape[1]
    c.K = a.edge_attr.shape[0] - 1
    c.M = a.mlp_b1.shape[0]
    c.tiles, c.groups, c.batches, c.cols = c.N // P, c.N // G, c.E // G, c.E // P
    c.full, c.rest = c.batches // SLOTS, c.batches % SLOTS
    c.uses = lambda k: c.full + (k < c.rest)
    assert c.groups == c.batches and c.rest and (c.groups - 1) * G < n_nodes and c.full > 1
    assert c.tiles <= min(SPREAD, 512) and (c.tiles // 16 + 1) <= P
    dram = lambda name, shape, dt=F32: nc.dram_tensor(f"t_{name}", shape, dt).ap()
    c.rec0, c.rec1 = dram("rec0", [c.E + 2 * EDGE, RW]), dram("rec1", [c.E + 2 * EDGE, D])
    c.x1, c.h1, c.hid_d = dram("x1", [c.N, D]), dram("h1", [c.N, D]), dram("hid_d", [D, c.N])
    c.dinv_d, c.spread_idx = dram("dinv_d", [P * SPREAD, 1]), dram("spread_idx", [(c.batches + SLOTS) * P, TILES], I32)
    c.hist_d = dram("hist_d", [16 * (c.tiles // 16 + 1)])
    with ExitStack() as ctx:
        sb = lambda name, shape, dt=F32: ctx.enter_context(nc.sbuf_tensor(f"c_{name}", shape, dt))
        c.none = ctx.enter_context(nc.semaphore("none"))
        c.gathered = [[ctx.enter_context(nc.semaphore(f"gathered_{tag}{k}")) for k in range(SLOTS)] for tag in "abcd"]
        c.ident, c.iota, c.iota_t = sb("ident", [P, P]), sb("iota", [P, P]), sb("iota_t", [P, c.tiles])
        c.iota_t_i = sb("iota_t_i", [P, c.tiles], I32)
        c.ones_row, c.none_row = sb("ones_row", [1, P]), sb("none_row", [1, P])
        c.W1, c.b1, c.w2, c.b2 = sb("W1", [D, 2, c.M]), sb("b1", [c.M, 1]), sb("w2", [c.M, 1]), sb("b2", [P, 1])
        c.conv_w, c.conv_b = sb("conv_w", [D, D]), sb("conv_b", [P, D])
        c.Wa, c.Wb, c.We = sb("Wa", [D, 2, D]), sb("Wb", [D, 2, D]), sb("We", [c.K + 1, 2, D])
        c.ba, c.bb, c.b4 = sb("ba", [D, 2]), sb("bb", [P, D]), sb("b4", [D, 1])
        c.gamma, c.beta, c.bn_mean, c.bn_var = (sb(n, [D, 1]) for n in ("gamma", "beta", "bn_mean", "bn_var"))
        c.w_all, c.dst_f, c.dst_lo, c.dst_hi = (sb(n, [P, c.cols]) for n in ("w_all", "dst_f", "dst_lo", "dst_hi"))
        c.dinv = sb("dinv", [P, SPREAD])
        c.base, c.place = sb("base", [P, c.tiles]), sb("place", [P, c.groups * PAIRS])
        c.starts, c.extra, c.flag = sb("starts", [1, c.tiles], I32), sb("extra", [1, c.tiles], I32), sb("flag", [1, 1], I32)
        build_setup(nc, c, a)
        build_edge_weights(nc, c, a)
        build_gcn(nc, c, a)
        build_gine(nc, c, a, 0, c.x1)
        build_gine(nc, c, a, 1, c.h1)
        build_final(nc, c, a)


def arrays_of(x, src, dst, edge_attr_64, L0_gnn_mlp_w1, L0_gnn_mlp_b1, L0_gnn_mlp_w2, L0_gnn_mlp_b2, L0_gnn_conv_w,
              L0_gnn_conv_b, L1_gnn_We1, L1_gnn_be1, L1_gnn_W1, L1_gnn_b1, L1_gnn_W2, L1_gnn_b2, L1_gnn_We2, L1_gnn_be2,
              L1_gnn_W3, L1_gnn_b3, L1_gnn_W4, L1_gnn_b4, L1_gnn_gamma, L1_gnn_beta):
    import numpy as np
    n, e = x.shape[0], src.shape[0]
    batches = max(-(-(max(n, e) + 1) // G), 2 * SLOTS + 1)
    batches += batches % SLOTS == 0
    size = batches * G

    def pad(arr, rows, fill=0):
        out = np.full((rows,) + tuple(arr.shape[1:]), fill, arr.dtype)
        out[:arr.shape[0]] = arr
        return out
    pad_nodes = np.minimum(n + np.arange(size - e), size - 1).astype(np.asarray(dst).dtype)
    src_p, dst_p = (np.concatenate([np.asarray(v), pad_nodes]) for v in (src, dst))
    by_batch = lambda v: v.reshape(batches, P, TILES)
    edge_idx = np.concatenate([by_batch(src_p), by_batch(dst_p)], axis=2)
    attr = pad(np.asarray(edge_attr_64), size).reshape(batches, P, TILES, -1)
    attr = attr.transpose(3, 0, 2, 1).reshape(attr.shape[3], size)
    return {
        "x": pad(np.asarray(x), size),
        "dst_order": pad(dst_p, size + 1, size - 1),
        "src_cols": by_batch(src_p).transpose(1, 0, 2).reshape(P, -1),
        "dst_cols": by_batch(dst_p).transpose(1, 0, 2).reshape(P, -1),
        "edge_idx": pad(edge_idx, batches + SLOTS).reshape(-1, 2 * TILES),
        "edge_attr": np.concatenate([attr, np.ones((1, size), attr.dtype)]),
        "mlp_w1": L0_gnn_mlp_w1, "mlp_b1": L0_gnn_mlp_b1, "mlp_w2": L0_gnn_mlp_w2, "mlp_b2": L0_gnn_mlp_b2,
        "conv_w": L0_gnn_conv_w, "conv_b": L0_gnn_conv_b, "We1": L1_gnn_We1, "be1": L1_gnn_be1, "W1": L1_gnn_W1,
        "b1": L1_gnn_b1, "W2": L1_gnn_W2, "b2": L1_gnn_b2, "We2": L1_gnn_We2, "be2": L1_gnn_be2, "W3": L1_gnn_W3,
        "b3": L1_gnn_b3, "W4": L1_gnn_W4, "b4": L1_gnn_b4, "gamma": L1_gnn_gamma, "beta": L1_gnn_beta,
    }


def kernel(**inputs):
    import numpy as np
    import concourse.bacc as bacc
    from concourse.bass_utils import run_bass_kernel_spmd

    arrays = {f"in_{k}": np.ascontiguousarray(v) for k, v in arrays_of(**inputs).items()}
    nc = bacc.Bacc("TRN2", target_bir_lowering=False, num_devices=1)
    a = Names(**{k[3:]: nc.dram_tensor(k, v.shape, mybir.dt.from_np(v.dtype), kind="ExternalInput").ap()
                           for k, v in arrays.items()})
    a.out = nc.dram_tensor("out_rows", a.x.shape, F32, kind="ExternalOutput").ap()
    n_nodes = inputs["x"].shape[0]
    build(nc, a, n_nodes)
    r = run_bass_kernel_spmd(nc, [arrays], core_ids=[0])
    return r.results[0]["out_rows"][:n_nodes]
```

```python
from contextlib import ExitStack, contextmanager

import concourse.bass as bass
from concourse import mybir
from concourse.alu_op_type import AluOpType as ALU

P = 128
TILES = 4
G = TILES * P
CHUNKS = TILES + 1
PAIRS = 2 * TILES
WIN = CHUNKS * P
EDGE = WIN // 2
AHEAD = 6
NEAR = 16
XJ = 2
XW = P * XJ
D = 128
SLOTS = 4
LAG = 2
RW = D + 2
SPREAD = 512
EPS = 1e-5

F32 = mybir.dt.float32
BF16 = mybir.dt.bfloat16
F32R = mybir.dt.float32r
I32 = mybir.dt.int32
ACT = mybir.ActivationFunctionType
AX = mybir.AxisListType


class Names(dict):

    def __getattr__(self, name):
        return self[name]

    def __setattr__(self, name, value):
        self[name] = value


def ds(start, size):
    return bass.ds(start, size)


def over_rows(ap, rows):
    return ap.unsqueeze(1).broadcast_to([ap.shape[0], rows, ap.shape[1]])


def over_cols(ap, cols):
    return ap.unsqueeze(2).broadcast_to([ap.shape[0], ap.shape[1], cols])


def window(table, start):
    return table[ds(start, WIN), :].rearrange("(i p) f -> p i f", p=P)


def kept_rows(c, table):
    return table[EDGE:EDGE + c.E, :]


def node_rows(dram, group):
    return dram[ds(group * G, G), :].rearrange("(q p) f -> p q f", p=P)


def edge_rows(dram, batch):
    return dram[ds(batch * G, G), :].rearrange("(j p) f -> p j f", p=P)


def done(n):
    return n + 1 + SLOTS


def freed(n):
    return n + 1


def credit(eng, *sems, by=SLOTS):
    for s in sems:
        eng.sem_inc(s, by)


@contextmanager
def semaphores(nc, tag, last=False):
    made = []
    with ExitStack() as held:
        def sem(name):
            made.append(held.enter_context(nc.semaphore(f"{tag}_{name}")))
            return made[-1]
        yield sem
        if last:
            return
        with nc.Block() as block:
            def clear(eng, part):
                for s in made[part::4]:
                    eng.sem_clear(s)

            @block.vector
            def _(dve):
                clear(dve, 0)

            @block.tensor
            def _(pe):
                clear(pe, 1)

            @block.scalar
            def _(act):
                clear(act, 2)

            @block.sync
            def _(sp):
                clear(sp, 3)


def pipeline(eng, c, order, steps):
    stages = [(steps[name[0]], int(name[1:])) for name in order.split() if name[0] in steps]
    if not stages:
        return
    lag = max(lag for _, lag in stages)

    def turn(q):
        for k in range(SLOTS):
            for step, back in stages:
                slot, item_turn = (k - back) % SLOTS, q + (k - back) // SLOTS
                n = SLOTS * item_turn + slot
                if not isinstance(q, int) or 0 <= n < c.batches:
                    step(n, slot, item_turn)
    first = min(-(-lag // SLOTS), c.full)
    for q in range(first):
        turn(q)
    if first < c.full:
        with eng.Fori(first, c.full) as q:
            turn(q)
    for q in range(c.full, -(-(c.batches + lag) // SLOTS)):
        turn(q)


def one_by_one(order):
    return " ".join(name[0] + "0" for name in sorted(order.split(), key=lambda name: int(name[1:])))


def interleave(eng, c, order, edges, nodes, nodes_general=None):
    regular = eng.value_load(c.flag[0:1, 0:1], min_val=0, max_val=1)
    with eng.If(regular == 1):
        pipeline(eng, c, order, {**edges, **nodes})
    with eng.Else():
        pipeline(eng, c, one_by_one(order), edges)
        pipeline(eng, c, one_by_one(order), nodes_general or nodes)


def choose(eng, c, flag, order, steps):
    near = eng.value_load(flag[0:1, 0:1], min_val=0, max_val=1)
    with eng.If(near == 1):
        pipeline(eng, c, order, steps(False))
    with eng.Else():
        pipeline(eng, c, order, steps(True))


def build_setup(nc, c, a):
    A_ROWS = c.tiles // 16 + 1
    assert EDGE % (P // 2) == 0 and EDGE >= XW
    with semaphores(nc, "s0") as sem, ExitStack() as ctx:
        sb = lambda name, shape, dt=F32: ctx.enter_context(nc.sbuf_tensor(name, shape, dt))
        iota_i = sb("iota_i", [P, P], I32)
        zeros = sb("zeros", [P, EDGE * RW // P])
        dst_nat = sb("dst_nat", [P, c.cols], I32)
        dst_next = sb("dst_next", [P, c.cols], I32)
        part = sb("part", [P, 2, c.cols], I32)
        part_f = sb("part_f", [P, 2, c.cols])
        hot_a = sb("hot_a", [P, c.cols, A_ROWS], BF16)
        hot_b = sb("hot_b", [P, c.cols, 16], BF16)
        disorder = sb("disorder", [P, c.cols])
        disorder_sum = sb("disorder_sum", [P, 1])
        ones_col = sb("ones_col", [P, 1])
        hist = sb("hist", [A_ROWS, 16])
        row = sb("row", [1, 8, A_ROWS * 16])
        row_i = sb("row_i", [1, A_ROWS * 16], I32)
        late = sb("late", [1, 4])
        ends_i = sb("ends_i", [c.batches, G], I32)
        ends = sb("ends", [c.batches, 2, G])
        offs_i, offs = sb("offs_i", [c.batches, G], I32), sb("offs", [c.batches, G])
        first_i, first = sb("first_i", [c.batches, 1], I32), sb("first", [c.batches, 1])
        rel_i = sb("rel_i", [P, CHUNKS], I32)
        nth_i, nth = sb("nth_i", [P, c.cols], I32), sb("nth", [P, c.cols])
        far = sb("far", [c.batches, 8])
        base_i = sb("base_i", [P, c.tiles], I32)
        off_i = sb("off_i", [1, c.tiles], I32)
        off = sb("off", [1, c.tiles])
        src_i = sb("src_i", [P, c.cols], I32)
        dst_i = sb("dst_i", [P, c.cols], I32)
        bits = sb("bits", [P, 4, c.cols], I32)
        p_hist = ctx.enter_context(nc.psum_tensor("p_hist", [A_ROWS, 16], F32))
        p_dis = ctx.enter_context(nc.psum_tensor("p_dis", [1, 2], F32))
        loaded, consts, made, step, one_hots, counted, hist_done, hist_out, hist_in, pads, kept, near = (sem(n) for n in (
            "loaded", "consts", "made", "step", "one_hots", "counted", "hist_done", "hist_out", "hist_in", "pads", "kept", "near"))
        block = ctx.enter_context(nc.Block())
        t_used = c.tiles
        loads = [
            (c.W1[:, 0, :], a.mlp_w1[0:D, :]), (c.W1[:, 1, :], a.mlp_w1[D:2 * D, :]),
            (c.b1[:, :], a.mlp_b1.unsqueeze(1)), (c.w2[:, :], a.mlp_w2),
            (c.b2[:, :], a.mlp_b2.unsqueeze(0).to_broadcast([P, 1])),
            (c.conv_w[:, :], a.conv_w),
            (c.conv_b[:, :], a.conv_b.unsqueeze(0).to_broadcast([P, D])),
            (c.Wa[:, 0, :], a.W1), (c.Wb[:, 0, :], a.W2), (c.Wa[:, 1, :], a.W3), (c.Wb[:, 1, :], a.W4),
            (c.We[0:c.K, 0, :], a.We1), (c.We[0:c.K, 1, :], a.We2),
            (c.We[c.K:c.K + 1, 0, :], a.be1.unsqueeze(0)), (c.We[c.K:c.K + 1, 1, :], a.be2.unsqueeze(0)),
            (c.ba[:, 0:1], a.b1.unsqueeze(1)), (c.ba[:, 1:2], a.b3.unsqueeze(1)),
            (c.bb[:, :], a.b2.unsqueeze(0).to_broadcast([P, D])),
            (c.b4[:, :], a.b4.unsqueeze(1)), (c.gamma[:, :], a.gamma.unsqueeze(1)),
            (c.beta[:, :], a.beta.unsqueeze(1)),
        ]

        @block.sync
        def _(sp):
            sp.dma_start(dst_nat[:, :], a.dst_order[0:c.E].rearrange("(p n) -> p n", p=P)).then_inc(loaded, 16)
            sp.dma_start(dst_next[:, :], a.dst_order[1:c.E + 1].rearrange("(p n) -> p n", p=P)).then_inc(loaded, 16)
            by_batch = a.dst_order[0:c.E].rearrange("(b e) -> b e", e=G)
            sp.dma_start(ends_i[:, :], by_batch).then_inc(loaded, 16)
            with nc.allow_non_contiguous_dma(reason="one value of each batch"):
                sp.dma_start(c.mid[:, :], by_batch[:, G // 2:G // 2 + 1].rearrange("b o -> o b")).then_inc(consts, 16)
            sp.dma_start(src_i[:, :], a.src_cols).then_inc(loaded, 16)
            sp.dma_start(dst_i[:, :], a.dst_cols).then_inc(loaded, 16)
            for to, of in loads:
                sp.dma_start(to, of).then_inc(consts, 16)
            sp.wait_ge(made, 2)
            for table in (c.rec0, c.rec1):
                for start in (0, EDGE + c.E):
                    rows = table[start:start + EDGE, :]
                    sp.dma_start(rows.rearrange("r f -> (r f)").rearrange("(p n) -> p n", p=P),
                                 zeros[:, 0:EDGE * table.shape[1] // P]).then_inc(pads, 16)
            sp.wait_ge(near, 1)
            sp.dma_start(c.rel_d[:].rearrange("(b e) -> b e", e=G), ends[:, 1, :]).then_inc(pads, 16)
            sp.wait_ge(hist_done, 1)
            sp.dma_start(c.hist_d[:].rearrange("(r n) -> r n", n=16), hist[:, :]).then_inc(hist_out, 16)
            sp.wait_ge(hist_out, 16)
            sp.dma_start(row[:, 0, :], c.hist_d[:].unsqueeze(0)).then_inc(hist_in, 16)
            sp.wait_ge(kept, 1)
            by_batch = c.spread_idx[:, :].rearrange("(b p) j -> p b j", p=P)
            idx_now = bits[:, 3, :].rearrange("p (b j) -> p b j", j=TILES)
            sp.dma_start(by_batch[:, 0:c.batches, :], idx_now).then_inc(pads, 16)
            sp.dma_start(by_batch[:, c.batches:, :], idx_now[:, 0:SLOTS, :]).then_inc(pads, 16)
            sp.wait_ge(pads, 16 * 7)
            sp.wait_ge(consts, 16 * (len(loads) + 1))

        @block.gpsimd
        def _(pool):
            nc.gpsimd.memset(c.ident[:, :], 0.0).then_inc(made, 1)
            nc.gpsimd.memset(zeros[:, :], 0.0).then_inc(made, 1)
            pool.wait_ge(made, 2)
            nc.gpsimd.affine_select(out=c.ident[:, :], in_=c.ident[:, :], compare_op=ALU.not_equal, fill=1.0, base=0,
                                    pattern=[[-1, P]], channel_multiplier=1).then_inc(made, 1)
            nc.gpsimd.iota(iota_i[:, :], pattern=[[1, P]], base=0, channel_multiplier=0).then_inc(made, 1)
            nc.gpsimd.iota(base_i[:, :], pattern=[[P, c.tiles]], base=0, channel_multiplier=0).then_inc(made, 1)
            nc.gpsimd.iota(offs_i[:, :], pattern=[[-P, TILES], [0, P]], base=EDGE, channel_multiplier=0).then_inc(made, 1)
            nc.gpsimd.iota(first_i[:, :], pattern=[[0, 1]], base=0, channel_multiplier=G).then_inc(made, 1)
            nc.gpsimd.iota(rel_i[:, :], pattern=[[P, CHUNKS]], base=-EDGE, channel_multiplier=1).then_inc(made, 1)
            nc.gpsimd.iota(nth_i[:, :], pattern=[[-TILES, c.batches], [0, TILES]], base=AHEAD, channel_multiplier=0)\
                .then_inc(made, 1)
            nc.gpsimd.iota(off_i[:, :], pattern=[[0, c.groups], [P, TILES]], base=-EDGE, channel_multiplier=0).then_inc(made, 1)
            nc.gpsimd.iota(c.iota_t_i[:, :], pattern=[[1, c.tiles]], base=0, channel_multiplier=0).then_inc(made, 1)

        @block.vector
        def _(dve):
            n = [0]

            def link(ins):
                n[0] += 1
                ins.then_inc(step, 1)
                dve.wait_ge(step, n[0])

            v = nc.vector
            v.memset(c.ones_row[:, :], 1.0)
            v.memset(c.none_row[:, :], 0.0)
            v.memset(c.dinv[:, :], 0.0)
            link(v.memset(ones_col[:, :], 1.0))
            dve.wait_ge(made, 11)
            v.tensor_copy(c.iota[:, :], iota_i[:, :])
            v.tensor_copy(c.iota_t[:, :], c.iota_t_i[:, :])
            v.tensor_copy(off[:, :], off_i[:, :])
            v.tensor_copy(offs[:, :], offs_i[:, :])
            v.tensor_copy(first[:, :], first_i[:, :])
            v.tensor_copy(c.rel[:, :], rel_i[:, :])
            v.tensor_copy(nth[:, :], nth_i[:, :])
            link(v.tensor_copy(c.base[:, :], base_i[:, :]))
            dve.wait_ge(loaded, 80)
            link(v.tensor_copy(ends[:, 0, :], ends_i[:, :]))
            link(v.tensor_scalar(ends[:, 1, :], ends[:, 0, :], ends[:, 0, G // 2:G // 2 + 1], None, ALU.subtract))
            dve.sem_inc(near, 1)
            link(v.tensor_tensor(offs[:, :], ends[:, 1, :], offs[:, :], ALU.add))
            v.tensor_reduce(far[:, 0:1], offs[:, :], AX.X, ALU.max)
            v.tensor_reduce(far[:, 1:2], offs[:, :], AX.X, ALU.min)
            v.tensor_reduce(far[:, 2:3], ends[:, 0, :], AX.X, ALU.max)
            link(v.tensor_reduce(far[:, 3:4], ends[:, 0, :], AX.X, ALU.min))
            v.tensor_scalar(far[:, 4:5], far[:, 0:1], float(2 * P - 1), None, ALU.is_gt)
            v.tensor_scalar(far[:, 5:6], far[:, 1:2], 0.0, None, ALU.is_lt)
            link(v.tensor_scalar(far[:, 2:4], far[:, 2:4], first[:, 0:1], None, ALU.subtract))
            v.tensor_scalar(far[:, 6:7], far[:, 2:3], float((NEAR - AHEAD) * P - 1), None, ALU.is_gt)
            link(v.tensor_scalar(far[:, 7:8], far[:, 3:4], -float(AHEAD * P), None, ALU.is_lt))
            link(v.tensor_reduce(far[:, 0:1], far[:, 4:8], AX.X, ALU.max))
            v.tensor_scalar(part[:, 0, :], dst_nat[:, :], 11, None, ALU.logical_shift_right)
            link(v.tensor_scalar(part[:, 1, :], dst_nat[:, :], 7, 15, ALU.logical_shift_right, ALU.bitwise_and))
            link(v.tensor_copy(part_f[:, :, :], part[:, :, :]))
            v.tensor_tensor(hot_a[:, :, :], over_cols(part_f[:, 0, :], A_ROWS), over_rows(c.iota[:, 0:A_ROWS], c.cols),
                            ALU.is_equal)
            v.tensor_tensor(hot_b[:, :, :], over_cols(part_f[:, 1, :], 16), over_rows(c.iota[:, 0:16], c.cols),
                            ALU.is_equal)
            link(v.tensor_tensor(disorder[:, :], dst_nat[:, :], dst_next[:, :], ALU.is_gt))
            link(v.tensor_reduce(disorder_sum[:, :], disorder[:, :], AX.X, ALU.add))
            link(v.memset(late[:, :], 0.0))
            dve.sem_inc(one_hots, 1)
            v.tensor_scalar(bits[:, 0, :], src_i[:, :], P - 1, 9, ALU.bitwise_and, ALU.logical_shift_left)
            v.tensor_scalar(bits[:, 1, :], src_i[:, :], 7, None, ALU.logical_shift_right)
            link(v.tensor_scalar(bits[:, 2, :], dst_i[:, :], P - 1, None, ALU.bitwise_and))
            v.tensor_tensor(bits[:, 3, :], bits[:, 0, :], bits[:, 1, :], ALU.bitwise_or).then_inc(kept, 1)
            v.tensor_copy(c.dst_f[:, :], dst_i[:, :])
            v.tensor_copy(c.dst_lo[:, :], bits[:, 2, :])
            link(v.tensor_scalar(part[:, 0, :], dst_i[:, :], 7, None, ALU.logical_shift_right))
            link(v.tensor_copy(c.dst_hi[:, :], part[:, 0, :]))
            v.tensor_tensor(c.dst_near[:, :], c.dst_hi[:, :], nth[:, :], ALU.add)
            dve.wait_ge(counted, 3)
            v.tensor_scalar(c.near[:, :], p_dis[:, 1:2], 0.5, None, ALU.is_lt)
            v.tensor_copy(late[:, 0:1], p_dis[:, 0:1]).then_inc(step, 1)
            n[0] += 1
            v.tensor_copy(hist[:, :], p_hist[:, :]).then_inc(hist_done, 1)
            dve.wait_ge(step, n[0])
            link(v.tensor_scalar(late[:, 1:2], late[:, 0:1], 1.0, None, ALU.min))
            link(v.tensor_scalar(late[:, 2:3], late[:, 1:2], -1.0, 1.0, ALU.mult, ALU.add))
            link(v.tensor_scalar(late[:, 3:4], late[:, 1:2], float(c.E), None, ALU.mult))
            dve.wait_ge(hist_in, 16)
            link(v.memset(row[:, 7, :], 1.0))
            link(v.tensor_tensor_scan(row[:, 1, :], row[:, 7, :], row[:, 0, :], 0.0, ALU.mult, ALU.add))
            link(v.tensor_tensor(row[:, 2, :], row[:, 1, :], row[:, 0, :], ALU.subtract))
            link(v.tensor_scalar(row[:, 3, :], row[:, 2, :], late[:, 2:3], None, ALU.mult))
            link(v.tensor_scalar(row[:, 4, :], row[:, 1, :], late[:, 2:3], late[:, 3:4], ALU.mult, ALU.add))
            v.tensor_copy(c.starts[:, :], row[:, 3, 0:t_used])
            link(v.tensor_tensor(row[:, 5, :], row[:, 4, :], row[:, 3, :], ALU.subtract))
            link(v.tensor_scalar(row[:, 6, :], row[:, 5, :], -0.5, 1.0 / XW, ALU.add, ALU.mult))
            link(v.tensor_scalar(row[:, 5, :], row[:, 6, :], 0.5, 0.0, ALU.add, ALU.max))
            link(v.tensor_copy(row_i[:, :], row[:, 5, :]))
            v.tensor_copy(c.extra[:, :], row_i[:, 0:t_used])
            middle = over_cols(row[:, 3, 0:t_used].rearrange("o (g t) -> o g t", t=TILES)[:, :, TILES // 2], TILES)
            link(v.tensor_copy(row[:, 5, 0:t_used].rearrange("o (g t) -> o g t", t=TILES), middle))
            link(v.tensor_tensor(row[:, 6, 0:t_used], row[:, 5, 0:t_used], off[:, :], ALU.add))
            link(v.tensor_tensor(row[:, 7, 0:t_used], row[:, 6, 0:t_used], row[:, 3, 0:t_used], ALU.subtract))
            link(v.scalar_tensor_tensor(row[:, 2, 0:t_used], row[:, 4, 0:t_used], -float(2 * P), row[:, 6, 0:t_used],
                                        ALU.add, ALU.subtract))
            link(v.tensor_tensor(row[:, 7, 0:t_used], row[:, 7, 0:t_used], row[:, 2, 0:t_used], ALU.max))
            link(v.tensor_scalar(row[:, 6, 0:t_used], row[:, 5, 0:t_used], float(EDGE), float(c.E), ALU.add, ALU.min))
            link(v.scalar_tensor_tensor(row[:, 6, 0:t_used], c.iota_t[0:1, :], -float(P), row[:, 6, 0:t_used],
                                        ALU.mult, ALU.add))
            link(v.scalar_tensor_tensor(row[:, 6, 0:t_used], off[:, :], float(EDGE - LAG * G), row[:, 6, 0:t_used],
                                        ALU.add, ALU.add))
            link(v.tensor_tensor(row[:, 7, 0:t_used], row[:, 7, 0:t_used], row[:, 6, 0:t_used], ALU.max))
            link(v.tensor_reduce(late[:, 0:1], row[:, 7, 0:t_used], AX.X, ALU.max))
            link(v.tensor_scalar(c.flag[:, :], late[:, 0:1], 0.5, None, ALU.is_lt))
            dve.wait_ge(consts, 16 * (len(loads) + 1))
            link(v.tensor_scalar(c.b2[:, :], c.b2[:, :], 0.5, None, ALU.mult))

        @block.tensor
        def _(pe):
            pe.wait_ge(one_hots, 1)
            for n in range(c.cols):
                mm = nc.tensor.matmul(p_hist[:, :], hot_a[:, n, :], hot_b[:, n, :], start=(n == 0), stop=(n == c.cols - 1))
            mm.then_inc(counted, 1)
            nc.tensor.matmul(p_dis[:, 0:1], disorder_sum[:, :], ones_col[:, :], start=True, stop=True).then_inc(counted, 1)
            nc.tensor.matmul(p_dis[:, 1:2], far[:, 0:1], ones_col[0:c.batches, :], start=True, stop=True).then_inc(counted, 1)


def build_edge_weights(nc, c, a):
    with semaphores(nc, "a") as sem, ExitStack() as ctx:
        sb = lambda name, shape, dt=F32: ctx.enter_context(nc.sbuf_tensor(name, shape, dt))
        slots = lambda make, name, *args: [make(f"{name}{k}", *args) for k in range(SLOTS)]
        psum = lambda name, shape: ctx.enter_context(nc.psum_tensor(name, shape, F32))
        idx = slots(sb, "a_idx", [P, 2 * TILES], I32)
        src_rows = slots(sb, "a_src_rows", [P, TILES, RW])
        dst_rows = slots(sb, "a_dst_rows", [P, CHUNKS, D])
        ends = slots(sb, "a_ends", [P, G])
        spread = slots(sb, "a_spread", [P, PAIRS, P], F32R)
        high, low = slots(sb, "a_high", [P, CHUNKS, D], F32R), slots(sb, "a_low", [P, CHUNKS, D], F32R)
        src_t, dst_t = slots(sb, "a_src_t", [P, G]), slots(sb, "a_dst_t", [P, G])
        hid = slots(sb, "a_hid", [c.M, G])
        tanh = slots(sb, "a_tanh", [P, TILES])
        wk = slots(sb, "a_wk", [P, TILES])
        hot_lo = slots(sb, "a_hot_lo", [P, TILES, P])
        hot_hi = slots(sb, "a_hot_hi", [P, TILES, c.tiles])
        place_hot, near_hot = slots(sb, "a_place_hot", [P, TILES, P], F32R), slots(sb, "a_near_hot", [P, TILES, NEAR])
        w_high, w_low = slots(sb, "a_w_high", [P, TILES], F32R), slots(sb, "a_w_low", [P, TILES], F32R)
        near_w = slots(sb, "a_near_w", [P, TILES, 2, NEAR], F32R)
        near_deg, deg = slots(sb, "a_near_deg", [P, NEAR]), sb("a_deg", [P, c.tiles + 2 * AHEAD])
        zero = sb("a_zero", [1, P + c.tiles])
        root = sb("a_root", [P, c.tiles])
        p_src, p_dst = ([psum(f"ap_{side}{k}", [P, G]) for k in range(2)] for side in ("src", "dst"))
        p_h = psum("ap_h", [c.M, G])
        p_w = psum("ap_w", [P, SLOTS, TILES])
        p_deg = psum("ap_deg", [P, c.tiles])
        p_near = [p_deg, psum("ap_near", [P, 2 * NEAR])]
        near_marked, near_read, near_added, w_high_done, w_low_done = (
            sem(n) for n in ("near_marked", "near_read", "near_added", "w_high_done", "w_low_done"))
        idx_in, gathered, kept = slots(sem, "idx_in"), c.gathered[0], slots(sem, "kept")
        marked, turned, src_copied, dst_copied, hidden, gelu_done, logits, tanh_done, w_done, hot, deg_added = (
            sem(n) for n in ("marked", "turned", "src_copied", "dst_copied", "hidden", "gelu_done",
                                    "logits", "tanh_done", "w_done", "hot", "deg_added"))
        deg_done, cleared, root_done, table_out = sem("deg_done"), sem("cleared"), sem("root_done"), sem("table_out")
        ends_in, spread_done, high_done, low_done = slots(sem, "ends_in"), sem("spread_done"), sem("high_done"), sem("low_done")
        rows_of = lambda general: 16 * TILES * (1 + general)
        block = ctx.enter_context(nc.Block())

        @block.sync
        def _(sp):
            credit(sp, *kept, by=16)
            for k in range(SLOTS):
                sp.dma_start(idx[k][:, :], a.edge_idx[k * P:(k + 1) * P, :]).then_inc(idx_in[k], 16)

            def steps(general):
                ROWS = rows_of(general)

                def keep_and_fetch(n, k, q):
                    sp.wait_ge(gathered[k], ROWS * q + ROWS)
                    sp.sem_inc(c.none, 1)
                    sp.wait_ge(marked, done(n))
                    sp.sem_inc(c.none, 1)
                    sp.dma_start(edge_rows(kept_rows(c, c.rec0), n), src_rows[k][:, :, :]).then_inc(kept[k], 16)
                    sp.dma_start(idx[k][:, :], a.edge_idx[ds((n + SLOTS) * P, P), :]).then_inc(idx_in[k], 16)

                def load_ends(n, k, q):
                    sp.wait_ge(turned, freed(n))
                    sp.sem_inc(c.none, 1)
                    mid = sp.value_load(c.mid[0:1, ds(n, 1)], min_val=0, max_val=c.N - 1)
                    sp.dma_start(ends[k][:, :], c.rel_d[ds(n * G, G)].unsqueeze(0).to_broadcast([P, G]))\
                        .then_inc(ends_in[k], 16)
                    sp.dma_start(dst_rows[k][:, :, :], window(a.x_wide, mid)).then_inc(ends_in[k], 16)
                return {"K": keep_and_fetch} if general else {"K": keep_and_fetch, "L": load_ends}
            choose(sp, c, c.near, "L0 K1", steps)
            for k in range(SLOTS):
                sp.wait_ge(idx_in[k], 16 * c.uses(k) + 16)
                sp.wait_ge(kept[k], 16 * c.uses(k) + 16)
            sp.wait_ge(root_done, 3)
            sp.dma_start(c.dinv_d[:, :].rearrange("(p n) o -> p (n o)", n=SPREAD), c.dinv[:, :]).then_inc(table_out, 16)
            sp.wait_ge(table_out, 16)

        @block.gpsimd
        def _(pool):
            def steps(general):
                def gather(n, k, q):
                    pool.wait_ge(idx_in[k], 16 * q + 16)
                    pool.sem_inc(c.none, 1)
                    pool.wait_ge(turned, freed(n))
                    pool.sem_inc(c.none, 1)
                    pool.wait_ge(kept[k], 16 * q + 16)
                    pool.sem_inc(c.none, 1)
                    for side, rows in enumerate((src_rows, dst_rows)[:1 + general]):
                        for j in range(TILES):
                            col = side * TILES + j
                            nc.gpsimd.indirect_dma_start(
                                rows[k][:, j, 0:D], None, a.x,
                                bass.IndirectOffsetOnAxis(ap=idx[k][:, col:col + 1], axis=0)).then_inc(gathered[k], 16)
                return {"G": gather}
            choose(pool, c, c.near, "G0", steps)

        @block.tensor
        def _(pe):
            credit(pe, turned, hidden, logits, deg_added)
            pe.wait_ge(cleared, 1)
            nc.tensor.matmul(p_deg[:, :], zero[0:1, 0:P], zero[0:1, P:P + c.tiles], start=True, stop=False,
                             skip_group_check=True)

            def turn_rows(general):
                ROWS = rows_of(general)

                def step(n, k, q):
                    pe.wait_ge(gathered[k], ROWS * q + ROWS)
                    pe.wait_ge(src_copied, done(n - 2))
                    pe.wait_ge(dst_copied, done(n - 2))
                    for j in range(TILES):
                        nc.tensor.transpose(p_src[k % 2][:, j * P:(j + 1) * P], src_rows[k][:, j, 0:D], c.ident[:, :])
                    if general:
                        for j in range(TILES):
                            mm = nc.tensor.transpose(p_dst[k % 2][:, j * P:(j + 1) * P], dst_rows[k][:, j, :], c.ident[:, :])
                    else:
                        pe.wait_ge(spread_done, done(n))
                        pe.wait_ge(low_done, done(n))
                        mm = add_chunks(nc, p_dst[k % 2], high[k], low[k], spread[k], start=True)
                    mm.then_inc(turned, 1)
                return step

            def hidden_layer(n, k, q):
                pe.wait_ge(src_copied, done(n))
                pe.wait_ge(dst_copied, done(n))
                pe.wait_ge(gelu_done, done(n - 1))
                nc.tensor.matmul(p_h[:, :], c.W1[:, 0, :], src_t[k][:, :], start=True, stop=False)
                nc.tensor.matmul(p_h[:, :], c.W1[:, 1, :], dst_t[k][:, :], start=False, stop=True).then_inc(hidden, 1)

            def logit(n, k, q):
                pe.wait_ge(tanh_done, done(n - 1))
                pe.wait_ge(gelu_done, done(n))
                for j in range(TILES):
                    mm = nc.tensor.matmul(p_w[:, k, j:j + 1], hid[k][:, j * P:(j + 1) * P], c.w2[:, :],
                                          start=True, stop=True)
                mm.then_inc(logits, 1)

            def degrees(general):
                def step(n, k, q):
                    pe.wait_ge(hot, n + 1)
                    if general:
                        for j in range(TILES):
                            mm = nc.tensor.matmul(p_deg[:, :], hot_lo[k][:, j, :], hot_hi[k][:, j, :], start=False, stop=False,
                                                  skip_group_check=True)
                    else:
                        pe.wait_ge(near_read, done(n - 2))
                        for j in range(TILES):
                            mm = nc.tensor.matmul(p_near[k % 2][:, 0:2 * NEAR], place_hot[k][:, j, :],
                                                  near_w[k][:, j, :, :].rearrange("p a t -> p (a t)"),
                                                  start=(j == 0), stop=(j == TILES - 1))
                    mm.then_inc(deg_added, 1)
                return step
            choose(pe, c, c.near, "D6 L4 H3 T2",
                   lambda general: {"T": turn_rows(general), "H": hidden_layer, "L": logit, "D": degrees(general)})

        @block.scalar
        def _(act):
            credit(act, src_copied, gelu_done, tanh_done, high_done)
            act.preload_act_table(ACT.Gelu)

            def copy_src(n, k, q):
                act.wait_ge(turned, done(n))
                act.wait_ge(hidden, freed(n))
                nc.scalar.activation(src_t[k][:, :], p_src[k % 2][:, :], ACT.Copy).then_inc(src_copied, 1)

            def gelu(n, k, q):
                act.wait_ge(hidden, done(n))
                act.wait_ge(logits, freed(n))
                nc.scalar.activation(hid[k][:, :], p_h[:, :], ACT.Gelu, bias=c.b1[:, 0:1]).then_inc(gelu_done, 1)

            def half_sigmoid(n, k, q):
                act.wait_ge(logits, done(n))
                act.wait_ge(w_done, freed(n))
                nc.scalar.activation(tanh[k][:, :], p_w[:, k, :], ACT.Tanh, bias=c.b2[:, 0:1], scale=0.5)\
                    .then_inc(tanh_done, 1)
            def split_high(n, k, q):
                act.wait_ge(ends_in[k], 32 * q + 32)
                act.wait_ge(turned, freed(n))
                nc.scalar.activation(high[k][:, :, :], dst_rows[k][:, :, :], ACT.Copy).then_inc(high_done, 1)

            def steps(general):
                return {"C": copy_src, "G": gelu, "S": half_sigmoid, **({} if general else {"I": split_high})}
            choose(act, c, c.near, "S4 G3 C2 I0", steps)
            act.wait_ge(root_done, 1)
            nc.scalar.activation(root[:, :], root[:, :], ACT.Sqrt).then_inc(root_done, 1)

        @block.vector
        def _(dve):
            v = nc.vector
            credit(dve, dst_copied, w_done, marked, spread_done, low_done, near_marked, near_read, w_high_done, w_low_done)
            for k in range(SLOTS):
                v.memset(src_rows[k][:, :, D + 1:RW], 0.0)
            v.memset(deg[:, :], 0.0).then_inc(near_added, SLOTS)
            v.memset(zero[:, :], 0.0).then_inc(cleared, 1)

            def mark(n, k, q):
                dve.wait_ge(kept[k], 16 * q + 16)
                v.tensor_copy(src_rows[k][:, :, D], c.dst_f[:, ds(TILES * n, TILES)]).then_inc(marked, 1)

            def spread_ends(n, k, q):
                dve.wait_ge(ends_in[k], 32 * q + 32)
                dve.wait_ge(turned, freed(n))
                for i in range(2):
                    ins = v.tensor_tensor(spread[k][:, :, :].rearrange("p (j i) e -> p i j e", i=2)[:, i, :, :], ends[k][:, :].rearrange("p (j e) -> p j e", j=TILES),
                                          over_cols(c.rel[:, i:i + TILES], P), ALU.is_equal)
                ins.then_inc(spread_done, 1)

            def split_low(n, k, q):
                dve.wait_ge(high_done, done(n))
                dve.wait_ge(ends_in[k], 32 * q + 32)
                dve.wait_ge(turned, freed(n))
                v.tensor_tensor(low[k][:, :, :], dst_rows[k][:, :, :], high[k][:, :, :].bitcast(F32), ALU.subtract)\
                    .then_inc(low_done, 1)

            def copy_dst(n, k, q):
                dve.wait_ge(turned, done(n))
                dve.wait_ge(hidden, freed(n))
                v.tensor_copy(dst_t[k][:, :], p_dst[k % 2][:, :]).then_inc(dst_copied, 1)

            def weights(n, k, q):
                dve.wait_ge(tanh_done, done(n))
                v.tensor_scalar(wk[k][:, :], tanh[k][:, :], 0.5, 0.5, ALU.mult, ALU.add).then_inc(w_done, 1)

            def mark_all(n, k, q):
                weights(n, k, q)
                dve.wait_ge(deg_added, freed(n))
                v.tensor_tensor(hot_hi[k][:, :, :], over_cols(c.dst_hi[:, ds(TILES * n, TILES)], c.tiles),
                                over_rows(c.iota_t[:, :], TILES), ALU.is_equal)
                dve.wait_ge(w_done, done(n))
                v.tensor_copy(c.w_all[:, ds(TILES * n, TILES)], wk[k][:, :])
                for j in range(TILES):
                    ins = v.tensor_scalar(hot_lo[k][:, j, :], c.iota[:, :], c.dst_lo[:, ds(TILES * n + j, 1)],
                                          wk[k][:, j:j + 1], ALU.is_equal, ALU.mult)
                ins.then_inc(hot, 1)

            def mark_near(n, k, q):
                dve.wait_ge(deg_added, freed(n))
                v.tensor_tensor(place_hot[k][:, :, :], over_cols(c.dst_lo[:, ds(TILES * n, TILES)], P),
                                over_rows(c.iota[:, :], TILES), ALU.is_equal)
                v.tensor_tensor(near_hot[k][:, :, :], over_cols(c.dst_near[:, ds(TILES * n, TILES)], NEAR),
                                over_rows(c.iota_t[:, 0:NEAR], TILES), ALU.is_equal).then_inc(near_marked, 1)

            def weight_high(n, k, q):
                dve.wait_ge(w_done, done(n))
                v.tensor_copy(c.w_all[:, ds(TILES * n, TILES)], wk[k][:, :])
                v.tensor_copy(w_high[k][:, :], wk[k][:, :]).then_inc(w_high_done, 1)

            def weight_low(n, k, q):
                dve.wait_ge(w_high_done, done(n))
                v.tensor_tensor(w_low[k][:, :], wk[k][:, :], w_high[k][:, :].bitcast(F32), ALU.subtract).then_inc(w_low_done, 1)

            def weigh_near(n, k, q):
                dve.wait_ge(near_marked, done(n))
                dve.wait_ge(w_low_done, done(n))
                for part, w in enumerate((w_high, w_low)):
                    ins = v.tensor_tensor(near_w[k][:, :, part, :], near_hot[k][:, :, :],
                                          over_cols(w[k][:, :].bitcast(F32), NEAR), ALU.mult)
                ins.then_inc(hot, 1)

            def read_near(n, k, q):
                dve.wait_ge(deg_added, done(n))
                v.tensor_reduce(near_deg[k][:, :], p_near[k % 2][:, 0:2 * NEAR].rearrange("p (a t) -> p t a", a=2), AX.X,
                                ALU.add).then_inc(near_read, 1)

            def add_near(n, k, q):
                dve.wait_ge(near_read, done(n))
                dve.wait_ge(near_added, done(n - 1))
                to = deg[:, ds(n * TILES, NEAR)]
                v.tensor_tensor(to, to, near_deg[k][:, :], ALU.add).then_inc(near_added, 1)

            near = dve.value_load(c.near[0:1, 0:1], min_val=0, max_val=1)
            with dve.If(near == 1):
                pipeline(dve, c, "R7 W5 X5 Z7 V5 M1 Q1 U5 J1 Y5 C2",
                         {"M": mark, "Q": spread_ends, "J": split_low, "C": copy_dst, "W": weights, "X": mark_near,
                          "V": weight_high, "U": weight_low, "Y": weigh_near, "R": read_near, "Z": add_near})
                dve.wait_ge(near_added, done(c.batches - 1))
                dve.sem_inc(deg_done, 1)
            with dve.Else():
                pipeline(dve, c, "M1 Y5 C2", {"M": mark, "C": copy_dst, "Y": mark_all})
                dve.wait_ge(deg_added, done(c.batches - 1))
                v.tensor_copy(deg[:, AHEAD:AHEAD + c.tiles], p_deg[:, :]).then_inc(deg_done, 1)
            dve.wait_ge(deg_done, 1)
            v.tensor_scalar(root[:, :], deg[:, AHEAD:AHEAD + c.tiles], 1.0, None, ALU.add).then_inc(root_done, 1)
            dve.wait_ge(root_done, 2)
            v.reciprocal(c.dinv[:, 0:c.tiles], root[:, :]).then_inc(root_done, 1)


class Extras:

    def __init__(self, nc, c, sb, sem, name):
        self.nc, self.c = nc, c
        self.rows = sb(f"{name}_rows", [P, XJ, D])
        self.val = sb(f"{name}_val", [P, XJ, 2])
        self.place = sb(f"{name}_place", [P, XJ])
        self.hot = sb(f"{name}_hot", [P, XJ, P])
        self.free, self.loaded, self.hot_done, self.place_done = (
            sem(f"{name}_{n}") for n in ("free", "loaded", "hot_done", "place_done"))

    def start(self, pe):
        pe.sem_inc(self.free, 1)

    def _each(self, eng, tile, body):
        count = eng.value_load(self.c.extra[0:1, ds(tile, 1)], min_val=0, max_val=self.c.E // XW + 1)
        with eng.If(count > 0):
            with eng.Fori(0, count) as i:
                body(i)
        with eng.Else():
            eng.sem_inc(self.c.none, 1)

    def load(self, sp, tile, table):
        start = sp.value_load(self.c.starts[0:1, ds(tile, 1)], min_val=0, max_val=self.c.E)

        def one(i):
            sp.wait_ge(self.free, 1)
            sp.sem_clear(self.free)
            at = self.nc.s_assert_within(start + EDGE + i * XW, 0, EDGE + self.c.E,
                                         skip_runtime_bounds_check_because="a further window starts before its tile's last edge")
            sp.dma_start(self.rows[:, :, :], table[ds(at, XW), 0:D].rearrange("(p j) f -> p j f", j=XJ))\
                .then_inc(self.loaded, 16)
            sp.dma_start(self.val[:, :, :], self.c.rec0[ds(at, XW), D:RW].rearrange("(p j) f -> p j f", j=XJ))\
                .then_inc(self.loaded, 16)
        self._each(sp, tile, one)

    def one_hot(self, dve, tile, weigh):
        v = self.nc.vector

        def one(i):
            dve.wait_ge(self.loaded, 32)
            dve.sem_clear(self.loaded)
            v.tensor_scalar(self.place[:, :], self.val[:, :, 0], self.c.base[:, ds(tile, 1)], None,
                            ALU.subtract).then_inc(self.place_done, 1)
            dve.wait_ge(self.place_done, 1)
            dve.sem_clear(self.place_done)
            for j in range(XJ):
                if weigh:
                    ins = v.tensor_scalar(self.hot[:, j, :], self.c.iota[:, :], self.place[:, j:j + 1],
                                          self.val[:, j, 1:2], ALU.is_equal, ALU.mult)
                else:
                    ins = v.tensor_scalar(self.hot[:, j, :], self.c.iota[:, :], self.place[:, j:j + 1], None,
                                          ALU.is_equal)
            ins.then_inc(self.hot_done, 1)
        self._each(dve, tile, one)

    def add(self, pe, tile, out):
        def one(i):
            pe.wait_ge(self.hot_done, 1)
            pe.sem_clear(self.hot_done)
            for j in range(XJ):
                mm = self.nc.tensor.matmul(out, self.rows[:, j, :], self.hot[:, j, :], start=False,
                                             stop=False, skip_group_check=True)
            mm.then_inc(self.free, 1)
        self._each(pe, tile, one)


def add_chunks(nc, out, high, low, hot, start):
    for i in range(CHUNKS):
        first, last = max(i - 1, 0), min(i, TILES - 1)
        pairs = hot[:, max(2 * i - 1, 0):min(2 * i + 1, PAIRS), :].rearrange("p a n -> p (a n)")
        for part in (high, low):
            mm = nc.tensor.matmul(out[:, first * P:(last + 1) * P], part[:, i, :], pairs,
                                  start=start and i == 0 and part is high, stop=(i == CHUNKS - 1 and part is low),
                                  skip_group_check=True)
    return mm


def aggregate_split(nc, c, pe, ex, g, out, rows, parts, hot, general):
    for q in range(TILES):
        cols = slice(q * P, (q + 1) * P)
        mm = nc.tensor.matmul(out[:, cols], rows[:, q, :], c.ident[:, :], start=(q == 0 or general), stop=False,
                              is_transpose=True, skip_group_check=True)
        if general:
            ex.add(pe, g * TILES + q, out[:, cols])
    if general:
        return nc.tensor.matmul(out[:, cols], c.none_row[0:1, 0:P], c.ones_row[0:1, :], start=False, stop=True,
                                skip_group_check=True)
    return add_chunks(nc, out, *parts, hot, start=False)


def aggregate(nc, c, pe, ex, g, out, rows, win, hot, general):
    for q in range(TILES):
        cols = slice(q * P, (q + 1) * P)
        mm = nc.tensor.transpose(out[:, cols], rows[:, q, :], c.ident[:, :])
        if general:
            ex.add(pe, g * TILES + q, out[:, cols])
        else:
            for j in range(2):
                mm = nc.tensor.matmul(out[:, cols], win[:, q + j, 0:D], hot[:, 2 * q + j, :],
                                      start=False, stop=(j == 1), skip_group_check=True)
    if general:
        mm = nc.tensor.matmul(out[:, cols], c.none_row[0:1, 0:P], c.ones_row[0:1, :], start=False, stop=True,
                              skip_group_check=True)
    return mm


class LayerNorm:

    def __init__(self, nc, c, sb, sem, name):
        slots = lambda make, what, *args: [make(f"{name}_{what}{k}", *args) for k in range(SLOTS)]
        self.nc = nc
        self.y = slots(sb, "y", [P, TILES, D])
        self.out = slots(sb, "out", [P, TILES, D])
        self.stats = slots(sb, "stats", [P, TILES, 6])
        self.mv = slots(sb, "mv", [P, TILES, 2])
        self.std = slots(sb, "std", [P, TILES])
        self.rstd = slots(sb, "rstd", [P, TILES])
        self.shift = slots(sb, "shift", [P, TILES])
        self.y_done, self.stats_done, self.mean_done, self.var_done, self.root_done, self.rstd_done, self.shift_done, self.normed = (
            sem(f"{name}_{n}") for n in ("y_done", "stats_done", "mean_done", "var_done", "root_done", "rstd_done",
                                         "shift_done", "normed"))
        self.stored, self.none = slots(sem, "stored"), c.none

    def start_vector(self, dve):
        credit(dve, self.y_done, self.stats_done, self.mean_done, self.var_done, self.rstd_done, self.shift_done)

    def start_scalar(self, act):
        credit(act, self.root_done, self.normed)
        credit(act, *self.stored, by=16)

    def statistics(self, dve, n, k):
        v = self.nc.vector
        dve.wait_ge(self.y_done, done(n))
        for q in range(TILES):
            ins = v.bn_stats(self.stats[k][:, q, :], self.y[k][:, q, :])
        ins.then_inc(self.stats_done, 1)

    def moments(self, dve, n, k):
        v = self.nc.vector
        dve.wait_ge(self.stats_done, done(n))
        dve.sem_inc(self.none, 1)
        for q in range(TILES):
            ins = v.bn_aggr(self.mv[k][:, q, :], self.stats[k][:, q, :])
        ins.then_inc(self.mean_done, 1)

    def variance(self, dve, n, k):
        dve.wait_ge(self.mean_done, done(n))
        self.nc.vector.tensor_scalar(self.std[k][:, :], self.mv[k][:, :, 1], EPS, None, ALU.add).then_inc(self.var_done, 1)

    def vector_steps(self, dve):
        return {"T": lambda g, k, q: self.statistics(dve, g, k), "U": lambda g, k, q: self.moments(dve, g, k),
                "V": lambda g, k, q: self.variance(dve, g, k), "S": lambda g, k, q: self.scales(dve, g, k),
                "F": lambda g, k, q: self.shifts(dve, g, k)}

    def root(self, act, n, k):
        act.wait_ge(self.var_done, done(n))
        self.nc.scalar.activation(self.std[k][:, :], self.std[k][:, :], ACT.Sqrt).then_inc(self.root_done, 1)

    def scales(self, dve, n, k):
        v = self.nc.vector
        dve.wait_ge(self.root_done, done(n))
        dve.wait_ge(self.normed, freed(n))
        v.reciprocal(self.rstd[k][:, :], self.std[k][:, :]).then_inc(self.rstd_done, 1)

    def shifts(self, dve, n, k):
        dve.wait_ge(self.rstd_done, done(n))
        self.nc.vector.scalar_tensor_tensor(self.shift[k][:, :], self.mv[k][:, :, 0], -1.0, self.rstd[k][:, :], ALU.mult,
                               ALU.mult).then_inc(self.shift_done, 1)

    def apply(self, act, n, k, q):
        act.wait_ge(self.shift_done, done(n))
        act.wait_ge(self.stored[k], 16 * q + 16)
        for t in range(TILES):
            ins = self.nc.scalar.activation(self.out[k][:, t, :], self.y[k][:, t, :], ACT.Identity,
                                            bias=self.shift[k][:, t:t + 1], scale=self.rstd[k][:, t:t + 1])
        ins.then_inc(self.normed, 1)

    def store(self, sp, n, k, to):
        sp.wait_ge(self.normed, done(n))
        sp.sem_inc(self.none, 1)
        sp.dma_start(to, self.out[k][:, :, :]).then_inc(self.stored[k], 16)

    def finish(self, sp, c):
        for k in range(SLOTS):
            sp.wait_ge(self.stored[k], 16 * c.uses(k) + 16)


def load_windows(sp, c, s, ex, g, k, q, table, rows_of, rows, win, general):
    for slot in range(SLOTS):
        if general:
            upto = c.uses(slot)
        else:
            upto = q + 1 + (k + LAG - 1 - slot) // SLOTS
            upto = min(upto, c.uses(slot)) if isinstance(q, int) else upto
        sp.wait_ge(s.edges_out[slot], 16 * upto + 16)
        sp.sem_inc(c.none, 1)
    sp.wait_ge(s.agg_done, freed(g))
    sp.sem_inc(c.none, 1)
    sp.wait_ge(s.prepared, freed(g))
    sp.sem_inc(c.none, 1)
    if "resid_done" in s:
        sp.wait_ge(s.resid_done[k], q + 1)
        sp.sem_inc(c.none, 1)
    sp.dma_start(rows[k][:, :, :], node_rows(rows_of, g)).then_inc(s.win_in[k], 16)
    middle = sp.value_load(c.starts[0:1, ds(g * TILES + TILES // 2, 1)], min_val=0, max_val=c.E)
    sp.dma_start(win[k][:, :, :], window(table, middle)).then_inc(s.win_in[k], 16)
    if general:
        for t in range(TILES):
            ex.load(sp, g * TILES + t, table)


def build_gcn(nc, c, a):
    with semaphores(nc, "b") as sem, ExitStack() as ctx:
        sb = lambda name, shape, dt=F32: ctx.enter_context(nc.sbuf_tensor(f"b_{name}", shape, dt))
        slots = lambda make, name, *args: [make(f"{name}{k}", *args) for k in range(SLOTS)]
        psum = lambda name, shape: ctx.enter_context(nc.psum_tensor(f"bp_{name}", shape, F32))
        idx = slots(sb, "idx", [P, TILES], I32)
        dsrc = slots(sb, "dsrc", [P, TILES])
        scale = slots(sb, "scale", [P, TILES, 1])
        win = slots(sb, "win", [P, CHUNKS, RW])
        place = slots(sb, "place", [P, TILES, 2])
        hot = slots(sb, "hot", [P, PAIRS, P])
        less, away = slots(sb, "less", [P, 2]), slots(sb, "away", [P, 2, P])
        rows = slots(sb, "rows", [P, TILES, D])
        own = slots(sb, "own", [P, TILES, D])
        resid = slots(sb, "resid", [P, TILES, D])
        summed = slots(sb, "summed", [P, G])
        p_sum, p_out = ([psum(f"{n}{k}", [P, G]) for k in range(4)] for n in ("sum", "out"))
        ex = Extras(nc, c, sb, sem, "x")
        ln = LayerNorm(nc, c, sb, sem, "ln")
        s = Names(**{n: sem(n) for n in (
            "scaled", "placed", "prepared", "own_done", "agg_done", "sum_copied", "projected", "away_done", "last_hot")})
        s.idx_in, s.edges_out, s.win_in = (slots(sem, n) for n in ("idx_in", "edges_out", "win_in"))
        s.resid_done = slots(sem, "resid_done")
        s.gathered = c.gathered[1]
        LOADS = 16 * 2
        ROWS = 16 * TILES
        block = ctx.enter_context(nc.Block())

        @block.sync
        def _(sp):
            for k in range(SLOTS):
                sp.dma_start(idx[k][:, :], c.spread_idx[k * P:(k + 1) * P, :]).then_inc(s.idx_in[k], 16)

            def fetch(n, k, q):
                sp.wait_ge(s.gathered[k], ROWS * q + ROWS)
                sp.sem_inc(c.none, 1)
                sp.dma_start(idx[k][:, :], c.spread_idx[ds((n + SLOTS) * P, P), :]).then_inc(s.idx_in[k], 16)

            def windows(general):
                return {"W": lambda g, k, q: load_windows(sp, c, s, ex, g, k, q, c.rec0, a.x, rows, win, general),
                        "Z": lambda g, k, q: ln.store(sp, g, k, node_rows(c.x1, g))}
            interleave(sp, c, "F1 W6 Z15", {"F": fetch}, windows(False), windows(True))
            ln.finish(sp, c)
            for k in range(SLOTS):
                sp.wait_ge(s.idx_in[k], 16 * c.uses(k) + 16)

        @block.gpsimd
        def _(pool):
            def gather(n, k, q):
                pool.wait_ge(s.idx_in[k], 16 * q + 16)
                pool.sem_inc(c.none, 1)
                pool.wait_ge(s.scaled, freed(n))
                pool.sem_inc(c.none, 1)
                for j in range(TILES):
                    nc.gpsimd.indirect_dma_start(
                        dsrc[k][:, j:j + 1], None, c.dinv_d[:, :],
                        bass.IndirectOffsetOnAxis(ap=idx[k][:, j:j + 1], axis=0)).then_inc(s.gathered[k], 16)

            def with_bias(g, k, q):
                if k % 2 == 0:
                    pool.wait_ge(s.win_in[k], LOADS * q + LOADS)
                    pool.wait_ge(ln.y_done, freed(g))
                    nc.gpsimd.tensor_tensor(resid[k][:, :, :], rows[k][:, :, :], over_rows(c.conv_b[:, :], TILES), ALU.add)\
                        .then_inc(s.resid_done[k], 1)
            for k in range(0, SLOTS, 2):
                credit(pool, s.resid_done[k], by=1)
            interleave(pool, c, "G0 R8", {"G": gather}, {"R": with_bias})

        @block.tensor
        def _(pe):
            credit(pe, s.agg_done, s.projected)
            ex.start(pe)

            def sums(general):
                def step(g, k, q):
                    pe.wait_ge(s.prepared, done(g))
                    pe.wait_ge(s.last_hot, done(g))
                    pe.wait_ge(s.own_done, done(g))
                    pe.wait_ge(s.win_in[k], LOADS * q + LOADS)
                    pe.wait_ge(s.sum_copied, freed(g))
                    aggregate(nc, c, pe, ex, g, p_sum[k], own[k], win[k], hot[k], general).then_inc(s.agg_done, 1)
                return step

            def project(g, k, q):
                pe.wait_ge(s.sum_copied, done(g))
                pe.wait_ge(ln.y_done, freed(g))
                for t in range(TILES):
                    mm = nc.tensor.matmul(p_out[k][:, t * P:(t + 1) * P], summed[k][:, t * P:(t + 1) * P],
                                          c.conv_w[:, :], start=True, stop=True)
                mm.then_inc(s.projected, 1)
            interleave(pe, c, "O10 A9", {}, {"A": sums(False), "O": project},
                       {"A": sums(True), "O": project})

        @block.scalar
        def _(act):
            credit(act, s.sum_copied, s.own_done, s.away_done, s.last_hot)
            credit(act, *s.edges_out, by=16)
            ln.start_scalar(act)
            act.preload_act_table(ACT.Sqrt)

            def store_scales(n, k, q):
                act.wait_ge(s.scaled, done(n))
                with nc.allow_non_contiguous_dma(reason="one value of each kept row"):
                    act.dma_start(edge_rows(kept_rows(c, c.rec0), n)[:, :, D + 1:RW], scale[k][:, :, :])\
                        .then_inc(s.edges_out[k], 16)

            def own_rows(g, k, q):
                act.wait_ge(s.win_in[k], LOADS * q + LOADS)
                act.wait_ge(s.agg_done, freed(g))
                for t in range(TILES):
                    ins = nc.scalar.activation(own[k][:, t, :], rows[k][:, t, :], ACT.Copy,
                                               scale=c.dinv[:, ds(g * TILES + t, 1)])
                ins.then_inc(s.own_done, 1)

            def last_tile_hot(g, k, q):
                act.wait_ge(s.placed, done(g))
                act.wait_ge(s.agg_done, freed(g))
                for j in range(2):
                    ins = nc.scalar.activation(away[k][:, j, :], c.iota[:, :], ACT.Abs, bias=place[k][:, TILES - 1, j:j + 1],
                                               scale=-1.0)
                ins.then_inc(s.away_done, 1)
                act.wait_ge(s.away_done, done(g))
                for j in range(2):
                    ins = nc.scalar.activation(hot[k][:, PAIRS - 2 + j, :], away[k][:, j, :], ACT.Relu,
                                               bias=win[k][:, TILES - 1 + j, D + 1:RW], scale=less[k][:, j:j + 1])
                ins.then_inc(s.last_hot, 1)

            def copy_sums(g, k, q):
                act.wait_ge(s.agg_done, done(g))
                act.wait_ge(s.projected, freed(g))
                nc.scalar.activation(summed[k][:, :], p_sum[k][:, :], ACT.Copy).then_inc(s.sum_copied, 1)
            interleave(act, c, "E2 R13 X8 H8 C9 N14",
                       {"E": store_scales},
                       {"X": own_rows, "H": last_tile_hot, "C": copy_sums, "R": lambda g, k, q: ln.root(act, g, k),
                        "N": lambda g, k, q: ln.apply(act, g, k, q)})
            for k in range(SLOTS):
                act.wait_ge(s.edges_out[k], 16 * c.uses(k) + 16)

        @block.vector
        def _(dve):
            v = nc.vector
            credit(dve, s.scaled, s.placed, s.prepared)
            for k in range(1, SLOTS, 2):
                credit(dve, s.resid_done[k], by=1)
            ln.start_vector(dve)

            def scales(n, k, q):
                dve.wait_ge(s.gathered[k], ROWS * q + ROWS)
                dve.wait_ge(s.edges_out[k], 16 * q + 16)
                v.tensor_tensor(scale[k][:, :, 0], dsrc[k][:, :], c.w_all[:, ds(TILES * n, TILES)], ALU.mult)\
                    .then_inc(s.scaled, 1)

            def places(g, k, q):
                dve.wait_ge(s.win_in[k], LOADS * q + LOADS)
                v.tensor_scalar(less[k][:, :], win[k][:, TILES - 1:, D + 1], -1.0, None, ALU.mult)
                for j in range(2):
                    ins = v.tensor_tensor(place[k][:, :, j], win[k][:, j:j + TILES, D],
                                          c.base[:, ds(g * TILES, TILES)], ALU.subtract)
                ins.then_inc(s.placed, 1)

            def prepare(general):
                def step(g, k, q):
                    dve.wait_ge(s.agg_done, freed(g))
                    dve.wait_ge(s.placed, done(g))
                    v.tensor_copy(c.place[:, ds(g * PAIRS, PAIRS)], place[k][:, :, :].rearrange("p t j -> p (t j)"))
                    for t in range(TILES - 1):
                        for j in range(2):
                            ins = v.tensor_scalar(hot[k][:, 2 * t + j, :], c.iota[:, :], place[k][:, t, j:j + 1],
                                                  win[k][:, t + j, D + 1:RW], ALU.is_equal, ALU.mult)
                    ins.then_inc(s.prepared, 1)
                    if general:
                        for t in range(TILES):
                            ex.one_hot(dve, g * TILES + t, weigh=True)
                return step

            def with_bias(g, k, q):
                if k % 2:
                    dve.wait_ge(s.win_in[k], LOADS * q + LOADS)
                    v.tensor_tensor(resid[k][:, :, :], rows[k][:, :, :], over_rows(c.conv_b[:, :], TILES), ALU.add)\
                        .then_inc(s.resid_done[k], 1)

            def residual(g, k, q):
                dve.wait_ge(s.projected, done(g))
                dve.wait_ge(s.resid_done[k], q + 2)
                dve.wait_ge(ln.normed, freed(g))
                for t in range(TILES):
                    ins = v.scalar_tensor_tensor(ln.y[k][:, t, :], p_out[k][:, t * P:(t + 1) * P],
                                                 c.dinv[:, ds(g * TILES + t, 1)], resid[k][:, t, :], ALU.mult, ALU.add)
                ins.then_inc(ln.y_done, 1)
            common = {"A": places, "B": with_bias, "Y": residual, **ln.vector_steps(dve)}
            interleave(dve, c, "E2 S14 P8 F14 B10 Y11 U12 T11 V12 A7", {"E": scales},
                       {"P": prepare(False), **common}, {"P": prepare(True), **common})


def build_gine(nc, c, a, layer, h_in):
    last = layer == 1
    with semaphores(nc, "cd"[layer]) as sem, ExitStack() as ctx:
        tag = "cd"[layer]
        sb = lambda name, shape, dt=F32: ctx.enter_context(nc.sbuf_tensor(f"{tag}_{name}", shape, dt))
        slots = lambda make, name, *args: [make(f"{name}{k}", *args) for k in range(SLOTS)]
        psum = lambda name, shape: ctx.enter_context(nc.psum_tensor(f"{tag}p_{name}", shape, F32))
        idx = slots(sb, "idx", [P, 2 * TILES], I32)
        attr = slots(sb, "attr", [c.K + 1, G])
        src_rows = slots(sb, "src_rows", [P, TILES, D])
        msg = slots(sb, "msg", [P, TILES, D])
        win = slots(sb, "win", [P, CHUNKS, D])
        hot = slots(sb, "hot", [P, PAIRS, P], F32R)
        high, low = slots(sb, "high", [P, CHUNKS, D], F32R), slots(sb, "low", [P, CHUNKS, D], F32R)
        rows = slots(sb, "rows", [P, TILES, D])
        summed = slots(sb, "summed", [P, G])
        hid = slots(sb, "hid", [P, G])
        out = slots(sb, "out", [P, TILES, D])
        bn = sb("bn", [P, c.groups, 6])
        mv = sb("mv", [P, 2])
        p_edge, p_sum, p_hid, p_out = ([psum(f"{n}{k}", [P, G]) for k in range(2)] for n in ("edge", "sum", "hid", "out"))
        ex = Extras(nc, c, sb, sem, "x")
        s = Names(**{n: sem(n) for n in (
            "lifted", "added", "msg_done", "prepared", "agg_done", "sum_copied", "hidden", "hid_done",
            "projected", "high_done", "low_done", "read", "out_done", "bn_done")})
        s.idx_in, s.attr_in, s.edges_out, s.win_in, s.stored = (
            slots(sem, n) for n in ("idx_in", "attr_in", "edges_out", "win_in", "stored"))
        s.gathered = c.gathered[2 + layer]
        LOADS = 16 * 2
        ROWS = 16 * TILES
        block = ctx.enter_context(nc.Block())

        @block.sync
        def _(sp):
            for k in range(SLOTS):
                sp.dma_start(idx[k][:, :], a.edge_idx[k * P:(k + 1) * P, :]).then_inc(s.idx_in[k], 16)

            def attributes(n, k, q):
                sp.wait_ge(s.lifted, freed(n))
                sp.sem_inc(c.none, 1)
                sp.dma_start(attr[k][:, :], a.edge_attr[:, ds(n * G, G)]).then_inc(s.attr_in[k], 16)

            def fetch(n, k, q):
                sp.wait_ge(s.gathered[k], ROWS * q + ROWS)
                sp.sem_inc(c.none, 1)
                sp.dma_start(idx[k][:, :], a.edge_idx[ds((n + SLOTS) * P, P), :]).then_inc(s.idx_in[k], 16)

            def windows(general):
                return {"W": lambda g, k, q: load_windows(sp, c, s, ex, g, k, q, c.rec1, h_in, rows, win, general)}
            interleave(sp, c, "B0 W5 F0", {"B": attributes, "F": fetch},
                       windows(False), windows(True))
            for k in range(SLOTS):
                sp.wait_ge(s.idx_in[k], 16 * c.uses(k) + 16)

        @block.gpsimd
        def _(pool):
            def gather(n, k, q):
                pool.wait_ge(s.idx_in[k], 16 * q + 16)
                pool.sem_inc(c.none, 1)
                pool.wait_ge(s.added, freed(n))
                pool.sem_inc(c.none, 1)
                for j in range(TILES):
                    nc.gpsimd.indirect_dma_start(
                        src_rows[k][:, j, :], None, h_in,
                        bass.IndirectOffsetOnAxis(ap=idx[k][:, j:j + 1], axis=0)).then_inc(s.gathered[k], 16)
            pipeline(pool, c, "G0", {"G": gather})

        @block.tensor
        def _(pe):
            credit(pe, s.lifted, s.agg_done, s.hidden, s.projected)
            ex.start(pe)

            def lift(n, k, q):
                pe.wait_ge(s.attr_in[k], 16 * q + 16)
                pe.wait_ge(s.added, done(n - 2))
                for j in range(TILES):
                    mm = nc.tensor.matmul(p_edge[k % 2][:, j * P:(j + 1) * P], attr[k][:, j * P:(j + 1) * P],
                                          c.We[:, layer, :], start=True, stop=True)
                mm.then_inc(s.lifted, 1)

            def sums(general):
                def step(g, k, q):
                    pe.wait_ge(s.prepared, done(g))
                    pe.wait_ge(s.low_done, done(g))
                    pe.wait_ge(s.win_in[k], LOADS * q + LOADS)
                    pe.wait_ge(s.sum_copied, done(g - 2))
                    aggregate_split(nc, c, pe, ex, g, p_sum[k % 2], rows[k], (high[k], low[k]), hot[k], general)\
                        .then_inc(s.agg_done, 1)
                return step

            def hidden_layer(g, k, q):
                pe.wait_ge(s.sum_copied, done(g))
                pe.wait_ge(s.hid_done, done(g - 2))
                nc.tensor.matmul(p_hid[k % 2][:, :], c.Wa[:, layer, :], summed[k][:, :], start=True, stop=True)\
                    .then_inc(s.hidden, 1)

            def project(g, k, q):
                pe.wait_ge(s.hid_done, done(g))
                pe.wait_ge(s.read, done(g - 2))
                if last:
                    mm = nc.tensor.matmul(p_out[k % 2][:, :], c.Wb[:, layer, :], hid[k][:, :], start=True, stop=True)
                else:
                    for t in range(TILES):
                        mm = nc.tensor.matmul(p_out[k % 2][:, t * P:(t + 1) * P], hid[k][:, t * P:(t + 1) * P],
                                              c.Wb[:, layer, :], start=True, stop=True)
                mm.then_inc(s.projected, 1)
            common = {"H": hidden_layer, "O": project}
            interleave(pe, c, "E1 O10 H9 A8", {"E": lift},
                       {"A": sums(False), **common}, {"A": sums(True), **common})

        @block.scalar
        def _(act):
            credit(act, s.high_done, s.msg_done, s.sum_copied, s.hid_done, s.out_done)
            credit(act, *s.edges_out, *s.stored, by=16)
            act.preload_act_table(ACT.Relu)

            def messages(n, k, q):
                act.wait_ge(s.added, done(n))
                nc.scalar.activation(msg[k][:, :, :], msg[k][:, :, :], ACT.Relu).then_inc(s.msg_done, 1)
                act.wait_ge(s.msg_done, done(n))
                act.dma_start(edge_rows(kept_rows(c, c.rec1), n), msg[k][:, :, :]).then_inc(s.edges_out[k], 16)

            def split_high(g, k, q):
                act.wait_ge(s.win_in[k], LOADS * q + LOADS)
                act.wait_ge(s.agg_done, freed(g))
                nc.scalar.activation(high[k][:, :, :], win[k][:, :, :], ACT.Copy).then_inc(s.high_done, 1)

            def copy_sums(g, k, q):
                act.wait_ge(s.agg_done, done(g))
                act.wait_ge(s.hidden, freed(g))
                nc.scalar.activation(summed[k][:, :], p_sum[k % 2][:, :], ACT.Copy).then_inc(s.sum_copied, 1)

            def relu_hidden(g, k, q):
                act.wait_ge(s.hidden, done(g))
                act.wait_ge(s.projected, freed(g))
                if last:
                    act.wait_ge(s.stored[k], 16 * q + 16)
                nc.scalar.activation(hid[k][:, :], p_hid[k % 2][:, :], ACT.Relu, bias=c.ba[:, layer:layer + 1])\
                    .then_inc(s.hid_done, 1)

            def store(g, k, q):
                if last:
                    act.wait_ge(s.hid_done, done(g))
                    act.dma_start(c.hid_d[:, ds(g * G, G)], hid[k][:, :]).then_inc(s.stored[k], 16)
                else:
                    act.wait_ge(s.read, done(g))
                    nc.scalar.activation(out[k][:, :, :], out[k][:, :, :], ACT.Relu).then_inc(s.out_done, 1)
                    act.wait_ge(s.out_done, done(g))
                    act.dma_start(node_rows(c.h1, g), out[k][:, :, :]).then_inc(s.stored[k], 16)
            interleave(act, c, "E1 S12 H9 C8 I6", {"E": messages},
                       {"I": split_high, "C": copy_sums, "H": relu_hidden, "S": store})
            for k in range(SLOTS):
                act.wait_ge(s.edges_out[k], 16 * c.uses(k) + 16)
                act.wait_ge(s.stored[k], 16 * c.uses(k) + 16)

        @block.vector
        def _(dve):
            v = nc.vector
            credit(dve, s.low_done, s.added, s.prepared, s.read)

            def add(n, k, q):
                dve.wait_ge(s.gathered[k], ROWS * q + ROWS)
                dve.wait_ge(s.lifted, done(n))
                dve.wait_ge(s.edges_out[k], 16 * q + 16)
                v.tensor_tensor(msg[k][:, :, :], p_edge[k % 2][:, :].rearrange("p (j f) -> p j f", j=TILES),
                                src_rows[k][:, :, :], ALU.add).then_inc(s.added, 1)

            def split_low(g, k, q):
                dve.wait_ge(s.high_done, done(g))
                dve.wait_ge(s.win_in[k], LOADS * q + LOADS)
                dve.wait_ge(s.agg_done, freed(g))
                v.tensor_tensor(low[k][:, :, :], win[k][:, :, :], high[k][:, :, :].bitcast(F32), ALU.subtract)\
                    .then_inc(s.low_done, 1)

            def prepare(general):
                def step(g, k, q):
                    dve.wait_ge(s.agg_done, freed(g))
                    v.tensor_tensor(hot[k][:, :, :], over_cols(c.place[:, ds(g * PAIRS, PAIRS)], P),
                                    over_rows(c.iota[:, :], PAIRS), ALU.is_equal).then_inc(s.prepared, 1)
                    if general:
                        for t in range(TILES):
                            ex.one_hot(dve, g * TILES + t, weigh=False)
                return step

            def read(g, k, q):
                dve.wait_ge(s.projected, done(g))
                if last:
                    cols = min(G, c.n_nodes - g * G) if isinstance(g, int) else G
                    v.bn_stats(bn[:, ds(g, 1), :].rearrange("p a s -> p (a s)"), p_out[k % 2][:, 0:cols]).then_inc(s.read, 1)
                else:
                    dve.wait_ge(s.stored[k], 16 * q + 16)
                    v.tensor_tensor(out[k][:, :, :], p_out[k % 2][:, :].rearrange("p (t f) -> p t f", t=TILES),
                                    over_rows(c.bb[:, :], TILES), ALU.add).then_inc(s.read, 1)
            interleave(dve, c, "E1 R11 J7 P7", {"E": add},
                       {"J": split_low, "P": prepare(False), "R": read},
                       {"J": split_low, "P": prepare(True), "R": read})
            if last:
                dve.wait_ge(s.read, done(c.groups - 1))
                v.bn_aggr(mv[:, :], bn[:, :, :].rearrange("p g s -> p (g s)")).then_inc(s.bn_done, 1)
                dve.wait_ge(s.bn_done, 1)
                v.tensor_tensor(c.bn_mean[:, :], mv[:, 0:1], c.b4[:, :], ALU.add)
                v.tensor_scalar(c.bn_var[:, :], mv[:, 1:2], EPS, None, ALU.add)


def build_final(nc, c, a):
    with semaphores(nc, "e", last=True) as sem, ExitStack() as ctx:
        sb = lambda name, shape, dt=F32: ctx.enter_context(nc.sbuf_tensor(name, shape, dt))
        slots = lambda make, name, *args: [make(f"{name}{k}", *args) for k in range(SLOTS)]
        psum = lambda name, shape: ctx.enter_context(nc.psum_tensor(name, shape, F32))
        col = sb("e_col", [P, 4])
        diag = sb("e_diag", [P, 2, P])
        ones = sb("e_ones", [P, P])
        row = sb("e_row", [P, 2, P])
        Wn = sb("e_Wn", [P, D])
        hid = slots(sb, "e_hid", [P, G])
        rows = slots(sb, "e_rows", [P, TILES, D])
        p_out = slots(psum, "ep_out", [P, G])
        p_row = psum("ep_row", [P, 2 * P])
        ln = LayerNorm(nc, c, sb, sem, "e_ln")
        step, shifted, projected, p_done = sem("step"), sem("shifted"), sem("projected"), sem("row_done")
        loaded = slots(sem, "loaded")
        STEPS = 9
        block = ctx.enter_context(nc.Block())

        @block.sync
        def _(sp):
            def load(g, k, q):
                sp.wait_ge(projected, freed(g))
                sp.sem_inc(c.none, 1)
                sp.wait_ge(ln.y_done, freed(g))
                sp.sem_inc(c.none, 1)
                sp.dma_start(hid[k][:, :], c.hid_d[:, ds(g * G, G)]).then_inc(loaded[k], 16)
                sp.dma_start(rows[k][:, :, :], node_rows(c.x1, g)).then_inc(loaded[k], 16)
            pipeline(sp, c, "L0 Z7", {"L": load, "Z": lambda g, k, q: ln.store(sp, g, k, node_rows(a.out, g))})
            ln.finish(sp, c)

        @block.tensor
        def _(pe):
            credit(pe, projected)
            pe.wait_ge(step, 7)
            nc.tensor.matmul(p_row[:, :], ones[:, :], diag[:, :, :].rearrange("p a f -> p (a f)"), start=True,
                             stop=True).then_inc(p_done, 1)
            pe.wait_ge(step, STEPS)

            def project(g, k, q):
                pe.wait_ge(loaded[k], 32 * q + 32)
                pe.wait_ge(ln.y_done, freed(g))
                for t in range(TILES):
                    cols = slice(t * P, (t + 1) * P)
                    mm = nc.tensor.matmul(p_out[k][:, cols], hid[k][:, cols], Wn[:, :], start=True, stop=True)
                mm.then_inc(projected, 1)
            pipeline(pe, c, "O1", {"O": project})

        @block.gpsimd
        def _(pool):
            credit(pool, shifted)
            pool.wait_ge(step, STEPS)

            def shift(g, k, q):
                pool.wait_ge(loaded[k], 32 * q + 32)
                nc.gpsimd.tensor_tensor(rows[k][:, :, :], rows[k][:, :, :], over_rows(row[:, 1, :], TILES), ALU.add)\
                    .then_inc(shifted, 1)
            pipeline(pool, c, "X1", {"X": shift})

        @block.scalar
        def _(act):
            ln.start_scalar(act)
            act.preload_act_table(ACT.Sqrt)
            nc.scalar.activation(col[:, 0:1], c.bn_var[:, :], ACT.Sqrt).then_inc(step, 1)

            pipeline(act, c, "R4 N5",
                  {"R": lambda g, k, q: ln.root(act, g, k),
                   "N": lambda g, k, q: ln.apply(act, g, k, q)})

        @block.vector
        def _(dve):
            v = nc.vector
            ln.start_vector(dve)
            n = [1]

            def link(ins):
                n[0] += 1
                ins.then_inc(step, 1)
                dve.wait_ge(step, n[0])

            v.memset(ones[:, :], 1.0)
            dve.wait_ge(step, 1)
            link(v.reciprocal(col[:, 1:2], col[:, 0:1]))
            link(v.tensor_tensor(col[:, 2:3], col[:, 1:2], c.gamma[:, :], ALU.mult))
            link(v.tensor_tensor(col[:, 3:4], c.b4[:, :], c.bn_mean[:, :], ALU.subtract))
            link(v.scalar_tensor_tensor(col[:, 3:4], col[:, 3:4], col[:, 2:3], c.beta[:, :], ALU.mult, ALU.add))
            link(v.tensor_scalar(diag[:, 0, :], c.ident[:, :], col[:, 2:3], None, ALU.mult))
            link(v.tensor_scalar(diag[:, 1, :], c.ident[:, :], col[:, 3:4], None, ALU.mult))
            dve.wait_ge(p_done, 1)
            link(v.tensor_copy(row[:, :, :], p_row[:, :].rearrange("p (a f) -> p a f", a=2)))
            link(v.tensor_tensor(Wn[:, :], c.Wb[:, 1, :], row[:, 0, :], ALU.mult))
            assert n[0] == STEPS

            def add(g, k, q):
                dve.wait_ge(projected, done(g))
                dve.wait_ge(shifted, done(g))
                dve.wait_ge(ln.normed, freed(g))
                v.tensor_tensor(ln.y[k][:, :, :], p_out[k][:, :].rearrange("p (t f) -> p t f", t=TILES),
                                rows[k][:, :, :], ALU.add).then_inc(ln.y_done, 1)
            pipeline(dve, c, "S5 F5 Y2 U3 T2 V3", {"Y": add, **ln.vector_steps(dve)})


def build(nc, a, n_nodes):
    c = Names(nc=nc, n_nodes=n_nodes)
    c.N = a.x.shape[0]
    c.E = a.edge_attr.shape[1]
    c.K = a.edge_attr.shape[0] - 1
    c.M = a.mlp_b1.shape[0]
    c.tiles, c.groups, c.batches, c.cols = c.N // P, c.N // G, c.E // G, c.E // P
    c.full, c.rest = c.batches // SLOTS, c.batches % SLOTS
    c.uses = lambda k: c.full + (k < c.rest)
    assert c.batches <= P and c.groups == c.batches and c.rest and (c.groups - 1) * G < n_nodes and c.full > 1
    assert c.tiles <= min(SPREAD, 512) and (c.tiles // 16 + 1) <= P
    dram = lambda name, shape, dt=F32: nc.dram_tensor(f"t_{name}", shape, dt).ap()
    c.rec0, c.rec1 = dram("rec0", [c.E + 2 * EDGE, RW]), dram("rec1", [c.E + 2 * EDGE, D])
    c.x1, c.h1, c.hid_d = dram("x1", [c.N, D]), dram("h1", [c.N, D]), dram("hid_d", [D, c.N])
    c.dinv_d, c.spread_idx = dram("dinv_d", [P * SPREAD, 1]), dram("spread_idx", [(c.batches + SLOTS) * P, TILES], I32)
    c.rel_d = dram("rel_d", [c.E])
    c.hist_d = dram("hist_d", [16 * (c.tiles // 16 + 1)])
    with ExitStack() as ctx:
        sb = lambda name, shape, dt=F32: ctx.enter_context(nc.sbuf_tensor(f"c_{name}", shape, dt))
        c.none = ctx.enter_context(nc.semaphore("none"))
        c.gathered = [[ctx.enter_context(nc.semaphore(f"gathered_{tag}{k}")) for k in range(SLOTS)] for tag in "abcd"]
        c.ident, c.iota, c.iota_t = sb("ident", [P, P]), sb("iota", [P, P]), sb("iota_t", [P, c.tiles])
        c.iota_t_i = sb("iota_t_i", [P, c.tiles], I32)
        c.ones_row, c.none_row = sb("ones_row", [1, P]), sb("none_row", [1, P])
        c.W1, c.b1, c.w2, c.b2 = sb("W1", [D, 2, c.M]), sb("b1", [c.M, 1]), sb("w2", [c.M, 1]), sb("b2", [P, 1])
        c.conv_w, c.conv_b = sb("conv_w", [D, D]), sb("conv_b", [P, D])
        c.Wa, c.Wb, c.We = sb("Wa", [D, 2, D]), sb("Wb", [D, 2, D]), sb("We", [c.K + 1, 2, D])
        c.ba, c.bb, c.b4 = sb("ba", [D, 2]), sb("bb", [P, D]), sb("b4", [D, 1])
        c.gamma, c.beta, c.bn_mean, c.bn_var = (sb(n, [D, 1]) for n in ("gamma", "beta", "bn_mean", "bn_var"))
        c.w_all, c.dst_f, c.dst_lo, c.dst_hi = (sb(n, [P, c.cols]) for n in ("w_all", "dst_f", "dst_lo", "dst_hi"))
        c.dinv = sb("dinv", [P, SPREAD])
        c.base, c.place = sb("base", [P, c.tiles]), sb("place", [P, c.groups * PAIRS])
        c.rel, c.mid, c.near = sb("rel", [P, CHUNKS]), sb("mid", [1, c.batches], I32), sb("near", [1, 1], I32)
        c.dst_near = sb("dst_near", [P, c.cols])
        c.starts, c.extra, c.flag = sb("starts", [1, c.tiles], I32), sb("extra", [1, c.tiles], I32), sb("flag", [1, 1], I32)
        build_setup(nc, c, a)
        build_edge_weights(nc, c, a)
        build_gcn(nc, c, a)
        build_gine(nc, c, a, 0, c.x1)
        build_gine(nc, c, a, 1, c.h1)
        build_final(nc, c, a)


def arrays_of(x, src, dst, edge_attr_64, L0_gnn_mlp_w1, L0_gnn_mlp_b1, L0_gnn_mlp_w2, L0_gnn_mlp_b2, L0_gnn_conv_w,
              L0_gnn_conv_b, L1_gnn_We1, L1_gnn_be1, L1_gnn_W1, L1_gnn_b1, L1_gnn_W2, L1_gnn_b2, L1_gnn_We2, L1_gnn_be2,
              L1_gnn_W3, L1_gnn_b3, L1_gnn_W4, L1_gnn_b4, L1_gnn_gamma, L1_gnn_beta):
    import numpy as np
    n, e = x.shape[0], src.shape[0]
    batches = max(-(-(max(n, e) + 1) // G), 2 * SLOTS + 1)
    batches += batches % SLOTS == 0
    size = batches * G

    def pad(arr, rows, fill=0):
        out = np.full((rows,) + tuple(arr.shape[1:]), fill, arr.dtype)
        out[:arr.shape[0]] = arr
        return out
    pad_nodes = np.minimum(n + np.arange(size - e), size - 1).astype(np.asarray(dst).dtype)
    src_p, dst_p = (np.concatenate([np.asarray(v), pad_nodes]) for v in (src, dst))
    by_batch = lambda v: v.reshape(batches, TILES, P).transpose(0, 2, 1)
    edge_idx = np.concatenate([by_batch(src_p), by_batch(dst_p)], axis=2)
    attr = pad(np.asarray(edge_attr_64), size).T
    return {
        "x": pad(np.asarray(x), size),
        "x_wide": np.pad(pad(np.asarray(x), size), ((EDGE, EDGE), (0, 0))),
        "dst_order": pad(dst_p, size + 1, size - 1),
        "src_cols": by_batch(src_p).transpose(1, 0, 2).reshape(P, -1),
        "dst_cols": by_batch(dst_p).transpose(1, 0, 2).reshape(P, -1),
        "edge_idx": pad(edge_idx, batches + SLOTS).reshape(-1, 2 * TILES),
        "edge_attr": np.concatenate([attr, np.ones((1, size), attr.dtype)]),
        "mlp_w1": L0_gnn_mlp_w1, "mlp_b1": L0_gnn_mlp_b1, "mlp_w2": L0_gnn_mlp_w2, "mlp_b2": L0_gnn_mlp_b2,
        "conv_w": L0_gnn_conv_w, "conv_b": L0_gnn_conv_b, "We1": L1_gnn_We1, "be1": L1_gnn_be1, "W1": L1_gnn_W1,
        "b1": L1_gnn_b1, "W2": L1_gnn_W2, "b2": L1_gnn_b2, "We2": L1_gnn_We2, "be2": L1_gnn_be2, "W3": L1_gnn_W3,
        "b3": L1_gnn_b3, "W4": L1_gnn_W4, "b4": L1_gnn_b4, "gamma": L1_gnn_gamma, "beta": L1_gnn_beta,
    }


def kernel(**inputs):
    import numpy as np
    import concourse.bacc as bacc
    from concourse.bass_utils import run_bass_kernel_spmd

    arrays = {f"in_{k}": np.ascontiguousarray(v) for k, v in arrays_of(**inputs).items()}
    nc = bacc.Bacc("TRN2", target_bir_lowering=False, num_devices=1)
    a = Names(**{k[3:]: nc.dram_tensor(k, v.shape, mybir.dt.from_np(v.dtype), kind="ExternalInput").ap()
                           for k, v in arrays.items()})
    a.out = nc.dram_tensor("out_rows", a.x.shape, F32, kind="ExternalOutput").ap()
    n_nodes = inputs["x"].shape[0]
    build(nc, a, n_nodes)
    r = run_bass_kernel_spmd(nc, [arrays], core_ids=[0])
    return r.results[0]["out_rows"][:n_nodes]
```
